# Optimizing a Trainium2 kernel written in Bass

```python
import numpy as np
import jax
import jax.numpy as jnp

def _softmax(x, axis=-1):
    return jax.nn.softmax(x, axis=axis)

def _gelu(x):
    return jax.nn.gelu(x, approximate=True)

def _silu(x):
    return jax.nn.silu(x)

def _sigmoid(x):
    return jax.nn.sigmoid(x)

def _layernorm(x, axis=-1, eps=1e-05):
    m = jnp.mean(x, axis=axis, keepdims=True)
    v = jnp.var(x, axis=axis, keepdims=True)
    return (x - m) / jnp.sqrt(v + eps)

def _scatter_add(tgt, idx, src, axis=0):
    return tgt.at[idx].add(src)

def _segment_sum(src, seg, n):
    return jax.ops.segment_sum(src, seg, n)
kernel_name = 'mk_seq_preln_d2_jaxref_r8_445b5a'

def setup_inputs(seed: int=0):
    np.random.seed(seed)
    _w = jnp.asarray

    def _L0_attn_setup():
        import jax, jax.numpy as jnp
        import numpy as np
        B, N, DIM = (2, 256, 128)
        H = 16
        HD = DIM // H
        key = jax.random.key(seed)
        ks = jax.random.split(key, 4)
        x = jax.random.normal(ks[0], (B, N, DIM), dtype=jnp.float32)
        w_qkv = jax.random.normal(ks[1], (DIM, 3 * DIM), dtype=jnp.float32) / np.sqrt(DIM)
        w_proj = jax.random.normal(ks[2], (DIM, DIM), dtype=jnp.float32) / np.sqrt(DIM)
        b_proj = jax.random.normal(ks[3], (DIM,), dtype=jnp.float32) * 0.01
        return {'x': x, 'w_qkv': w_qkv, 'w_proj': w_proj, 'b_proj': b_proj}
    _L0_attn_in = _L0_attn_setup()

    def _L0_ffn_setup():
        import jax, jax.numpy as jnp
        import numpy as np
        BLOCK = 16
        _GRID = jnp.array([0.0, 0.5, 1.0, 1.5, 2.0, 3.0, 4.0, 6.0], dtype=jnp.float32)
        _MID = jnp.array([0.25, 0.75, 1.25, 1.75, 2.5, 3.5, 5.0], dtype=jnp.float32)

        def fp4_quant_dequant(x):
            shape = x.shape
            xb = x.reshape(shape[:-1] + (shape[-1] // BLOCK, BLOCK))
            scale = jnp.max(jnp.abs(xb), axis=-1, keepdims=True) / 6.0
            scale = jnp.maximum(scale, jnp.float32(1e-12))
            xn = xb / scale
            idx = jnp.searchsorted(_MID, jnp.abs(xn))
            q = _GRID[idx] * jnp.sign(xn) * scale
            return q.reshape(shape)

        def fp4_linear(x, w):
            xq = fp4_quant_dequant(x)
            wq = fp4_quant_dequant(w)
            return jnp.einsum('bsk,nk->bsn', xq, wq)
        key = jax.random.key(seed)
        k1, k2, k3, k4 = jax.random.split(key, 4)
        H, I = (128, 352)
        x = jax.random.normal(k1, (4, 512, H), dtype=jnp.float32)
        w_gate = jax.random.normal(k2, (I, H), dtype=jnp.float32) * 0.02
        w_up = jax.random.normal(k3, (I, H), dtype=jnp.float32) * 0.02
        w_down = jax.random.normal(k4, (H, I), dtype=jnp.float32) * 0.02
        return {'x': x, 'w_gate': w_gate, 'w_up': w_up, 'w_down': w_down}
    _L0_ffn_in = _L0_ffn_setup()

    def _L1_attn_setup():
        import jax, jax.numpy as jnp
        import numpy as np
        B, L, D, H, DK, DV, DI, NL = (8, 256, 128, 16, 64, 64, 512, 32)
        EPS = 1e-05

        def _layernorm(x, g, b):
            mu = jnp.mean(x, axis=-1, keepdims=True)
            var = jnp.mean(jnp.square(x - mu), axis=-1, keepdims=True)
            return (x - mu) * jax.lax.rsqrt(var + EPS) * g + b

        def _mha(x, wqs, wks, wvs, pw, pb, g, b):
            dk = wqs.shape[-1]
            q = jnp.einsum('mld,hdk->mhlk', x, wqs)
            k = jnp.einsum('mld,hdk->mhlk', x, wks)
            v = jnp.einsum('mld,hdv->mhlv', x, wvs)
            scores = jnp.einsum('mhqk,mhsk->mhqs', q, k) / jnp.sqrt(jnp.asarray(dk, x.dtype))
            attn = jax.nn.softmax(scores, axis=-1)
            out = jnp.einsum('mhqs,mhsv->mhqv', attn, v) - v
            m, h, l, dv = out.shape
            out = out.transpose(0, 2, 1, 3).reshape(m, l, h * dv)
            out = out @ pw + pb
            return _layernorm(out + x, g, b)

        def _ffn(x, w1, b1, w2, b2, g, b):
            h = jax.nn.relu(x @ w1 + b1)
            return _layernorm(h @ w2 + b2 + x, g, b)
        key = jax.random.key(seed)
        inp = {'enc_input': jax.random.normal(key, (B, L, D), jnp.float32)}
        shapes = {}
        for p in ['la', 'sa']:
            shapes[p + '_wqs'] = (H, D, DK)
            shapes[p + '_wks'] = (H, D, DK)
            shapes[p + '_wvs'] = (H, D, DV)
            shapes[p + '_pw'] = (H * DV, D)
            shapes[p + '_pb'] = (D,)
            shapes[p + '_g'] = (D,)
            shapes[p + '_b'] = (D,)
        for p in ['lf', 'pf']:
            shapes[p + '_w1'] = (D, DI)
            shapes[p + '_b1'] = (DI,)
            shapes[p + '_w2'] = (DI, D)
            shapes[p + '_b2'] = (D,)
            shapes[p + '_g'] = (D,)
            shapes[p + '_b'] = (D,)
        for i, (name, shp) in enumerate(shapes.items()):
            k = jax.random.fold_in(key, i + 1)
            if name.endswith('_g'):
                inp[name] = jnp.ones(shp, jnp.float32)
            elif name.endswith(('_b', '_pb', '_b1', '_b2')):
                inp[name] = jnp.zeros(shp, jnp.float32)
            else:
                inp[name] = jax.random.normal(k, shp, jnp.float32) * 0.02
        return inp
    _L1_attn_in = _L1_attn_setup()

    def _L1_ffn_setup():
        import jax, jax.numpy as jnp
        import numpy as np
        DIM = 128
        DEPTH = 6
        HEADS = 16
        DIM_HEAD = 64
        WINDOW = 32
        INNER = HEADS * DIM_HEAD
        DIM_INNER = int(DIM * 4 * 2 / 3)
        QK_SCALE = 8.0

        def shift_tokens(t):
            a, s = jnp.split(t, 2, -1)
            s = jnp.pad(s, ((0, 0), (1, 0), (0, 0)))[:, :-1]
            return jnp.concatenate([a, s], -1)

        def l2norm(t):
            return t / jnp.maximum(jnp.linalg.norm(t, axis=-1, keepdims=True), 1e-12)

        def rotate_half(x):
            x1, x2 = jnp.split(x, 2, -1)
            return jnp.concatenate([-x2, x1], -1)

        def rotary_tables(n):
            half = jnp.arange(0, DIM_HEAD, 2, dtype=jnp.float32)
            inv_freq = 1.0 / 10000.0 ** (half / DIM_HEAD)
            t = jnp.arange(n, dtype=jnp.float32)
            freqs = t[:, None] * inv_freq[None, :]
            freqs = jnp.concatenate([freqs, freqs], -1)
            base_scale = (half + 0.4 * DIM_HEAD) / (1.4 * DIM_HEAD)
            power = (t - n // 2) / (WINDOW // 2)
            scale = base_scale[None, :] ** power[:, None]
            scale = jnp.concatenate([scale, scale], -1)
            return (freqs, scale)

        def local_attention(q, k, v):
            b, h, n, d = q.shape
            w = WINDOW
            nw = n // w
            bq = q.reshape(b, h, nw, w, d)
            bk = k.reshape(b, h, nw, w, d)
            bv = v.reshape(b, h, nw, w, d)

            def look(t):
                p = jnp.pad(t, ((0, 0), (0, 0), (1, 0), (0, 0), (0, 0)))
                return jnp.concatenate([p[:, :, :nw], p[:, :, 1:]], axis=3)
            bk2, bv2 = (look(bk), look(bv))
            seq = jnp.arange(n).reshape(nw, w)
            seq_p = jnp.pad(seq, ((1, 0), (0, 0)), constant_values=-1)
            jt = jnp.concatenate([seq_p[:nw], seq_p[1:]], axis=1)
            it = seq[:, :, None]
            jb = jt[:, None, :]
            mask = (it < jb) | (it > jb + w) | (jb == -1)
            sim = jnp.einsum('bhwie,bhwje->bhwij', bq, bk2) * QK_SCALE
            sim = jnp.where(mask, -jnp.finfo(sim.dtype).max, sim)
            attn = jax.nn.softmax(sim, -1)
            out = jnp.einsum('bhwij,bhwje->bhwie', attn, bv2)
            return out.reshape(b, h, n, d)

        def attn_layer(x, Wqkv, qs, ksc, Wo):
            b, n, _ = x.shape
            qkv = x @ Wqkv
            q, k, v = jnp.split(qkv, 3, -1)
            sh = lambda t: t.reshape(b, n, HEADS, DIM_HEAD).transpose(0, 2, 1, 3)
            q, k, v = (sh(q), sh(k), sh(v))
            q = l2norm(q) * qs
            k = l2norm(k) * ksc
            freqs, scale = rotary_tables(n)
            cos, sin = (jnp.cos(freqs), jnp.sin(freqs))
            q = q * cos * scale + rotate_half(q) * sin * scale
            inv = 1.0 / scale
            k = k * cos * inv + rotate_half(k) * sin * inv
            out = local_attention(q, k, v)
            out = out.transpose(0, 2, 1, 3).reshape(b, n, INNER)
            return out @ Wo

        def ffn_layer(x, g, bln, W1, b1, W2, b2):
            mu = x.mean(-1, keepdims=True)
            var = ((x - mu) ** 2).mean(-1, keepdims=True)
            xn = (x - mu) / jnp.sqrt(var + 1e-05) * g + bln
            hg = xn @ W1 + b1
            a, gate = jnp.split(hg, 2, -1)
            return a * jax.nn.gelu(gate, approximate=False) @ W2 + b2
        key = jax.random.key(seed)
        ks = jax.random.split(key, 8)
        B, N = (2, 256)
        init = lambda k, shape: jax.random.normal(k, shape, jnp.float32) * 0.02
        return {'x': jax.random.normal(ks[0], (B, N, DIM), jnp.float32), 'Wqkv': init(ks[1], (DEPTH, DIM, 3 * INNER)), 'q_scale': jnp.ones((DEPTH, DIM_HEAD), jnp.float32), 'k_scale': jnp.ones((DEPTH, DIM_HEAD), jnp.float32), 'Wo': init(ks[2], (DEPTH, INNER, DIM)), 'ln_g': jnp.ones((DEPTH, DIM), jnp.float32), 'ln_b': jnp.zeros((DEPTH, DIM), jnp.float32), 'W1': init(ks[3], (DEPTH, DIM, 2 * DIM_INNER)), 'b1': jnp.zeros((DEPTH, 2 * DIM_INNER), jnp.float32), 'W2': init(ks[4], (DEPTH, DIM_INNER, DIM)), 'b2': jnp.zeros((DEPTH, DIM), jnp.float32)}
    _L1_ffn_in = _L1_ffn_setup()
    _d = {'L0_attn_x': _L0_attn_in['x'], 'L0_attn_w_qkv': _L0_attn_in['w_qkv'], 'L0_attn_w_proj': _L0_attn_in['w_proj'], 'L0_attn_b_proj': _L0_attn_in['b_proj'], 'L0_ffn_w_gate': _L0_ffn_in['w_gate'], 'L0_ffn_w_up': _L0_ffn_in['w_up'], 'L0_ffn_w_down': _L0_ffn_in['w_down'], 'L1_attn_la_wqs': _L1_attn_in['la_wqs'], 'L1_attn_la_wks': _L1_attn_in['la_wks'], 'L1_attn_la_wvs': _L1_attn_in['la_wvs'], 'L1_attn_la_pw': _L1_attn_in['la_pw'], 'L1_attn_la_pb': _L1_attn_in['la_pb'], 'L1_attn_la_g': _L1_attn_in['la_g'], 'L1_attn_la_b': _L1_attn_in['la_b'], 'L1_attn_lf_w1': _L1_attn_in['lf_w1'], 'L1_attn_lf_b1': _L1_attn_in['lf_b1'], 'L1_attn_lf_w2': _L1_attn_in['lf_w2'], 'L1_attn_lf_b2': _L1_attn_in['lf_b2'], 'L1_attn_lf_g': _L1_attn_in['lf_g'], 'L1_attn_lf_b': _L1_attn_in['lf_b'], 'L1_attn_sa_wqs': _L1_attn_in['sa_wqs'], 'L1_attn_sa_wks': _L1_attn_in['sa_wks'], 'L1_attn_sa_wvs': _L1_attn_in['sa_wvs'], 'L1_attn_sa_pw': _L1_attn_in['sa_pw'], 'L1_attn_sa_pb': _L1_attn_in['sa_pb'], 'L1_attn_sa_g': _L1_attn_in['sa_g'], 'L1_attn_sa_b': _L1_attn_in['sa_b'], 'L1_attn_pf_w1': _L1_attn_in['pf_w1'], 'L1_attn_pf_b1': _L1_attn_in['pf_b1'], 'L1_attn_pf_w2': _L1_attn_in['pf_w2'], 'L1_attn_pf_b2': _L1_attn_in['pf_b2'], 'L1_attn_pf_g': _L1_attn_in['pf_g'], 'L1_attn_pf_b': _L1_attn_in['pf_b'], 'L1_ffn_Wqkv': _L1_ffn_in['Wqkv'], 'L1_ffn_q_scale': _L1_ffn_in['q_scale'], 'L1_ffn_k_scale': _L1_ffn_in['k_scale'], 'L1_ffn_Wo': _L1_ffn_in['Wo'], 'L1_ffn_ln_g': _L1_ffn_in['ln_g'], 'L1_ffn_ln_b': _L1_ffn_in['ln_b'], 'L1_ffn_W1': _L1_ffn_in['W1'], 'L1_ffn_b1': _L1_ffn_in['b1'], 'L1_ffn_W2': _L1_ffn_in['W2'], 'L1_ffn_b2': _L1_ffn_in['b2']}
    _x0 = _d['L0_attn_x']
    _d['L0_attn_x'] = jax.random.normal(jax.random.fold_in(jax.random.key(seed), 1), (2, 2048, 128), dtype=_x0.dtype)
    del _x0
    return _d

def reference(L0_attn_x, L0_attn_w_qkv, L0_attn_w_proj, L0_attn_b_proj, L0_ffn_w_gate, L0_ffn_w_up, L0_ffn_w_down, L1_attn_la_wqs, L1_attn_la_wks, L1_attn_la_wvs, L1_attn_la_pw, L1_attn_la_pb, L1_attn_la_g, L1_attn_la_b, L1_attn_lf_w1, L1_attn_lf_b1, L1_attn_lf_w2, L1_attn_lf_b2, L1_attn_lf_g, L1_attn_lf_b, L1_attn_sa_wqs, L1_attn_sa_wks, L1_attn_sa_wvs, L1_attn_sa_pw, L1_attn_sa_pb, L1_attn_sa_g, L1_attn_sa_b, L1_attn_pf_w1, L1_attn_pf_b1, L1_attn_pf_w2, L1_attn_pf_b2, L1_attn_pf_g, L1_attn_pf_b, L1_ffn_Wqkv, L1_ffn_q_scale, L1_ffn_k_scale, L1_ffn_Wo, L1_ffn_ln_g, L1_ffn_ln_b, L1_ffn_W1, L1_ffn_b1, L1_ffn_W2, L1_ffn_b2):

    def _L0_attn_ref(x, w_qkv, w_proj, b_proj):
        import jax, jax.numpy as jnp
        import numpy as np
        B, N, DIM = (2, 256, 128)
        H = 16
        HD = DIM // H
        b, n, c = x.shape
        scale = HD ** (-0.5)
        qkv = jnp.einsum('bnc,cd->bnd', x, w_qkv)
        qkv = qkv.reshape(b, n, 3, H, HD).transpose(2, 0, 3, 1, 4)
        q, k, v = (qkv[0], qkv[1], qkv[2])
        q = q * scale
        attn = jnp.einsum('bhnd,bhmd->bhnm', q, k)
        attn = jax.nn.softmax(attn, axis=-1)
        out = jnp.einsum('bhnm,bhmd->bhnd', attn, v)
        out = out.transpose(0, 2, 1, 3).reshape(b, n, c)
        return jnp.einsum('bnc,cd->bnd', out, w_proj) + b_proj

    def _L0_ffn_ref(x, w_gate, w_up, w_down):
        import jax, jax.numpy as jnp
        import numpy as np
        BLOCK = 16
        _GRID = jnp.array([0.0, 0.5, 1.0, 1.5, 2.0, 3.0, 4.0, 6.0], dtype=jnp.float32)
        _MID = jnp.array([0.25, 0.75, 1.25, 1.75, 2.5, 3.5, 5.0], dtype=jnp.float32)

        def fp4_quant_dequant(x):
            shape = x.shape
            xb = x.reshape(shape[:-1] + (shape[-1] // BLOCK, BLOCK))
            scale = jnp.max(jnp.abs(xb), axis=-1, keepdims=True) / 6.0
            scale = jnp.maximum(scale, jnp.float32(1e-12))
            xn = xb / scale
            idx = jnp.searchsorted(_MID, jnp.abs(xn))
            q = _GRID[idx] * jnp.sign(xn) * scale
            return q.reshape(shape)

        def fp4_linear(x, w):
            xq = fp4_quant_dequant(x)
            wq = fp4_quant_dequant(w)
            return jnp.einsum('bsk,nk->bsn', xq, wq)
        gate = fp4_linear(x, w_gate)
        y = fp4_linear(x, w_up)
        h = jax.nn.silu(gate) * y
        return fp4_linear(h, w_down)

    def _L1_attn_ref(enc_input, la_wqs, la_wks, la_wvs, la_pw, la_pb, la_g, la_b, lf_w1, lf_b1, lf_w2, lf_b2, lf_g, lf_b, sa_wqs, sa_wks, sa_wvs, sa_pw, sa_pb, sa_g, sa_b, pf_w1, pf_b1, pf_w2, pf_b2, pf_g, pf_b):
        import jax, jax.numpy as jnp
        import numpy as np
        B, L, D, H, DK, DV, DI, NL = (8, 256, 128, 16, 64, 64, 512, 32)
        EPS = 1e-05

        def _layernorm(x, g, b):
            mu = jnp.mean(x, axis=-1, keepdims=True)
            var = jnp.mean(jnp.square(x - mu), axis=-1, keepdims=True)
            return (x - mu) * jax.lax.rsqrt(var + EPS) * g + b

        def _mha(x, wqs, wks, wvs, pw, pb, g, b):
            dk = wqs.shape[-1]
            q = jnp.einsum('mld,hdk->mhlk', x, wqs)
            k = jnp.einsum('mld,hdk->mhlk', x, wks)
            v = jnp.einsum('mld,hdv->mhlv', x, wvs)
            scores = jnp.einsum('mhqk,mhsk->mhqs', q, k) / jnp.sqrt(jnp.asarray(dk, x.dtype))
            attn = jax.nn.softmax(scores, axis=-1)
            out = jnp.einsum('mhqs,mhsv->mhqv', attn, v) - v
            m, h, l, dv = out.shape
            out = out.transpose(0, 2, 1, 3).reshape(m, l, h * dv)
            out = out @ pw + pb
            return _layernorm(out + x, g, b)

        def _ffn(x, w1, b1, w2, b2, g, b):
            h = jax.nn.relu(x @ w1 + b1)
            return _layernorm(h @ w2 + b2 + x, g, b)
        b, l, d = enc_input.shape
        nl = NL
        x = enc_input.reshape(-1, nl, d)
        x = _mha(x, la_wqs, la_wks, la_wvs, la_pw, la_pb, la_g, la_b)
        x = _ffn(x, lf_w1, lf_b1, lf_w2, lf_b2, lf_g, lf_b)
        x = x.reshape(b, l // nl, nl, d).transpose(0, 2, 1, 3).reshape(-1, l // nl, d)
        x = _mha(x, sa_wqs, sa_wks, sa_wvs, sa_pw, sa_pb, sa_g, sa_b)
        x = _ffn(x, pf_w1, pf_b1, pf_w2, pf_b2, pf_g, pf_b)
        out = x.reshape(b, nl, l // nl, d).transpose(0, 2, 1, 3).reshape(b, l, d)
        return out

    def _L1_ffn_ref(x, Wqkv, q_scale, k_scale, Wo, ln_g, ln_b, W1, b1, W2, b2):
        import jax, jax.numpy as jnp
        import numpy as np
        DIM = 128
        DEPTH = 6
        HEADS = 16
        DIM_HEAD = 64
        WINDOW = 32
        INNER = HEADS * DIM_HEAD
        DIM_INNER = int(DIM * 4 * 2 / 3)
        QK_SCALE = 8.0

        def shift_tokens(t):
            a, s = jnp.split(t, 2, -1)
            s = jnp.pad(s, ((0, 0), (1, 0), (0, 0)))[:, :-1]
            return jnp.concatenate([a, s], -1)

        def l2norm(t):
            return t / jnp.maximum(jnp.linalg.norm(t, axis=-1, keepdims=True), 1e-12)

        def rotate_half(x):
            x1, x2 = jnp.split(x, 2, -1)
            return jnp.concatenate([-x2, x1], -1)

        def rotary_tables(n):
            half = jnp.arange(0, DIM_HEAD, 2, dtype=jnp.float32)
            inv_freq = 1.0 / 10000.0 ** (half / DIM_HEAD)
            t = jnp.arange(n, dtype=jnp.float32)
            freqs = t[:, None] * inv_freq[None, :]
            freqs = jnp.concatenate([freqs, freqs], -1)
            base_scale = (half + 0.4 * DIM_HEAD) / (1.4 * DIM_HEAD)
            power = (t - n // 2) / (WINDOW // 2)
            scale = base_scale[None, :] ** power[:, None]
            scale = jnp.concatenate([scale, scale], -1)
            return (freqs, scale)

        def local_attention(q, k, v):
            b, h, n, d = q.shape
            w = WINDOW
            nw = n // w
            bq = q.reshape(b, h, nw, w, d)
            bk = k.reshape(b, h, nw, w, d)
            bv = v.reshape(b, h, nw, w, d)

            def look(t):
                p = jnp.pad(t, ((0, 0), (0, 0), (1, 0), (0, 0), (0, 0)))
                return jnp.concatenate([p[:, :, :nw], p[:, :, 1:]], axis=3)
            bk2, bv2 = (look(bk), look(bv))
            seq = jnp.arange(n).reshape(nw, w)
            seq_p = jnp.pad(seq, ((1, 0), (0, 0)), constant_values=-1)
            jt = jnp.concatenate([seq_p[:nw], seq_p[1:]], axis=1)
            it = seq[:, :, None]
            jb = jt[:, None, :]
            mask = (it < jb) | (it > jb + w) | (jb == -1)
            sim = jnp.einsum('bhwie,bhwje->bhwij', bq, bk2) * QK_SCALE
            sim = jnp.where(mask, -jnp.finfo(sim.dtype).max, sim)
            attn = jax.nn.softmax(sim, -1)
            out = jnp.einsum('bhwij,bhwje->bhwie', attn, bv2)
            return out.reshape(b, h, n, d)

        def attn_layer(x, Wqkv, qs, ksc, Wo):
            b, n, _ = x.shape
            qkv = x @ Wqkv
            q, k, v = jnp.split(qkv, 3, -1)
            sh = lambda t: t.reshape(b, n, HEADS, DIM_HEAD).transpose(0, 2, 1, 3)
            q, k, v = (sh(q), sh(k), sh(v))
            q = l2norm(q) * qs
            k = l2norm(k) * ksc
            freqs, scale = rotary_tables(n)
            cos, sin = (jnp.cos(freqs), jnp.sin(freqs))
            q = q * cos * scale + rotate_half(q) * sin * scale
            inv = 1.0 / scale
            k = k * cos * inv + rotate_half(k) * sin * inv
            out = local_attention(q, k, v)
            out = out.transpose(0, 2, 1, 3).reshape(b, n, INNER)
            return out @ Wo

        def ffn_layer(x, g, bln, W1, b1, W2, b2):
            mu = x.mean(-1, keepdims=True)
            var = ((x - mu) ** 2).mean(-1, keepdims=True)
            xn = (x - mu) / jnp.sqrt(var + 1e-05) * g + bln
            hg = xn @ W1 + b1
            a, gate = jnp.split(hg, 2, -1)
            return a * jax.nn.gelu(gate, approximate=False) @ W2 + b2
        for i in range(DEPTH):
            x = attn_layer(shift_tokens(x), Wqkv[i], q_scale[i], k_scale[i], Wo[i]) + x
            x = ffn_layer(shift_tokens(x), ln_g[i], ln_b[i], W1[i], b1[i], W2[i], b2[i]) + x
        return x
    x = L0_attn_x
    x = x + _L0_attn_ref(_layernorm(x, axis=-1), L0_attn_w_qkv, L0_attn_w_proj, L0_attn_b_proj)
    x = x + _L0_ffn_ref(_layernorm(x, axis=-1), L0_ffn_w_gate, L0_ffn_w_up, L0_ffn_w_down)
    x = x + _L1_attn_ref(_layernorm(x, axis=-1), L1_attn_la_wqs, L1_attn_la_wks, L1_attn_la_wvs, L1_attn_la_pw, L1_attn_la_pb, L1_attn_la_g, L1_attn_la_b, L1_attn_lf_w1, L1_attn_lf_b1, L1_attn_lf_w2, L1_attn_lf_b2, L1_attn_lf_g, L1_attn_lf_b, L1_attn_sa_wqs, L1_attn_sa_wks, L1_attn_sa_wvs, L1_attn_sa_pw, L1_attn_sa_pb, L1_attn_sa_g, L1_attn_sa_b, L1_attn_pf_w1, L1_attn_pf_b1, L1_attn_pf_w2, L1_attn_pf_b2, L1_attn_pf_g, L1_attn_pf_b)
    x = x + _L1_ffn_ref(_layernorm(x, axis=-1), L1_ffn_Wqkv, L1_ffn_q_scale, L1_ffn_k_scale, L1_ffn_Wo, L1_ffn_ln_g, L1_ffn_ln_b, L1_ffn_W1, L1_ffn_b1, L1_ffn_W2, L1_ffn_b2)
    return x

_drawn_inputs = setup_inputs


def setup_inputs(seed=0):
    import zlib

    import numpy as np

    out = dict(_drawn_inputs(seed))
    spreads = {'L1_attn_la_pb': (0.0, 0.1),
     'L1_attn_la_g': (1.0, 0.2),
     'L1_attn_la_b': (0.0, 0.1),
     'L1_attn_lf_b1': (0.0, 0.505),
     'L1_attn_lf_b2': (0.0, 0.1),
     'L1_attn_lf_g': (1.0, 0.2),
     'L1_attn_lf_b': (0.0, 0.1),
     'L1_attn_sa_pb': (0.0, 0.1),
     'L1_attn_sa_g': (1.0, 0.2),
     'L1_attn_sa_b': (0.0, 0.1),
     'L1_attn_pf_b1': (0.0, 0.579),
     'L1_attn_pf_b2': (0.0, 0.1),
     'L1_attn_pf_g': (1.0, 0.2),
     'L1_attn_pf_b': (0.0, 0.1),
     'L1_ffn_q_scale': (1.0, 0.6),
     'L1_ffn_k_scale': (1.0, 0.6),
     'L1_ffn_ln_g': (1.0, 0.6),
     'L1_ffn_ln_b': (0.0, 0.8),
     'L1_ffn_b1': (0.0, 0.8),
     'L1_ffn_b2': (0.0, 0.1)}
    factors = {'L0_attn_b_proj': 5.717,
     'L0_ffn_w_gate': 5.701,
     'L0_ffn_w_up': 5.551,
     'L0_ffn_w_down': 5.552,
     'L1_attn_la_wqs': 8.0,
     'L1_attn_la_wks': 8.0,
     'L1_attn_sa_wqs': 8.0,
     'L1_attn_sa_wks': 8.0,
     'L1_ffn_W1': 5.407,
     'L1_ffn_W2': 5.307}
    for name, (base, spread) in spreads.items():
        noise = np.random.default_rng([zlib.crc32(name.encode()), seed]).standard_normal(out[name].shape)
        drawn = base * np.exp(spread * noise) if base else spread * noise
        out[name] = jnp.asarray(drawn.astype(out[name].dtype))
    for name, factor in factors.items():
        out[name] = (out[name] * factor).astype(out[name].dtype)
    return out
```

```python
from contextlib import ExitStack

import concourse.bass as bass
from concourse import mybir
from concourse.alu_op_type import AluOpType as ALU
import numpy as np

F32 = mybir.dt.float32
BF16 = mybir.dt.bfloat16
ACT = mybir.ActivationFunctionType
AX = mybir.AxisListType
ds = bass.ds

P = 128
D = 128
BATCH, SEQ = 2, 2048
TOK = BATCH * SEQ
NT = TOK // P
NTB = SEQ // P
CH = 4
NC = NT // CH
CW = CH * P
EPS = 1e-5
W32 = 32

H0, HD0 = 16, 8
NPART = 3
KST = NPART * NPART * HD0
MROW = 96
HPG = 4
NG0 = H0 // HPG
QC = 512

H, HD = 16, 64
INNER = H * HD
HP = H // 2
DEPTH = 6
F0 = 352
FB = 16
F1 = 512
F2 = 341
NJ2 = 3
JW2 = [128, 128, F2 - 256]
ONE_ROW = 96


def counter(eng):
    def need(sem, i, per=1, extra=0):
        if isinstance(i, int) and i < 0:
            return
        eng.wait_ge(sem, (i + 1) * per + extra)
    return need


def lagged(eng, n, unroll, lag, ahead, emit, peel=0):
    head = max(lag + (-lag) % unroll, peel)
    rounds = (n - head - ahead) // unroll
    for t in range(head):
        emit(t, t % unroll)
    if rounds > 0:
        with eng.Fori(0, rounds) as r:
            for p in range(unroll):
                emit(r * unroll + (head + p), p)
    for t in range(head + rounds * unroll, n + lag):
        emit(t, t % unroll)


def has(t, n):
    return not isinstance(t, int) or 0 <= t < n


class Kit:
    def __init__(self, nc, ctx, tag):
        self.nc, self.ctx, self.tag = nc, ctx, tag
        self.sems = []
        ctx.callback(self.clear)

    def sb(self, name, shape, dt=F32):
        return self.ctx.enter_context(self.nc.sbuf_tensor(self.tag + name, shape, dt))

    def ps(self, name, shape, dt=F32):
        return self.ctx.enter_context(self.nc.psum_tensor(self.tag + name, shape, dt))

    def sem(self, name):
        self.sems.append(self.nc.alloc_semaphore(name=self.tag + name))
        return self.sems[-1]

    def clear(self):
        if self.sems:
            self.nc.clear_and_free_semaphores(self.sems)
            self.nc.all_engine_barrier()


def bcast(ap, n):
    return ap.unsqueeze(2).broadcast_to([ap.shape[0], ap.shape[1], n])


def fetch(sp, moves, arrived):
    if not moves:
        return
    for to, src in moves:
        sp.dma_start(to, src).then_inc(arrived, 16)
    sp.wait_ge(arrived, 16 * len(moves))


def move_pass(nc, tag, moves):
    with ExitStack() as ctx:
        k = Kit(nc, ctx, tag)
        moved = k.sem("moved")
        block = ctx.enter_context(nc.Block())

        @block.sync
        def _(sp):
            fetch(sp, moves, moved)


def add_norm_pass(nc, tag, X, Y, add):
    with ExitStack() as ctx:
        k = Kit(nc, ctx, tag)
        st, mv = k.sb("st", [P, NT, 6]), k.sb("mv", [P, NT, 2])
        sd, rs = k.sb("sd", [P, NT]), k.sb("rs", [P, NT])
        eps = k.sb("eps", [P, 1])
        momented, rooted = k.sem("momented"), k.sem("rooted")
        block = ctx.enter_context(nc.Block())

        @block.scalar
        def _(act):
            act.wait_ge(momented, 1)
            nc.scalar.activation(sd[:, :], mv[:, :, 1], ACT.Sqrt, bias=eps[:, 0:1]).then_inc(rooted, 1)

        @block.vector
        def _(dve):
            nc.vector.memset(eps[:, :], EPS)
            if add:
                with dve.Fori(0, NC) as c:
                    x4 = X[:, ds(c * CH, CH), :]
                    nc.vector.tensor_tensor(out=x4, in0=x4, in1=Y[:, ds(c * CH, CH), :], op=ALU.add)
                dve.drain()
            with dve.Fori(0, NC) as c:
                for i in range(CH):
                    nc.vector.bn_stats(st[:, ds(c * CH + i, 1), :].rearrange("p a s -> p (a s)"),
                                       X[:, ds(c * CH + i, 1), :].rearrange("p a f -> p (a f)"))
            dve.drain()
            for t in range(NT):
                nc.vector.bn_aggr(mv[:, t, :], st[:, t, :])
            dve.drain().then_inc(momented, 1)
            dve.wait_ge(rooted, 1)
            nc.vector.reciprocal(rs[:, :], sd[:, :])
            dve.drain()
            with dve.Fori(0, NC) as c:
                for i in range(CH):
                    t = c * CH + i
                    nc.vector.tensor_scalar(Y[:, ds(t, 1), :].rearrange("p a f -> p (a f)"),
                                            X[:, ds(t, 1), :].rearrange("p a f -> p (a f)"),
                                            mv[:, ds(t, 1), 0:1].rearrange("p a s -> p (a s)"), rs[:, ds(t, 1)],
                                            ALU.subtract, ALU.mult)


def add_pass(nc, X, Y):
    with nc.Block() as block:

        @block.vector
        def _(dve):
            with dve.Fori(0, NC) as c:
                x4 = X[:, ds(c * CH, CH), :]
                nc.vector.tensor_tensor(out=x4, in0=x4, in1=Y[:, ds(c * CH, CH), :], op=ALU.add)


def load_pass(nc, const, X, x):
    with ExitStack() as ctx:
        k = Kit(nc, ctx, "ld_")
        loaded = k.sem("loaded")
        block = ctx.enter_context(nc.Block())

        @block.sync
        def _(sp):
            sp.dma_start(X[:, :, :], x.rearrange("b (t p) f -> p (b t) f", p=P)).then_inc(loaded, 16)
            sp.dma_start(const["ident"][:, :], const["ident_d"]).then_inc(loaded, 16)
            sp.dma_start(const["identb"][:, :], const["identb_d"]).then_inc(loaded, 16)
            sp.wait_ge(loaded, 48)

        @block.vector
        def _(dve):
            nc.vector.memset(const["eps"][:, :], EPS)


def store_pass(nc, X, out):
    with ExitStack() as ctx:
        k = Kit(nc, ctx, "st_")
        stored = k.sem("stored")
        block = ctx.enter_context(nc.Block())

        @block.sync
        def _(sp):
            sp.dma_start(out.rearrange("b (t p) f -> p (b t) f", p=P), X[:, :, :]).then_inc(stored, 16)
            sp.wait_ge(stored, 16)


def attention_pass(nc, tag, kind, R, w, const, prefetch=()):
    local = kind == "local"
    W = 32 if kind == "w32" else 64
    SCALE = 8.0 if local else 1.0 / 8.0
    with ExitStack() as ctx:
        k = Kit(nc, ctx, tag)
        xt = k.sb("xt", [P, 2, D])
        xs = k.sb("xs", [P, 2, P])
        carry = k.sb("carry", [P, 2])
        qT = k.sb("qT", [P, HP, P])
        kT = k.sb("kT", [P, 2, HP, W32 + P])
        v = k.sb("v", [P, 2, INNER])
        z = k.sb("z", [P, H * W])
        pr = k.sb("pr", [P, H * W])
        pn = k.sb("pn", [P, H * W])
        pT = k.sb("pT", [P, H, W // 32, 32])
        band = k.sb("band", [P, H, P])
        edge = k.sb("edge", [P, H, W32]) if local else None
        oT = k.sb("oT", [P, HP, P])
        mx = k.sb("mx", [P, H])
        sm = k.sb("sm", [P, H])
        rs = k.sb("rs", [P, H])
        if local:
            sq = k.sb("sq", [P, 2, 512])
            ss = k.sb("ss", [P, 2 * H])
            nr = k.sb("nr", [P, 2 * H])
            rn = k.sb("rn", [P, 2 * H])
            qc = k.sb("qc", [P, 4, 512])
            qs = k.sb("qs", [P, 4, 512])
            qn = k.sb("qn", [P, 4, 512])
            rot = k.sb("rot", [P, 2, 256])

        pj = k.ps("pj", [P, 2, 512])
        pt = k.ps("pt", [P, 2, 512])
        pS = k.ps("pS", [P, 2, 512])
        pO = k.ps("pO", [P, 2, 512])

        x_in = k.sem("x_in")
        x_T = k.sem("x_T")
        x_s = k.sem("x_s")
        projected = k.sem("projected")
        squared = k.sem("squared")
        rotated = k.sem("rotated")
        added = k.sem("added")
        clamped = k.sem("clamped")
        rooted = k.sem("rooted")
        normed = k.sem("normed")
        rot_ready = k.sem("rot_ready")
        t_ps = k.sem("t_ps")
        t_sb = k.sem("t_sb")
        k_next = k.sem("k_next")
        scored = k.sem("scored")
        shifted = k.sem("shifted")
        exped = k.sem("exped")
        scaled = k.sem("scaled")
        p_T = k.sem("p_T")
        banded = k.sem("banded")
        v_ps = k.sem("v_ps")
        v_sb = k.sem("v_sb")
        o_ps = k.sem("o_ps")
        o_sb = k.sem("o_sb")
        y_ps = k.sem("y_ps")
        y_sb = k.sem("y_sb")
        zeroed = k.sem("zeroed")
        fetched = k.sem("fetched")
        block = ctx.enter_context(nc.Block())

        @block.sync
        def _(sp):
            fetch(sp, prefetch, fetched)

        def heads(ap):
            return ap.rearrange("p (r h w) -> p (r h) w", r=2, w=W)

        S4 = pS[:, :, 0:HP * W].rearrange("p r (h w) -> p r h w", w=W)
        if W == 64:
            S3 = pS[:, :, :].rearrange("p r (h w) -> p (r h) w", w=W)

        @block.tensor
        def _(pe):
            need = counter(pe)
            need(zeroed, 0)

            def x_transpose(t, p):
                need(x_in, t)
                if isinstance(t, int) and t == 1:
                    need(x_s, 0)
                need(t_sb, t - 2, 4, 0)
                nc.tensor.transpose(pt[:, 0, 0:P], xt[:, p, :], const["ident"][:, :]).then_inc(x_T, 1)

            def qk_chunk(t, p, c):
                if c == 0:
                    need(x_s, t)
                if c >= 2:
                    need(squared, t, 4, c - 5)
                    need(rotated, t, 4, c - 5)
                else:
                    need(v_sb, t - 2, 2, c - 1)
                nc.tensor.matmul(pj[:, c % 2, :], xs[:, p, :], w["wqk"][:, c * 512:(c + 1) * 512],
                                 start=True, stop=True).then_inc(projected, 1)

            def qk_features(t, p):
                for c in range(4):
                    if c == 0:
                        need(x_s, t + 1 if has(t + 1, NT) else t)
                    if c == 1:
                        need(y_sb, t - 2)
                    if c >= 2:
                        need(t_sb, t, 4, c - 5)
                    if local:
                        need(normed, t, 4, c - 3)
                    for i in range(4):
                        o = pt[:, c % 2, i * P:(i + 1) * P]
                        if local:
                            last = nc.tensor.transpose(o, qn[:, c, i * P:(i + 1) * P], const["ident"][:, :])
                        else:
                            col = (c * 4 + i) * P
                            last = nc.tensor.matmul(o, w["wqk"][:, col:col + P], xs[:, p, :],
                                                    start=True, stop=True)
                    last.then_inc(t_ps, 1)

            def scores(t, p, r):
                if r == 0:
                    need(t_sb, t, 4)
                    if local:
                        need(k_next, t - 1)
                    need(shifted, t - 1)
                    if not local:
                        nc.tensor.matmul(pS[:, 0, 0:2], const["identb"][:, :], const["identb"][:, 0:2],
                                         start=True, stop=True, skip_group_check=True)
                if local:
                    nc.tensor.matmul(pS[:, r, :], const["identb"][:, :],
                                     w["mask"][:, ds(t, 1), :].broadcast_to([P, HP, 64]),
                                     start=True, stop=False, skip_group_check=True)
                for i in range(HP):
                    n = P // (32 if local else W)
                    m = P // n
                    for q in range(n):
                        lo = m * q if local else W32 + m * q
                        last = nc.tensor.matmul(
                            pS[m * q:m * (q + 1), r, i * W:(i + 1) * W],
                            qT[64 * r:64 * r + 64, i, m * q:m * (q + 1)],
                            kT[64 * r:64 * r + 64, p, i, lo:lo + W],
                            start=not local, stop=True, skip_group_check=True)
                if r == 1:
                    last.then_inc(scored, 1)

            def attend(t, p):
                need(banded, t)
                need(v_sb, t, 2)
                need(o_sb, t - 1)
                for i in range(HP):
                    for r in range(2):
                        o = pO[64 * r:64 * r + 64, i // 4, (i % 4) * P:(i % 4 + 1) * P]
                        h = r * HP + i
                        col = (2 * i + r) * HD
                        last = nc.tensor.matmul(o, v[:, p, col:col + HD], band[:, h, :],
                                                start=True, stop=not local)
                        if local:
                            last = nc.tensor.matmul(o[:, 0:W32], v[:, 1 - p, col:col + HD], edge[:, h, :],
                                                    start=False, stop=True)
                last.then_inc(o_ps, 1)

            def v_chunks(t, p):
                for c in range(2):
                    if local and has(t + 1, NT):
                        need(squared, t + 1, 4, c - 1)
                        need(rotated, t + 1, 4, c - 1)
                    else:
                        need(v_sb, t - 1, 2, c - 1)
                    nc.tensor.matmul(pj[:, c, :], xs[:, p, :], w["wv"][:, c * 512:(c + 1) * 512],
                                     start=True, stop=True).then_inc(v_ps, 1)

            def project(t):
                need(o_sb, t)
                if has(t + 1, NT):
                    need(t_sb, t + 1, 4)
                else:
                    need(y_sb, t - 1)
                for i in range(HP):
                    last = nc.tensor.matmul(pt[:, 1, 0:D], oT[:, i, :], w["wo"][:, i, :],
                                            start=(i == 0), stop=(i == HP - 1))
                last.then_inc(y_ps, 1)

            def step(t, p):
                if isinstance(t, int) and t == 0:
                    x_transpose(0, 0)
                now, one, two = has(t, NT), has(t - 1, NT), has(t - 2, NT)
                if local and now:
                    qk_chunk(t, p, 0)
                    qk_chunk(t, p, 1)
                if one:
                    qk_features(t - 1, 1 - p)
                if has(t + 1, NT):
                    x_transpose(t + 1, 1 - p)
                if one:
                    scores(t - 1, 1 - p, 0)
                if local and now:
                    qk_chunk(t, p, 2)
                if one:
                    scores(t - 1, 1 - p, 1)
                if local and now:
                    qk_chunk(t, p, 3)
                if two:
                    attend(t - 2, p)
                if one:
                    v_chunks(t - 1, 1 - p)
                if two:
                    project(t - 2)

            lagged(pe, NT, 2, 2, 2, step)

        @block.scalar
        def _(act):
            need = counter(act)

            def x_copy(t, p):
                need(x_T, t - 2)
                nc.scalar.copy(xt[:, p, :], R[:, ds(t, 1), :].rearrange("p a f -> p (a f)")).then_inc(x_in, 1)

            def step(t, p):
                one = has(t - 1, NT)
                two = has(t - 2, NT)
                if isinstance(t, int) and t == 0:
                    x_copy(0, 0)
                    x_copy(1, 1)
                if local and has(t, NT):
                    for c in range(2):
                        need(projected, t, 4, c - 3)
                        need(rotated, t, 4, c - 5) if not isinstance(t, int) or t > 0 else None
                        nc.scalar.activation(sq[:, c % 2, :], pj[:, c % 2, :], ACT.Square).then_inc(squared, 1)
                if one:
                    for c in range(4):
                        need(t_ps, t - 1, 4, c - 3)
                        if c == 0:
                            need(scored, t - 2)
                        src = pt[:, c % 2, :].rearrange("p (a n) -> p a n", n=P)
                        dst = (qT[:, 4 * c:4 * c + 4, :] if c < 2 else
                               kT[:, 1 - p, 4 * (c - 2):4 * (c - 2) + 4, W32:])
                        nc.scalar.copy(dst, src).then_inc(t_sb, 1)
                    if local:
                        need(t_sb, t - 1, 4)
                        nc.scalar.activation(kT[:, p, :, 0:W32], kT[:, 1 - p, :, P:P + W32], ACT.Copy,
                                             scale=w["kfac"][:, 0:1]).then_inc(k_next, 1)
                if has(t + 2, NT):
                    x_copy(t + 2, p)
                if local and has(t, NT):
                    for c in range(2, 4):
                        need(projected, t, 4, c - 3)
                        need(rotated, t, 4, c - 5)
                        nc.scalar.activation(sq[:, c % 2, :], pj[:, c % 2, :], ACT.Square).then_inc(squared, 1)
                    need(clamped, t)
                    nc.scalar.activation(nr[:, :], ss[:, :], ACT.Sqrt).then_inc(rooted, 1)
                if one:
                    need(shifted, t - 1)
                    need(scaled, t - 2)
                    nc.scalar.activation(pr[:, :], z[:, :], ACT.Exp, scale=SCALE).then_inc(exped, 1)
                if two:
                    need(o_ps, t - 2)
                    need(y_ps, t - 3)
                    nc.scalar.copy(oT[:, :, :].rearrange("p h q -> p (h q)"),
                                   pO[:, :, :].rearrange("p a b -> p (a b)")).then_inc(o_sb, 1)
                if one:
                    for c in range(2):
                        need(v_ps, t - 1, 2, c - 1)
                        nc.scalar.copy(v[:, 1 - p, c * 512:(c + 1) * 512], pj[:, c, :]).then_inc(v_sb, 1)
                if one:
                    need(p_T, t - 1)
                    need(o_ps, t - 2)
                    if kind == "w64":
                        moves = [(64 * a + 32 * kb, 64 * a + 32 * qb, kb) for a in range(2)
                                 for kb in range(2) for qb in range(2)]
                    elif kind == "w32":
                        moves = [(32 * a, 32 * a, 0) for a in range(4)]
                    else:
                        moves = [(32 * a, 32 * a, 1) for a in range(4)] + [(32 * a - 32, 32 * a, 0) for a in range(4)]
                    for kp, qp, kb in moves:
                        dst = (band[kp:kp + 32, :, qp:qp + 32] if kp >= 0 else edge[96:128, :, :])
                        last = nc.scalar.copy(dst, pT[qp:qp + 32, :, kb, :])
                    last.then_inc(banded, 1)

            lagged(act, NT, 2, 2, 2, step)

        @block.vector
        def _(dve):
            need = counter(dve)
            nc.vector.memset(band[:, :, :], 0.0)
            if local:
                nc.vector.memset(edge[:, :, :], 0.0)
                nc.vector.memset(carry[:, :], 0.0)
                nc.vector.memset(kT[:, 0, :, 0:W32], 0.0)
                nc.vector.memset(v[:, 1, :], 0.0)
            dve.drain()
            nc.vector.memset(mx[:, :], 0.0).then_inc(zeroed, 1)

            def x_shift(t, p):
                need(x_T, t)
                need(v_ps, t - 2, 2)
                if not local:
                    nc.vector.tensor_copy(xs[:, p, :], pt[:, 0, 0:P]).then_inc(x_s, 1)
                    return
                nc.vector.tensor_tensor(out=xs[64:128, p, 0:1], in0=carry[64:128, 1 - p:2 - p],
                                        in1=w["inner"][64:128, ds(t, 1)], op=ALU.mult)
                nc.vector.tensor_copy(carry[64:128, p:p + 1], pt[64:128, 0, P - 1:P])
                nc.vector.tensor_copy(xs[0:64, p, :], pt[0:64, 0, 0:P])
                nc.vector.tensor_copy(xs[64:128, p, 1:P], pt[64:128, 0, 0:P - 1])
                dve.drain().then_inc(x_s, 1)

            def rotate(t, p, c):
                if c == 0:
                    need(rot_ready, t)
                need(projected, t, 4, c - 3)
                need(squared, t, 4, c - 3)
                need(added, t - 1, 4, c - 3)
                src = pj[:, c % 2, :].rearrange("p (h d) -> p h d", d=HD)
                tab = rot[:, p, 128 * (c // 2):128 * (c // 2) + 128]
                for d, o in ((qc, 0), (qs, HD)):
                    last = nc.vector.tensor_tensor(
                        out=d[:, c, :].rearrange("p (h d) -> p h d", d=HD), in0=src,
                        in1=tab[:, o:o + HD].unsqueeze(1).broadcast_to([P, 8, HD]), op=ALU.mult)
                nc.vector.tensor_reduce(ss[:, 8 * c:8 * c + 8], sq[:, c % 2, :].rearrange("p (h d) -> p h d", d=HD),
                                        AX.X, ALU.add).then_inc(rotated, 1)

            def step(t, p):
                one = has(t - 1, NT)
                two = has(t - 2, NT)
                if isinstance(t, int) and t == 0:
                    x_shift(0, 0)
                if local and has(t, NT):
                    rotate(t, p, 0)
                    rotate(t, p, 1)
                if local and has(t, NT):
                    rotate(t, p, 2)
                    rotate(t, p, 3)
                    dve.drain()
                    nc.vector.tensor_scalar(ss[:, :], ss[:, :], 1e-24, None, ALU.max).then_inc(clamped, 1)
                if one:
                    need(scored, t - 1)
                    if W == 64:
                        nc.vector.tensor_reduce(mx[:, :], S3, AX.X, ALU.max)
                    else:
                        nc.vector.tensor_reduce(mx[:, :].rearrange("p (r h) -> p r h", r=2), S4, AX.X, ALU.max)
                    dve.drain()
                    need(exped, t - 2)
                    if W == 64:
                        nc.vector.tensor_tensor(out=heads(z[:, :]), in0=S3, in1=bcast(mx[:, :], W),
                                                op=ALU.subtract).then_inc(shifted, 1)
                    else:
                        for r in range(2):
                            last = nc.vector.tensor_tensor(
                                out=z[:, r * HP * W:(r + 1) * HP * W].rearrange("p (h w) -> p h w", w=W),
                                in0=S4[:, r], in1=bcast(mx[:, r * HP:(r + 1) * HP], W), op=ALU.subtract)
                        last.then_inc(shifted, 1)
                if local and has(t, NT):
                    need(rooted, t)
                    nc.vector.reciprocal(rn[:, :], nr[:, :])
                    dve.drain()
                    for c in range(4):
                        need(added, t, 4, c - 3)
                        need(t_ps, t - 1, 4, c - 3)
                        nc.vector.tensor_tensor(
                            out=qn[:, c, :].rearrange("p (h d) -> p h d", d=HD),
                            in0=qc[:, c, :].rearrange("p (h d) -> p h d", d=HD),
                            in1=bcast(rn[:, 8 * c:8 * c + 8], HD), op=ALU.mult).then_inc(normed, 1)
                if one:
                    need(exped, t - 1)
                    nc.vector.tensor_reduce(sm[:, :], heads(pr[:, :]), AX.X, ALU.add)
                    dve.drain()
                    nc.vector.reciprocal(rs[:, :], sm[:, :])
                    dve.drain()
                    nc.vector.tensor_tensor(out=heads(pn[:, :]), in0=heads(pr[:, :]), in1=bcast(rs[:, :], W),
                                            op=ALU.mult).then_inc(scaled, 1)
                    dve.drain()
                    if not local:
                        nc.vector.tensor_tensor(out=heads(pn[:, :]), in0=heads(pn[:, :]),
                                                in1=w["own"][:, 0:W].unsqueeze(1).broadcast_to([P, H, W]),
                                                op=ALU.subtract)
                        dve.drain()
                    need(banded, t - 2)
                    nc.vector.transpose(pT[:, :, :, :].rearrange("p h a b -> p (h a b)"), pn[:, :]).then_inc(p_T, 1)
                if has(t + 1, NT):
                    x_shift(t + 1, 1 - p)
                if two:
                    need(y_ps, t - 2)
                    r2 = R[:, ds(t - 2, 1), :].rearrange("p a f -> p (a f)")
                    if "pb" in w:
                        nc.vector.tensor_tensor(out=r2, in0=r2, in1=w["pb"][:, :], op=ALU.add)
                        dve.drain()
                    nc.vector.tensor_tensor(out=r2, in0=r2, in1=pt[:, 1, 0:D], op=ALU.add).then_inc(y_sb, 1)

            lagged(dve, NT, 2, 2, 2, step)

        if local:
            @block.gpsimd
            def _(pool):
                need = counter(pool)

                def step(t, p):
                    if not has(t, NT):
                        return
                    need(rotated, t - 2, 4)
                    nc.gpsimd.tensor_tensor(out=rot[:, p, :], in0=w["rot"][:, ds(t, 1), :].rearrange("p a f -> p (a f)"),
                                            in1=w["qk_scale"][:, :], op=ALU.mult).then_inc(rot_ready, 1)
                    for c in range(4):
                        need(rotated, t, 4, c - 3)
                        a = qc[:, c, :].rearrange("p (h e d) -> p h e d", e=2, d=32)
                        b = qs[:, c, :].rearrange("p (h e d) -> p h e d", e=2, d=32)
                        for e in range(2):
                            last = nc.gpsimd.tensor_tensor(out=a[:, :, e, :], in0=a[:, :, e, :],
                                                           in1=b[:, :, 1 - e, :], op=ALU.add)
                        last.then_inc(added, 1)

                lagged(pool, NT, 2, 2, 2, step)


def moments(nc, dve, st, mv, src):
    for i in range(CH):
        nc.vector.bn_stats(st[:, i, :], src[:, i, :])
    dve.drain()
    for i in range(CH):
        last = nc.vector.bn_aggr(mv[:, i, :], st[:, i, :])
    return last


def normalise(nc, dve, out, src, mv, sd, rs):
    nc.vector.reciprocal(rs[:, :], sd[:, :])
    dve.drain()
    for i in range(CH):
        last = nc.vector.tensor_scalar(out[:, i, :], src[:, i, :], mv[:, i, 0:1], rs[:, i:i + 1],
                                       ALU.subtract, ALU.mult)
    return last


def gated_pass(nc, tag, R, w, const, prefetch=()):
    with ExitStack() as ctx:
        k = Kit(nc, ctx, tag)
        xt = k.sb("xt", [P, 2, CH, D])
        xs = k.sb("xs", [P, CW])
        carry = k.sb("carry", [P, 2])
        st = k.sb("st", [P, CH, 6])
        mv = k.sb("mv", [P, CH, 2])
        sd = k.sb("sd", [P, CH])
        rs = k.sb("rs", [P, CH])
        xn = k.sb("xn", [P, CH, D])
        xnT = k.sb("xnT", [P, 2, CW])
        gl = k.sb("gl", [P, 2, CW])
        hT = k.sb("hT", [P, NJ2, CW])
        pa = k.ps("pa", [P, CW])
        pb = k.ps("pb", [P, CW])
        pg = k.ps("pg", [P, 2, CW])
        ph = k.ps("ph", [P, 2, CW])
        py = k.ps("py", [P, CW])
        x_in, x_T, x_s = k.sem("x_in"), k.sem("x_T"), k.sem("x_s")
        s_ps = k.sem("s_ps")
        momented, rooted = k.sem("momented"), k.sem("rooted")
        n_sb, n_ps, n_T = k.sem("n_sb"), k.sem("n_ps"), k.sem("n_T")
        gate_ps, gate_sb = k.sem("gate_ps"), k.sem("gate_sb")
        a_ps, h_sb = k.sem("a_ps"), k.sem("h_sb")
        y_ps, y_sb = k.sem("y_ps"), k.sem("y_sb")
        ready = k.sem("ready")
        fetched = k.sem("fetched")
        block = ctx.enter_context(nc.Block())

        @block.sync
        def _(sp):
            fetch(sp, prefetch, fetched)

        def fm(ap):
            return ap.rearrange("p (a n) -> p a n", n=P)

        @block.tensor
        def _(pe):
            need = counter(pe)
            pe.wait_ge(ready, 1)

            def hidden(c, p, j):
                m = JW2[j]
                need(n_T, c)
                need(gate_sb, c, NJ2, j - 2 - NJ2 + 1) if not isinstance(c, int) or NJ2 * c + j >= 2 else None
                nc.tensor.matmul(pg[0:m, (NJ2 * p + j) % 2, :], w["w1"][:, F2 + 128 * j:F2 + 128 * j + m],
                                 xnT[:, p, :], start=True, stop=True).then_inc(gate_ps, 1)
                need(h_sb, c, NJ2, j - 2 - NJ2 + 1) if not isinstance(c, int) or NJ2 * c + j >= 2 else None
                nc.tensor.matmul(ph[0:m, (NJ2 * p + j) % 2, :], w["w1"][:, 128 * j:128 * j + m],
                                 xnT[:, p, :], start=True, stop=True).then_inc(a_ps, 1)

            def step(c, p):
                now, one = has(c, NC), has(c - 1, NC)
                if now:
                    need(x_in, c)
                    need(n_T, c - 1)
                    for i in range(CH):
                        last = nc.tensor.transpose(pa[:, i * P:(i + 1) * P], xt[:, p, i, :], const["ident"][:, :])
                    last.then_inc(x_T, 1)
                if one:
                    hidden(c - 1, 1 - p, 0)
                if now:
                    need(x_s, c)
                    need(n_sb, c - 1)
                    for i in range(CH):
                        last = nc.tensor.transpose(pb[:, i * P:(i + 1) * P], xs[:, i * P:(i + 1) * P], const["ident"][:, :])
                    last.then_inc(s_ps, 1)
                if one:
                    hidden(c - 1, 1 - p, 1)
                    hidden(c - 1, 1 - p, 2)
                    need(h_sb, c - 1, NJ2)
                    need(y_sb, c - 2)
                    for i in range(CH):
                        for j in range(NJ2):
                            m = P if j < NJ2 - 1 else ONE_ROW + 1
                            last = nc.tensor.matmul(py[:, i * P:(i + 1) * P], hT[0:m, j, i * P:(i + 1) * P],
                                                    w["w2"][0:m, j, :], start=(j == 0), stop=(j == NJ2 - 1))
                    last.then_inc(y_ps, 1)
                if now:
                    need(n_sb, c)
                    for i in range(CH):
                        last = nc.tensor.transpose(pa[:, i * P:(i + 1) * P], xn[:, i, :], const["ident"][:, :])
                    last.then_inc(n_ps, 1)

            lagged(pe, NC, 2, 1, 1, step)

        @block.scalar
        def _(act):
            need = counter(act)

            def x_copy(c, p):
                need(x_T, c - 2)
                nc.scalar.copy(xt[:, p, :, :], R[:, ds(c * CH, CH), :]).then_inc(x_in, 1)

            def step(c, p):
                now, one = has(c, NC), has(c - 1, NC)
                if isinstance(c, int) and c == 0:
                    x_copy(0, 0)
                if has(c + 1, NC):
                    x_copy(c + 1, 1 - p)
                if one:
                    for j in range(NJ2):
                        m = JW2[j]
                        need(gate_ps, c - 1, NJ2, j - NJ2 + 1)
                        if not isinstance(c, int) or NJ2 * (c - 1) + j >= 2:
                            need(h_sb, c - 1, NJ2, j - 2 - NJ2 + 1)
                        nc.scalar.activation(gl[0:m, (NJ2 * (1 - p) + j) % 2, :], pg[0:m, (NJ2 * (1 - p) + j) % 2, :],
                                             ACT.Gelu, bias=w["b1g"][0:m, j:j + 1]).then_inc(gate_sb, 1)
                if now:
                    need(momented, c)
                    nc.scalar.activation(sd[:, :], mv[:, :, 1], ACT.Sqrt, bias=const["eps"][:, 0:1]).then_inc(rooted, 1)
                    need(n_ps, c)
                    need(a_ps, c - 2, NJ2)
                    nc.scalar.activation(xnT[:, p, :], pa[:, :], ACT.Identity, scale=w["g"][:, 0:1],
                                         bias=w["b"][:, 0:1]).then_inc(n_T, 1)

            lagged(act, NC, 2, 1, 1, step)

        @block.vector
        def _(dve):
            need = counter(dve)
            nc.vector.memset(carry[:, :], 0.0)
            nc.vector.memset(hT[64:128, NJ2 - 1, :], 0.0)
            dve.drain()
            nc.vector.memset(hT[ONE_ROW:ONE_ROW + 1, NJ2 - 1, :], 1.0).then_inc(ready, 1)
            dve.drain()

            def step(c, p):
                now, one = has(c, NC), has(c - 1, NC)
                if now:
                    need(x_T, c)
                    need(s_ps, c - 1)
                    nc.vector.tensor_tensor(out=xs[64:128, 0:1], in0=carry[64:128, 1 - p:2 - p],
                                            in1=w["inner"][64:128, ds(c * CH, 1)], op=ALU.mult)
                    nc.vector.tensor_copy(carry[64:128, p:p + 1], pa[64:128, CW - 1:CW])
                    nc.vector.tensor_copy(xs[0:64, :], pa[0:64, :])
                    nc.vector.tensor_copy(xs[64:128, 1:CW], pa[64:128, 0:CW - 1])
                    dve.drain().then_inc(x_s, 1)
                    need(s_ps, c)
                    moments(nc, dve, st, mv, fm(pb[:, :])).then_inc(momented, 1)
                if one:
                    for j in range(NJ2):
                        m = JW2[j]
                        need(gate_sb, c - 1, NJ2, j - NJ2 + 1)
                        need(a_ps, c - 1, NJ2, j - NJ2 + 1)
                        need(y_ps, c - 2)
                        b = (NJ2 * (1 - p) + j) % 2
                        nc.vector.scalar_tensor_tensor(out=hT[0:m, j, :], in0=ph[0:m, b, :],
                                                       scalar=w["b1a"][0:m, j:j + 1], in1=gl[0:m, b, :],
                                                       op0=ALU.add, op1=ALU.mult).then_inc(h_sb, 1)
                if now:
                    need(rooted, c)
                    need(n_ps, c - 1)
                    normalise(nc, dve, xn, fm(pb[:, :]), mv, sd, rs).then_inc(n_sb, 1)
                if one:
                    need(y_ps, c - 1)
                    need(x_T, c - 1)
                    r4 = R[:, ds((c - 1) * CH, CH), :]
                    nc.vector.tensor_tensor(out=r4, in0=r4, in1=fm(py[:, :]), op=ALU.add).then_inc(y_sb, 1)

            lagged(dve, NC, 2, 1, 1, step)


def relu_pass(nc, tag, R, w, const):
    NJ = F1 // P
    with ExitStack() as ctx:
        k = Kit(nc, ctx, tag)
        st = k.sb("st", [P, 2, CH, 6])
        mv = k.sb("mv", [P, 2, CH, 2])
        sd = k.sb("sd", [P, 2, CH])
        rs = k.sb("rs", [P, 2, CH])
        xn = k.sb("xn", [P, CH, D])
        x1 = k.sb("x1", [P, 2, CH, D])
        x1T = k.sb("x1T", [P, 2, CW])
        hT = k.sb("hT", [P, NJ, CW])
        r2 = k.sb("r2", [P, CH, D])
        yn = k.sb("yn", [P, CH, D])
        pa = k.ps("pa", [P, CW])
        ph = k.ps("ph", [P, NJ, CW])
        py = k.ps("py", [P, CW])
        momented, rooted, n_sb = k.sem("momented"), k.sem("rooted"), k.sem("n_sb")
        gained, x1_sb, x_ps, x_T = k.sem("gained"), k.sem("x1_sb"), k.sem("x_ps"), k.sem("x_T")
        h_ps, h_sb, y_ps = k.sem("h_ps"), k.sem("h_sb"), k.sem("y_ps")
        y_in = k.sem("y_in")
        momented2, rooted2, n2_sb = k.sem("momented2"), k.sem("rooted2"), k.sem("n2_sb")
        gained2, done = k.sem("gained2"), k.sem("done")
        block = ctx.enter_context(nc.Block())

        def fm(ap):
            return ap.rearrange("p (a n) -> p a n", n=P)

        def wide(ap):
            return ap.unsqueeze(1).broadcast_to([P, CH, D])

        @block.tensor
        def _(pe):
            need = counter(pe)

            def step(c, p):
                if has(c, NC):
                    need(x1_sb, c)
                    need(x_T, c - 1)
                    for i in range(CH):
                        last = nc.tensor.transpose(pa[:, i * P:(i + 1) * P], x1[:, p, i, :], const["ident"][:, :])
                    last.then_inc(x_ps, 1)
                if has(c - 1, NC):
                    need(x_T, c - 1)
                    for j in range(NJ):
                        need(h_sb, c - 2, NJ, j - NJ + 1)
                        nc.tensor.matmul(ph[:, j, :], w["w1"][:, j * P:(j + 1) * P], x1T[:, 1 - p, :],
                                         start=True, stop=True).then_inc(h_ps, 1)
                    need(h_sb, c - 1, NJ)
                    need(y_in, c - 2)
                    for i in range(CH):
                        for j in range(NJ):
                            last = nc.tensor.matmul(py[:, i * P:(i + 1) * P], hT[:, j, i * P:(i + 1) * P],
                                                    w["w2"][:, j, :], start=(j == 0), stop=(j == NJ - 1))
                    last.then_inc(y_ps, 1)

            lagged(pe, NC, 2, 1, 1, step)

        @block.scalar
        def _(act):
            need = counter(act)

            def step(c, p):
                if has(c, NC):
                    need(momented, c)
                    nc.scalar.activation(sd[:, 0, :], mv[:, 0, :, 1], ACT.Sqrt, bias=const["eps"][:, 0:1]).then_inc(rooted, 1)
                    need(x_ps, c)
                    need(h_ps, c - 2, NJ)
                    nc.scalar.copy(x1T[:, p, :], pa[:, :]).then_inc(x_T, 1)
                if has(c - 1, NC):
                    need(y_ps, c - 2)
                    for j in range(NJ):
                        need(h_ps, c - 1, NJ, j - NJ + 1)
                        nc.scalar.activation(hT[:, j, :], ph[:, j, :], ACT.Relu, bias=w["b1"][:, j:j + 1]).then_inc(h_sb, 1)
                    need(momented2, c - 1)
                    nc.scalar.activation(sd[:, 1, :], mv[:, 1, :, 1], ACT.Sqrt, bias=const["eps"][:, 0:1]).then_inc(rooted2, 1)

            lagged(act, NC, 2, 1, 1, step)

        @block.vector
        def _(dve):
            need = counter(dve)

            def step(c, p):
                if has(c, NC):
                    moments(nc, dve, st[:, 0], mv[:, 0], R[:, ds(c * CH, CH), :]).then_inc(momented, 1)
                    need(rooted, c)
                    need(gained, c - 1)
                    normalise(nc, dve, xn, R[:, ds(c * CH, CH), :], mv[:, 0], sd[:, 0], rs[:, 0]).then_inc(n_sb, 1)
                if has(c - 1, NC):
                    need(y_ps, c - 1)
                    nc.vector.tensor_tensor(out=r2[:, :, :], in0=fm(py[:, :]), in1=x1[:, 1 - p, :, :],
                                            op=ALU.add).then_inc(y_in, 1)
                    dve.drain()
                    nc.vector.tensor_tensor(out=r2[:, :, :], in0=r2[:, :, :], in1=wide(w["b2"][:, :]), op=ALU.add)
                    dve.drain()
                    moments(nc, dve, st[:, 1], mv[:, 1], r2).then_inc(momented2, 1)
                    need(rooted2, c - 1)
                    need(gained2, c - 2)
                    normalise(nc, dve, yn, r2, mv[:, 1], sd[:, 1], rs[:, 1]).then_inc(n2_sb, 1)
                    dve.drain()

            lagged(dve, NC, 2, 1, 1, step)

        @block.gpsimd
        def _(pool):
            need = counter(pool)

            def step(c, p):
                if has(c, NC):
                    need(n_sb, c)
                    need(y_in, c - 2)
                    nc.gpsimd.tensor_tensor(out=x1[:, p, :, :], in0=xn[:, :, :], in1=wide(w["g1"][:, :]),
                                            op=ALU.mult).then_inc(gained, 1)
                    pool.drain()
                    nc.gpsimd.tensor_tensor(out=x1[:, p, :, :], in0=x1[:, p, :, :], in1=wide(w["o1"][:, :]),
                                            op=ALU.add).then_inc(x1_sb, 1)
                if has(c - 1, NC):
                    need(n2_sb, c - 1)
                    r4 = R[:, ds((c - 1) * CH, CH), :]
                    nc.gpsimd.tensor_tensor(out=r4, in0=yn[:, :, :], in1=wide(w["g2"][:, :]),
                                            op=ALU.mult).then_inc(gained2, 1)
                    pool.drain()
                    nc.gpsimd.tensor_tensor(out=r4, in0=r4, in1=wide(w["o2"][:, :]), op=ALU.add)
                    pool.drain()

            lagged(pool, NC, 2, 1, 1, step)


def split_qkv_pass(nc, R, Vc, scratch, w, const):
    with ExitStack() as ctx:
        k = Kit(nc, ctx, "sp_")
        st, mv = k.sb("st", [P, CH, 6]), k.sb("mv", [P, CH, 2])
        sd, rs = k.sb("sd", [P, CH]), k.sb("rs", [P, CH])
        xn = k.sb("xn", [P, CH, D])
        xnT = k.sb("xnT", [P, CW])
        rest = k.sb("rest", [P, 2, CW])
        parts = k.sb("parts", [P, 2, 2, NPART, CW], BF16)
        pa = k.ps("pa", [P, CW])
        pqk = k.ps("pqk", [P, 2, CW])
        pv = k.ps("pv", [P, CW])
        momented, rooted, n_sb, n_ps, n_T = (k.sem(n) for n in ("momented", "rooted", "n_sb", "n_ps", "n_T"))
        qk_ps, high, split = k.sem("qk_ps"), k.sem("high"), k.sem("split")
        v_ps, v_sb, ones = k.sem("v_ps"), k.sem("v_sb"), k.sem("ones")
        written = [k.sem(f"written{p}") for p in range(2)]
        NW = 2 * NPART * NG0 * 16
        block = ctx.enter_context(nc.Block())
        CPB = NC // BATCH

        @block.tensor
        def _(pe):
            need = counter(pe)

            def step(c, p):
                need(n_sb, c)
                need(n_T, c - 1)
                for i in range(CH):
                    last = nc.tensor.transpose(pa[:, i * P:(i + 1) * P], xn[:, i, :], const["ident"][:, :])
                last.then_inc(n_ps, 1)
                need(n_T, c)
                need(split, c - 1)
                for i in range(2):
                    last = nc.tensor.matmul(pqk[:, i, :], w["qkv"][:, i * D:(i + 1) * D], xnT[:, :],
                                            start=True, stop=True)
                last.then_inc(qk_ps, 1)
                need(v_sb, c - 1)
                for i in range(CH):
                    last = nc.tensor.matmul(pv[:, i * P:(i + 1) * P], xnT[:, i * P:(i + 1) * P],
                                            w["qkv"][:, 2 * D:3 * D], start=True, stop=True)
                last.then_inc(v_ps, 1)

            for c in range(2):
                step(c, c)
            with pe.Fori(1, NC // 2) as r:
                for p in range(2):
                    step(r * 2 + p, p)

        @block.scalar
        def _(act):
            need = counter(act)
            act.wait_ge(ones, 1)

            def step(c, p, b, cb, before):
                need(momented, c)
                nc.scalar.activation(sd[:, :], mv[:, :, 1], ACT.Sqrt, bias=const["eps"][:, 0:1]).then_inc(rooted, 1)
                need(n_ps, c)
                need(v_ps, c - 1)
                nc.scalar.copy(xnT[:, :], pa[:, :]).then_inc(n_T, 1)
                need(qk_ps, c)
                need(written[p], before - 1, NW)
                nc.scalar.copy(parts[:, p, :, 0, :], pqk[:, :, :]).then_inc(high, 1)
                need(v_ps, c)
                for i in range(CH):
                    dst = Vc[:, ds(b * NG0, NG0), ds(cb * CH + i, 1), :, 0:HD0].rearrange("p g a j d -> p g (a j) d")
                    last = nc.scalar.copy(dst, pv[:, i * P:(i + 1) * P].rearrange("p (g j d) -> p g j d", g=NG0, j=HPG))
                last.then_inc(v_sb, 1)

            for c in range(2):
                step(c, c, 0, c, 0)
            for b in range(BATCH):
                first = 1 if b == 0 else 0
                with act.Fori(first, CPB // 2) as r:
                    for p in range(2):
                        step(r * 2 + (p + b * CPB), p, b, r * 2 + p, r + b * CPB // 2)

        @block.vector
        def _(dve):
            need = counter(dve)
            nc.vector.memset(Vc[:, :, :, :, :], 1.0).then_inc(ones, 1)

            def step(c, p):
                src = R[:, ds(c * CH, CH), :]
                moments(nc, dve, st, mv, src).then_inc(momented, 1)
                need(rooted, c)
                need(n_ps, c - 1)
                normalise(nc, dve, xn, src, mv, sd, rs).then_inc(n_sb, 1)
                need(high, c)
                nc.vector.tensor_tensor(out=rest[:, :, :], in0=pqk[:, :, :], in1=parts[:, p, :, 0, :], op=ALU.subtract)
                dve.drain()
                nc.vector.tensor_copy(parts[:, p, :, 1, :], rest[:, :, :])
                dve.drain()
                nc.vector.tensor_tensor(out=rest[:, :, :], in0=rest[:, :, :], in1=parts[:, p, :, 1, :], op=ALU.subtract)
                dve.drain()
                nc.vector.tensor_copy(parts[:, p, :, 2, :], rest[:, :, :]).then_inc(split, 1)
                dve.drain()

            for c in range(2):
                step(c, c)
            with dve.Fori(1, NC // 2) as r:
                for p in range(2):
                    step(r * 2 + p, p)

        @block.sync
        def _(sp):
            need = counter(sp)
            for b in range(BATCH):
                with sp.Fori(0, CPB // 2) as r:
                    for p in range(2):
                        cb = r * 2 + p
                        need(split, cb + b * CPB)
                        for i in range(2):
                            for a in range(NPART):
                                for g in range(NG0):
                                    sp.dma_start(
                                        scratch[b * NG0 + g, i, a, :, ds(cb * CW, CW)],
                                        parts[32 * g:32 * g + 32, p, i, a, :]).then_inc(written[p], 16)
            for p in range(2):
                sp.wait_ge(written[p], NC // 2 * NW)


def full_attention_pass(nc, Vc, AO, scratch, const):
    KT = NTB
    NQ = SEQ // QC
    NQT = QC // P
    NKB = SEQ // 512
    NGRP = BATCH * NG0
    with ExitStack() as ctx:
        k = Kit(nc, ctx, "fa_")
        qst = k.sb("qst", [P, 2, HPG, SEQ], BF16)
        kst = k.sb("kst", [P, 2, HPG, SEQ], BF16)
        vst = k.sb("vst", [P, 2, KT, HPG, 32])
        pe_ = k.sb("pexp", [P, 2, HPG, QC])
        mxb = k.sb("mxb", [P, HPG, NQT, NKB])
        mx = k.sb("mx", [P, NQT, HPG])
        mr = k.sb("mr", [P, NQT, HPG])
        mpart = k.sb("mpart", [P, NQT, HPG, NPART], BF16)
        oS = k.sb("oS", [P, QC])
        rs = k.sb("rs", [P, NQT * HPG])
        pM = k.ps("pM", [P, 2, 512])
        pS = k.ps("pS", [P, 4, 512])
        pO = k.ps("pO", [P, 512])
        pX = k.ps("pX", [P, 512])
        NDMA = 2 * NPART * NPART * HPG
        stacks = [k.sem(f"stacks{p}") for p in range(2)]
        v_in = k.sem("v_in")
        group_done = k.sem("group_done")
        cleared = k.sem("cleared")
        max_ps = k.sem("max_ps")
        max_sb = k.sem("max_sb")
        m_split = k.sem("m_split")
        m_ps = k.sem("m_ps")
        m_row = k.sem("m_row")
        s_ps = k.sem("s_ps")
        e_sb = k.sem("e_sb")
        pv_done = k.sem("pv_done")
        o_sb = k.sem("o_sb")
        o_tp = k.sem("o_tp")
        o_out = k.sem("o_out")
        block = ctx.enter_context(nc.Block())
        K3 = MROW + NPART

        def rounds(eng, emit):
            with eng.Fori(0, NGRP // 2) as r:
                for par in range(2):
                    gi = r * 2 + par
                    with eng.Fori(0, NQ - 1) as qc:
                        emit(gi, par, qc, gi * NQ + qc, False)
                    emit(gi, par, NQ - 1, gi * NQ + (NQ - 1), True)

        @block.sync
        def _(sp):
            need = counter(sp)

            def load(gi, par):
                for j in range(HPG):
                    for a in range(NPART):
                        for b in range(NPART):
                            row = (a * NPART + b) * HD0
                            for i, part, to in ((0, a, qst), (1, b, kst)):
                                src = scratch[ds(gi, 1), i, part, j * HD0:(j + 1) * HD0, :]
                                sp.dma_start(to[row:row + HD0, par, j, :],
                                             src.rearrange("g d t -> (g d) t")).then_inc(stacks[par], 16)

            sp.wait_ge(cleared, 1)
            load(0, 0)
            load(1, 1)
            with sp.Fori(1, NGRP // 2) as r:
                for par in range(2):
                    sp.wait_ge(group_done, r * 2 + (par - 1))
                    load(r * 2 + par, par)

        @block.gpsimd
        def _(pool):
            def take(gi, par):
                src = Vc[:, ds(gi, 1), :, :, :].rearrange("p g t j d -> p (g t) j d")
                nc.gpsimd.tensor_copy(vst[:, par, :, :, 0:HD0 + 1], src).then_inc(v_in, 1)
            nc.gpsimd.memset(vst[:, :, :, :, :], 0.0)
            pool.drain()
            take(0, 0)
            take(1, 1)
            with pool.Fori(1, NGRP // 2) as r:
                for par in range(2):
                    pool.wait_ge(group_done, r * 2 + (par - 1))
                    take(r * 2 + par, par)

        def n_max(n, s):
            return (n * KT + s) * NKB

        @block.tensor
        def _(pe):
            def max_scores(par, qc, n, s):
                j, qt = s // NQT, s % NQT
                for kb in range(NKB):
                    m = n_max(n, s) + kb
                    if not isinstance(m, int) or m >= 2:
                        pe.wait_ge(max_sb, m - 1)
                    nc.tensor.matmul(pM[:, kb % 2, :], qst[0:KST, par, j, ds(qc * QC + qt * P, P)],
                                     kst[0:KST, par, j, kb * 512:(kb + 1) * 512],
                                     start=True, stop=True).then_inc(max_ps, 1)

            def max_rows(n, first):
                pe.wait_ge(m_split, n + 1)
                if not first:
                    pe.wait_ge(o_out, n)
                for qt in range(NQT):
                    if not first or qt:
                        pe.wait_ge(m_row, n * NQT + qt)
                    for j in range(HPG):
                        last = nc.tensor.matmul(pX[MROW:MROW + NPART, j * P:(j + 1) * P], mpart[:, qt, j, :],
                                                const["identb"][:, :], start=True, stop=True)
                    last.then_inc(m_ps, 1)

            def scores(gi, par, qc, n, kt):
                for hp in range(2):
                    if kt == 0 and hp == 0:
                        pe.wait_ge(v_in, gi + 1)
                        pe.wait_ge(m_row, (n + 1) * NQT)
                    if kt:
                        pe.wait_ge(e_sb, (n * KT + kt) * 2 + (hp - 1))
                    for j in (2 * hp, 2 * hp + 1):
                        last = nc.tensor.matmul(pS[:, j, :], kst[0:K3, par, j, kt * P:(kt + 1) * P],
                                                qst[0:K3, par, j, ds(qc * QC, QC)], start=True, stop=True)
                    last.then_inc(s_ps, 1)

            def times_v(par, n, kt):
                pe.wait_ge(e_sb, (n * KT + kt + 1) * 2)
                for j in range(HPG):
                    last = nc.tensor.matmul(pO[32 * j:32 * j + 32, :], vst[:, par, kt, j, :], pe_[:, kt % 2, j, :],
                                            start=(kt == 0), stop=(kt == KT - 1))
                last.then_inc(pv_done, 1)

            def emit(r, par, qc, n, last_q, lead=True):
                if last_q and lead:
                    pe.wait_ge(stacks[1 - par], (r + (1 + par)) * (16 * NDMA))
                for kt in range(KT):
                    scores(r * 2 + par, par, qc, n, kt)
                    if lead:
                        if last_q:
                            max_scores(1 - par, 0, n + 1, kt)
                        else:
                            max_scores(par, qc + 1, n + 1, kt)
                    if kt:
                        times_v(par, n, kt - 1)
                times_v(par, n, KT - 1)
                if lead:
                    max_rows(n + 1, False)
                pe.wait_ge(o_sb, n + 1)
                if not lead:
                    pe.wait_ge(o_out, n + 1)
                pe.wait_ge(m_row, (n + 2) * NQT if lead else (n + 1) * NQT)
                for qt in range(NQT):
                    t = nc.tensor.transpose(pX[:, qt * P:(qt + 1) * P], oS[:, qt * P:(qt + 1) * P], const["ident"][:, :])
                t.then_inc(o_tp, 1)

            pe.wait_ge(stacks[0], 16 * NDMA)
            for s in range(KT):
                max_scores(0, 0, 0, s)
            max_rows(0, True)

            def group(r, par, lead):
                gi = r * 2 + par
                with pe.Fori(0, NQ - 1) as qc:
                    emit(r, par, qc, qc + gi * NQ, False)
                emit(r, par, NQ - 1, gi * NQ + (NQ - 1), True, lead)

            with pe.Fori(0, NGRP // 2 - 1) as r:
                group(r, 0, True)
                group(r, 1, True)
            group(NGRP // 2 - 1, 0, True)
            group(NGRP // 2 - 1, 1, False)

        @block.scalar
        def _(act):
            def emit(gi, par, qc, n, last_q):
                for kt in range(KT):
                    for hp in range(2):
                        act.wait_ge(s_ps, (n * KT + kt) * 2 + hp + 1)
                        if kt >= 2:
                            act.wait_ge(pv_done, n * KT + (kt - 1))
                        nc.scalar.activation(pe_[:, kt % 2, 2 * hp:2 * hp + 2, :], pS[:, 2 * hp:2 * hp + 2, :],
                                             ACT.Exp, scale=float(HD0) ** -0.5).then_inc(e_sb, 1)
                act.wait_ge(pv_done, (n + 1) * KT)
                nc.scalar.copy(oS[:, :], pO[:, :]).then_inc(o_sb, 1)

            rounds(act, emit)

        @block.vector
        def _(dve):
            nc.vector.memset(kst[:, :, :, :], 0.0)
            nc.vector.memset(qst[:, :, :, :], 0.0)
            dve.drain()
            nc.vector.memset(kst[MROW:MROW + NPART, :, :, :], -1.0).then_inc(cleared, 1)
            dve.drain()

            def maxima(n):
                for s in range(KT):
                    j, qt = s // NQT, s % NQT
                    for kb in range(NKB):
                        dve.wait_ge(max_ps, n_max(n, s) + kb + 1)
                        nc.vector.tensor_reduce(mxb[:, j, qt, kb:kb + 1], pM[:, kb % 2, :], AX.X, ALU.max).then_inc(max_sb, 1)

            def split(par, qc, n):
                dve.drain()
                nc.vector.tensor_reduce(mx[:, :, :].rearrange("p q j -> p j q"), mxb[:, :, :, :], AX.X, ALU.max)
                dve.drain()
                nc.vector.tensor_copy(mpart[:, :, :, 0], mx[:, :, :])
                dve.drain()
                nc.vector.tensor_tensor(out=mr[:, :, :], in0=mx[:, :, :], in1=mpart[:, :, :, 0], op=ALU.subtract)
                dve.drain()
                nc.vector.tensor_copy(mpart[:, :, :, 1], mr[:, :, :])
                dve.drain()
                nc.vector.tensor_tensor(out=mr[:, :, :], in0=mr[:, :, :], in1=mpart[:, :, :, 1], op=ALU.subtract)
                dve.drain()
                nc.vector.tensor_copy(mpart[:, :, :, 2], mr[:, :, :]).then_inc(m_split, 1)
                for qt in range(NQT):
                    dve.wait_ge(m_ps, n * NQT + qt + 1)
                    nc.vector.tensor_copy(qst[MROW:MROW + NPART, par, :, ds(qc * QC + qt * P, P)],
                                          pX[MROW:MROW + NPART, :].rearrange("p (j q) -> p j q", j=HPG)).then_inc(m_row, 1)

            def output(gi, qc, n):
                dve.wait_ge(o_tp, n + 1)
                o = pX[:, :].rearrange("p (a d) -> p a d", d=32)
                nc.vector.reciprocal(rs[:, :].unsqueeze(2), o[:, :, HD0:HD0 + 1])
                dve.drain()
                nc.vector.tensor_tensor(
                    out=AO[:, ds(gi * NQ + qc, 1), :, :].rearrange("p g a d -> p (g a) d"),
                    in0=o[:, :, 0:HD0], in1=bcast(rs[:, :], HD0), op=ALU.mult).then_inc(o_out, 1)

            def emit(gi, par, qc, n, last_q, lead=True):
                if lead:
                    maxima(n + 1)
                    if last_q:
                        split(1 - par, 0, n + 1)
                    else:
                        split(par, qc + 1, n + 1)
                output(gi, qc, n)
                if last_q:
                    dve.drain()
                    nc.vector.memset(mr[:, 0, 0:1], 0.0).then_inc(group_done, 1)

            nc.vector.memset(mx[:, :, :], 0.0).then_inc(o_out, 1)
            maxima(0)
            split(0, 0, 0)
            with dve.Fori(0, NGRP // 2 - 1) as r:
                for par in range(2):
                    gi = r * 2 + par
                    with dve.Fori(0, NQ - 1) as qc:
                        emit(gi, par, qc, gi * NQ + qc, False)
                    emit(gi, par, NQ - 1, gi * NQ + (NQ - 1), True)
            for par in range(2):
                gi = NGRP - 2 + par
                with dve.Fori(0, NQ - 1) as qc:
                    emit(gi, par, qc, qc + gi * NQ, False)
                emit(gi, par, NQ - 1, gi * NQ + (NQ - 1), True, lead=(par == 0))


def head_output_pass(nc, AO, R, w, const):
    NQ, NQT = SEQ // QC, QC // P
    with ExitStack() as ctx:
        k = Kit(nc, ctx, "ho_")
        at = k.sb("at", [P, 2, CH, D])
        aT = k.sb("aT", [P, CW])
        pa, py = k.ps("pa", [P, CW]), k.ps("py", [P, CW])
        a_in, a_ps, a_T, y_ps, y_in = (k.sem(n) for n in ("a_in", "a_ps", "a_T", "y_ps", "y_in"))
        block = ctx.enter_context(nc.Block())

        @block.tensor
        def _(pe):
            need = counter(pe)
            for c in range(NC):
                need(a_in, c)
                need(a_T, c - 1)
                for i in range(CH):
                    last = nc.tensor.transpose(pa[:, i * P:(i + 1) * P], at[:, c % 2, i, :], const["ident"][:, :])
                last.then_inc(a_ps, 1)
                need(a_T, c)
                need(y_in, c - 1)
                for i in range(CH):
                    last = nc.tensor.matmul(py[:, i * P:(i + 1) * P], aT[:, i * P:(i + 1) * P], w["proj"][:, :],
                                            start=True, stop=True)
                last.then_inc(y_ps, 1)

        @block.scalar
        def _(act):
            need = counter(act)
            for c in range(NC):
                b, qc = c // NQ, c % NQ
                need(a_ps, c - 2)
                for g in range(NG0):
                    src = AO[:, (b * NG0 + g) * NQ + qc, :, :].rearrange("p (t j) d -> p t (j d)", j=HPG)
                    last = nc.scalar.copy(at[:, c % 2, :, 32 * g:32 * g + 32], src)
                last.then_inc(a_in, 1)
                need(a_ps, c)
                need(y_ps, c - 1)
                nc.scalar.copy(aT[:, :], pa[:, :]).then_inc(a_T, 1)

        @block.vector
        def _(dve):
            need = counter(dve)
            for c in range(NC):
                r4 = R[:, c * CH:(c + 1) * CH, :]
                nc.vector.tensor_tensor(out=r4, in0=r4, in1=w["bias"][:, :].unsqueeze(1).broadcast_to([P, CH, D]), op=ALU.add)
                need(y_ps, c)
                dve.drain()
                nc.vector.tensor_tensor(out=r4, in0=r4, in1=py[:, :].rearrange("p (a n) -> p a n", n=D),
                                        op=ALU.add).then_inc(y_in, 1)
                dve.drain()


def fp4_levels(nc, dve, x, xabs, nb, b, halved, absed):
    ab, lev, up = b["ab"][:, 0:nb, :], b["lev"][:, 0:nb, :], b["up"][:, 0:nb, :]
    bm, sc, rc, hs = (b[n][:, 0:nb] for n in ("bm", "sc", "rc", "hs"))
    nc.vector.tensor_reduce(bm, x, AX.X, ALU.max, apply_absolute_value=True)
    dve.drain()
    nc.vector.tensor_scalar(sc, bm, 1.0 / 6.0, 1e-12, ALU.mult, ALU.max)
    dve.drain()
    nc.vector.tensor_scalar(hs, sc, 0.5, None, ALU.mult).then_inc(halved, 1)
    nc.vector.reciprocal(rc, sc)
    dve.drain()
    absed()
    nc.vector.tensor_tensor(out=ab, in0=xabs, in1=bcast(rc, FB), op=ALU.mult)
    dve.drain()
    nc.vector.tensor_scalar(lev, ab, 5.0, 2.0, ALU.is_gt, ALU.mult)
    nc.vector.tensor_scalar(up, ab, 1.75, None, ALU.is_gt)
    for mid in (3.5, 2.5):
        dve.drain()
        nc.vector.scalar_tensor_tensor(out=lev, in0=ab, scalar=mid, in1=lev, op0=ALU.is_gt, op1=ALU.add)
    dve.drain()
    nc.vector.scalar_tensor_tensor(out=lev, in0=lev, scalar=2.0, in1=up, op0=ALU.mult, op1=ALU.add)
    for mid in (1.25, 0.75, 0.25):
        dve.drain()
        nc.vector.scalar_tensor_tensor(out=lev, in0=ab, scalar=mid, in1=lev, op0=ALU.is_gt, op1=ALU.add)
    dve.drain()


def fp4_pass(nc, R, w_gate, w_up, w_down, const):
    NBX, NBH = D // FB, F0 // FB
    FCH = [P, P, F0 - 2 * P]
    NWB = 2 * 3 * NBX + NBH
    with ExitStack() as ctx:
        k = Kit(nc, ctx, "fp_")
        ws = k.sb("ws", [P, NWB, FB])
        wg, wu = k.sb("wg", [P, F0]), k.sb("wu", [P, F0])
        wd = k.sb("wd", [P, 3, D])
        buf = {"ab": k.sb("ab", [P, CH * NBH, FB]), "lev": k.sb("lev", [P, CH * NBH, FB]),
               "up": k.sb("up", [P, CH * NBH, FB])}
        for n in ("bm", "sc", "rc", "hs"):
            buf[n] = k.sb(n, [P, CH * NBH])
        sg = k.sb("sg", [P, CH * NBH, FB])
        ax = k.sb("ax", [P, CH * NBH, FB])
        st, mv = k.sb("st", [P, CH, 6]), k.sb("mv", [P, CH, 2])
        sd, rs = k.sb("sd", [P, CH]), k.sb("rs", [P, CH])
        xn = k.sb("xn", [P, CH, D])
        xq = k.sb("xq", [P, CH, D])
        xqT = k.sb("xqT", [P, 2, CW])
        gs = k.sb("gs", [P, 2, F0])
        h = k.sb("h", [P, CH, F0])
        hq = k.sb("hq", [P, CH, F0])
        hqT = k.sb("hqT", [P, 2, 3, P])
        pa = k.ps("pa", [P, CW])
        pg, pu = k.ps("pg", [P, 2, 512]), k.ps("pu", [P, 2, 512])
        pt = k.ps("pt", [P, 2, 512])
        py = k.ps("py", [P, CW])
        w_in, w_zero = k.sem("w_in"), k.sem("w_zero")
        halved, signs, signed = k.sem("halved"), k.sem("signs"), k.sem("signed")
        rounded, absed = k.sem("rounded"), k.sem("absed")
        w_ps, w_sb = k.sem("w_ps"), k.sem("w_sb")
        wctx = ExitStack()
        blockw = wctx.enter_context(nc.Block())

        @blockw.sync
        def _(sp):
            sp.wait_ge(w_zero, 1)
            n = 0
            for o, src in ((0, w_gate), (3 * NBX, w_up)):
                for j, m in enumerate(FCH):
                    sp.dma_start(ws[0:m, o + j * NBX:o + (j + 1) * NBX, :].rearrange("p a b -> p (a b)"),
                                 src[j * P:j * P + m, :]).then_inc(w_in, 16)
            sp.dma_start(ws[:, 6 * NBX:, :].rearrange("p a b -> p (a b)"), w_down).then_inc(w_in, 16)

        @blockw.scalar
        def _(act):
            act.wait_ge(w_in, 16 * 7)
            nc.scalar.activation(ax[:, 0:NWB, :], ws[:, :, :], ACT.Abs).then_inc(absed, 1)
            nc.scalar.activation(sg[:, 0:NWB, :], ws[:, :, :], ACT.Sign).then_inc(signs, 1)
            for n in range(9):
                act.wait_ge(w_ps, n + 1)
                kind, j = n // 3, n % 3
                if kind < 2:
                    dst = (wg, wu)[kind][:, j * P:j * P + FCH[j]]
                    src = pt[:, n % 2, 0:FCH[j]]
                else:
                    dst = wd[0:FCH[j], j, :]
                    src = pt[0:FCH[j], n % 2, 0:D]
                nc.scalar.copy(dst, src).then_inc(w_sb, 1)

        @blockw.gpsimd
        def _(pool):
            pool.wait_ge(signs, 1)
            pool.wait_ge(halved, 1)
            nc.gpsimd.tensor_tensor(out=sg[:, 0:NWB, :], in0=sg[:, 0:NWB, :], in1=bcast(buf["hs"][:, 0:NWB], FB),
                                    op=ALU.mult).then_inc(signed, 1)

        @blockw.vector
        def _(dve):
            nc.vector.memset(ws[:, :, :], 0.0).then_inc(w_zero, 1)
            dve.wait_ge(w_in, 16 * 7)
            fp4_levels(nc, dve, ws[:, :, :], ax[:, 0:NWB, :], NWB, buf, halved, lambda: dve.wait_ge(absed, 1))
            dve.wait_ge(signed, 1)
            nc.vector.tensor_tensor(out=ws[:, :, :], in0=buf["lev"][:, 0:NWB, :], in1=sg[:, 0:NWB, :],
                                    op=ALU.mult).then_inc(rounded, 1)

        @blockw.tensor
        def _(pe):
            pe.wait_ge(rounded, 1)
            for n in range(9):
                if n >= 2:
                    pe.wait_ge(w_sb, n - 1)
                kind, j = n // 3, n % 3
                m = FCH[j]
                if kind < 2:
                    src = ws[0:m, (kind * 3 + j) * NBX:(kind * 3 + j + 1) * NBX, :].rearrange("p a b -> p (a b)")
                    nc.tensor.transpose(pt[:, n % 2, 0:m], src, const["ident"][0:m, 0:m]).then_inc(w_ps, 1)
                else:
                    o = 6 * NBX + j * NBX
                    src = ws[:, o:o + m // FB, :].rearrange("p a b -> p (a b)")
                    nc.tensor.transpose(pt[0:m, n % 2, 0:D], src, const["ident"][:, :]).then_inc(w_ps, 1)

        wctx.close()
        sgx = k.sb("sgx", [P, CH * NBX, FB])
        axx = k.sb("axx", [P, CH * NBX, FB])
        n_in = k.sem("n_in")
        absed_x, absed_h = k.sem("absed_x"), k.sem("absed_h")
        momented, rooted = k.sem("momented"), k.sem("rooted")
        halved_x, signs_x, signed_x, xq_sb = (k.sem(n) for n in ("halved_x", "signs_x", "signed_x", "xq_sb"))
        halved_h, signs_h, signed_h, hq_sb = (k.sem(n) for n in ("halved_h", "signs_h", "signed_h", "hq_sb"))
        x_ps, x_T = k.sem("x_ps"), k.sem("x_T")
        g_ps, u_ps, g_sb, h_sb = k.sem("g_ps"), k.sem("u_ps"), k.sem("g_sb"), k.sem("h_sb")
        t_ps, t_sb, y_ps, y_in = k.sem("t_ps"), k.sem("t_sb"), k.sem("y_ps"), k.sem("y_in")
        block = ctx.enter_context(nc.Block())

        def blocks(ap):
            return ap.rearrange("p a (n b) -> p (a n) b", b=FB)

        @block.tensor
        def _(pe):
            need = counter(pe)

            def turn(c, i):
                need(t_sb, c, CH, i - 2 - CH + 1) if not isinstance(c, int) or c * CH + i >= 2 else None
                for j, m in enumerate(FCH):
                    last = nc.tensor.transpose(pt[0:m, i % 2, j * P:(j + 1) * P], hq[:, i, j * P:j * P + m],
                                               const["ident"][:, :])
                last.then_inc(t_ps, 1)

            def down(c, i):
                need(t_sb, c, CH, i - CH + 1)
                if i == 0:
                    need(y_in, c - 1)
                for j, m in enumerate(FCH):
                    last = nc.tensor.matmul(py[:, i * P:(i + 1) * P], hqT[0:m, i % 2, j, :], wd[0:m, j, :],
                                            start=(j == 0), stop=(j == 2))
                last.then_inc(y_ps, 1)

            def step(c, p):
                if has(c - 2, NC):
                    need(hq_sb, c - 2)
                    turn(c - 2, 0)
                    for i in range(1, CH):
                        turn(c - 2, i)
                        down(c - 2, i - 1)
                    down(c - 2, CH - 1)
                if has(c - 1, NC):
                    need(x_T, c - 1)
                    for i in range(CH):
                        skip = isinstance(c, int) and (c - 1) * CH + i < 2
                        if not skip:
                            need(g_sb, c - 1, CH, i - 2 - CH + 1)
                        nc.tensor.matmul(pg[:, i % 2, 0:F0], xqT[:, 1 - p, i * P:(i + 1) * P], wg[:, :],
                                         start=True, stop=True).then_inc(g_ps, 1)
                        if not skip:
                            need(h_sb, c - 1, CH, i - 2 - CH + 1)
                        nc.tensor.matmul(pu[:, i % 2, 0:F0], xqT[:, 1 - p, i * P:(i + 1) * P], wu[:, :],
                                         start=True, stop=True).then_inc(u_ps, 1)
                if has(c, NC):
                    need(xq_sb, c)
                    need(x_T, c - 1)
                    for i in range(CH):
                        last = nc.tensor.transpose(pa[:, i * P:(i + 1) * P], xq[:, i, :], const["ident"][:, :])
                    last.then_inc(x_ps, 1)

            lagged(pe, NC, 2, 2, 0, step, peel=4)

        @block.scalar
        def _(act):
            need = counter(act)

            def step(c, p):
                if has(c - 2, NC):
                    for i in range(CH):
                        need(t_ps, c - 2, CH, i - CH + 1)
                        if not (isinstance(c, int) and (c - 2) * CH + i < 2):
                            need(y_ps, c - 2, CH, i - 2 - CH + 1)
                        nc.scalar.copy(hqT[:, i % 2, 0:2, :], pt[:, i % 2, 0:2 * P].rearrange("p (j n) -> p j n", n=P))
                        nc.scalar.copy(hqT[0:FCH[2], i % 2, 2, :], pt[0:FCH[2], i % 2, 2 * P:3 * P]).then_inc(t_sb, 1)
                if has(c, NC):
                    need(momented, c)
                    nc.scalar.activation(sd[:, :], mv[:, :, 1], ACT.Sqrt, bias=const["eps"][:, 0:1]).then_inc(rooted, 1)
                    need(n_in, c)
                    need(xq_sb, c - 1)
                    nc.scalar.activation(axx[:, :, :], blocks(xn[:, :, :]), ACT.Abs).then_inc(absed_x, 1)
                    nc.scalar.activation(sgx[:, :, :], blocks(xn[:, :, :]), ACT.Sign).then_inc(signs_x, 1)
                if has(c - 1, NC):
                    for i in range(CH):
                        need(g_ps, c - 1, CH, i - CH + 1)
                        if not (isinstance(c, int) and (c - 1) * CH + i < 2):
                            need(h_sb, c - 1, CH, i - 2 - CH + 1)
                        nc.scalar.activation(gs[:, i % 2, :], pg[:, i % 2, 0:F0], ACT.Silu).then_inc(g_sb, 1)
                    need(h_sb, c - 1, CH)
                    need(hq_sb, c - 2)
                    nc.scalar.activation(ax[:, :, :], blocks(h[:, :, :]), ACT.Abs).then_inc(absed_h, 1)
                    nc.scalar.activation(sg[:, :, :], blocks(h[:, :, :]), ACT.Sign).then_inc(signs_h, 1)
                if has(c, NC):
                    need(x_ps, c)
                    nc.scalar.copy(xqT[:, p, :], pa[:, :]).then_inc(x_T, 1)

            lagged(act, NC, 2, 2, 0, step, peel=4)

        @block.gpsimd
        def _(pool):
            need = counter(pool)

            def step(c, p):
                for sign, hv, out, t, d, nb in ((signs_x, halved_x, signed_x, sgx, c, CH * NBX),
                                                (signs_h, halved_h, signed_h, sg, c - 1, CH * NBH)):
                    if has(d, NC):
                        need(sign, d)
                        need(hv, d)
                        nc.gpsimd.tensor_tensor(out=t[:, :, :], in0=t[:, :, :], in1=bcast(buf["hs"][:, 0:nb], FB),
                                                op=ALU.mult).then_inc(out, 1)

            lagged(pool, NC, 2, 2, 0, step, peel=4)

        @block.vector
        def _(dve):
            need = counter(dve)

            def step(c, p):
                if has(c, NC):
                    src = R[:, ds(c * CH, CH), :]
                    moments(nc, dve, st, mv, src).then_inc(momented, 1)
                    need(rooted, c)
                    need(signs_x, c - 1)
                    normalise(nc, dve, xn, src, mv, sd, rs).then_inc(n_in, 1)
                    dve.drain()
                    fp4_levels(nc, dve, blocks(xn[:, :, :]), axx[:, :, :], CH * NBX, buf, halved_x,
                               lambda: need(absed_x, c))
                    need(signed_x, c)
                    need(x_ps, c - 1)
                    nc.vector.tensor_tensor(out=blocks(xq[:, :, :]), in0=buf["lev"][:, 0:CH * NBX, :],
                                            in1=sgx[:, :, :], op=ALU.mult).then_inc(xq_sb, 1)
                if has(c - 1, NC):
                    need(signs_h, c - 2)
                    for i in range(CH):
                        need(g_sb, c - 1, CH, i - CH + 1)
                        need(u_ps, c - 1, CH, i - CH + 1)
                        nc.vector.tensor_tensor(out=h[:, i, :], in0=gs[:, i % 2, :], in1=pu[:, i % 2, 0:F0],
                                                op=ALU.mult).then_inc(h_sb, 1)
                    dve.drain()
                    fp4_levels(nc, dve, blocks(h[:, :, :]), ax[:, :, :], CH * NBH, buf, halved_h,
                               lambda: need(absed_h, c - 1))
                    need(signed_h, c - 1)
                    need(t_ps, c - 2, CH)
                    nc.vector.tensor_tensor(out=blocks(hq[:, :, :]), in0=buf["lev"][:, :, :],
                                            in1=sg[:, :, :], op=ALU.mult).then_inc(hq_sb, 1)
                    dve.drain()
                if has(c - 2, NC):
                    need(y_ps, c - 2, CH)
                    r4 = R[:, ds((c - 2) * CH, CH), :]
                    nc.vector.tensor_tensor(out=r4, in0=r4, in1=py[:, :].rearrange("p (a n) -> p a n", n=D),
                                            op=ALU.add).then_inc(y_in, 1)

            lagged(dve, NC, 2, 2, 0, step, peel=4)


def row(a, n=P):
    return a.unsqueeze(0).broadcast_to([P, n])


def global_attention_stage(nc, X, a, scratch, const):
    with ExitStack() as ctx:
        k = Kit(nc, ctx, "A_")
        w = {"qkv": k.sb("qkv", [P, 3 * D]), "proj": k.sb("proj", [P, D]), "bias": k.sb("bias", [P, D])}
        AO = k.sb("AO", [P, NT, H0, HD0])
        Vc = k.sb("Vc", [P, BATCH * NG0, NTB, HPG, HD0 + 1])
        move_pass(nc, "A_w_", [(w["qkv"][:, :], a["L0_attn_w_qkv"]), (w["proj"][:, :], a["L0_attn_w_proj"]),
                               (w["bias"][:, :], row(a["L0_attn_b_proj"]))])
        split_qkv_pass(nc, X, Vc, scratch, w, const)
        full_attention_pass(nc, Vc, AO, scratch, const)
        head_output_pass(nc, AO, X, w, const)


def window_stage(nc, E, a, scratch, const):
    perm = scratch.rearrange("(b m t j) f -> b j m t f", b=BATCH, m=64, t=NTB, j=2)
    plain = scratch.rearrange("(t p) f -> p t f", p=P)
    permuted = [(E[64 * j:64 * j + 64, b * NTB:(b + 1) * NTB, :], perm[b, j]) for b in range(BATCH) for j in range(2)]
    for pre, ff, kind, own in (("la", "lf", "w32", W32), ("sa", "pf", "w64", 64)):
        A, B = "L1_attn_" + pre, "L1_attn_" + ff
        with ExitStack() as ctx:
            k = Kit(nc, ctx, "C_" + pre)
            w = {"wqk": k.sb("wqk", [P, 2 * INNER]), "wv": k.sb("wv", [P, INNER]), "wo": k.sb("wo", [P, HP, D]),
                 "own": k.sb("own", [P, own]), "pb": k.sb("pb", [P, D])}
            f = {"w1": k.sb("w1", [P, F1]), "w2": k.sb("w2", [P, F1 // P, D]), "b1": k.sb("b1", [P, F1 // P])}
            for n in ("g1", "o1", "b2", "g2", "o2"):
                f[n] = k.sb(n, [P, D])

            def per_head(ap):
                return ap.rearrange("p (h k) -> p h k", k=HD)

            move_pass(nc, "C_w_" + pre, [
                (per_head(w["wqk"][:, 0:INNER]), a[A + "_wqs"].rearrange("h d k -> d h k")),
                (per_head(w["wqk"][:, INNER:]), a[A + "_wks"].rearrange("h d k -> d h k")),
                (per_head(w["wv"][:, :]), a[A + "_wvs"].rearrange("h d k -> d h k")),
                (w["wo"][:, :, :], a[A + "_pw"].rearrange("(c p) n -> p c n", p=P)),
                (w["own"][:, :], a["c_own%d" % own]), (w["pb"][:, :], row(a[A + "_pb"]))]
                + (permuted if kind == "w64" else []))
            attention_pass(nc, "C_a_" + pre, kind, E, w, const, prefetch=[
                (f["w1"][:, :], a[B + "_w1"]),
                (f["w2"][:, :, :], a[B + "_w2"].rearrange("(c p) n -> p c n", p=P)),
                (f["g1"][:, :], row(a[A + "_g"])), (f["o1"][:, :], row(a[A + "_b"])),
                (f["b2"][:, :], row(a[B + "_b2"])), (f["g2"][:, :], row(a[B + "_g"])),
                (f["o2"][:, :], row(a[B + "_b"]))] + [
                (f["b1"][:, j:j + 1], a[B + "_b1"][P * j:P * j + P].unsqueeze(1)) for j in range(F1 // P)])
            relu_pass(nc, "C_f_" + pre, E, f, const)
            if kind == "w32":
                move_pass(nc, "C_s_", [(plain, E[:, :, :])])
            else:
                move_pass(nc, "C_t_", [(src, to) for to, src in permuted])
                move_pass(nc, "C_u_", [(E[:, :, :], plain)])


def rotary_stage(nc, Y, a, const):
    with ExitStack() as ctx:
        k = Kit(nc, ctx, "D_")
        w = {"wqk": k.sb("wqk", [P, 2 * INNER]), "wv": k.sb("wv", [P, INNER]), "wo": k.sb("wo", [P, HP, D]),
             "mask": k.sb("mask", [P, NT, 64], BF16), "kfac": k.sb("kfac", [P, 1]), "inner": k.sb("inner", [P, NT]),
             "rot": k.sb("rot", [P, NT, 4 * HD]), "qk_scale": k.sb("qk_scale", [P, 4 * HD])}
        f = {"w1": k.sb("w1", [P, 2 * F2]), "w2": k.sb("w2", [P, NJ2, D]), "b1a": k.sb("b1a", [P, NJ2]),
             "b1g": k.sb("b1g", [P, NJ2]), "g": k.sb("g", [P, 1]), "b": k.sb("b", [P, 1]), "inner": w["inner"]}

        def layer_of(name, l):
            return a["L1_ffn_" + name][ds(l, 1)]

        def attention_weights(l):
            wqkv = layer_of("Wqkv", l).rearrange("l k n -> (l k) n")
            return [(w["wqk"][:, :], wqkv[:, 0:2 * INNER]), (w["wv"][:, :], wqkv[:, 2 * INNER:]),
                    (w["wo"][:, :, :], layer_of("Wo", l).rearrange("l (c p) n -> p (l c) n", p=P))] + [
                    (w["qk_scale"][:, HD * i:HD * i + HD],
                     layer_of("q_scale" if i < 2 else "k_scale", l).broadcast_to([P, HD])) for i in range(4)]

        def feed_weights(l):
            w2 = layer_of("W2", l)
            moves = [(f["w1"][:, :], layer_of("W1", l).rearrange("l k n -> (l k) n")),
                     (f["w2"][:, 0:2, :], w2[:, 0:2 * P, :].rearrange("l (c p) n -> p (l c) n", p=P)),
                     (f["w2"][0:JW2[2], 2, :], w2[:, 2 * P:F2, :].rearrange("l k n -> (l k) n")),
                     (f["w2"][ONE_ROW:ONE_ROW + 1, 2, :], layer_of("b2", l)),
                     (f["g"][:, :], layer_of("ln_g", l).rearrange("l p -> p l")),
                     (f["b"][:, :], layer_of("ln_b", l).rearrange("l p -> p l"))]
            b1 = layer_of("b1", l)
            for j, m in enumerate(JW2):
                for o, t in ((0, "b1a"), (F2, "b1g")):
                    moves.append((f[t][0:m, j:j + 1], b1[:, o + P * j:o + P * j + m].rearrange("l p -> p l")))
            return moves

        with nc.Block() as block:
            @block.vector
            def _(dve):
                nc.vector.memset(f["w2"][64:P, NJ2 - 1, :], 0.0)
        move_pass(nc, "D_w_", attention_weights(0) + [
            (w["mask"][:, :, :], a["c_mask"]), (w["kfac"][:, :], a["c_kfac"]),
            (w["inner"][:, :], a["c_inner"]), (w["rot"][:, :, :], a["c_rot"])])
        with nc.Fori(0, DEPTH - 1) as l:
            attention_pass(nc, "D_a_", "local", Y, w, const, prefetch=feed_weights(l))
            gated_pass(nc, "D_f_", Y, f, const, prefetch=attention_weights(l + 1))
        attention_pass(nc, "D_b_", "local", Y, w, const, prefetch=feed_weights(DEPTH - 1))
        gated_pass(nc, "D_g_", Y, f, const)


def preln_program(nc, a, out):
    parts = nc.dram_tensor("qk_parts", (BATCH * NG0, 2, NPART, HPG * HD0, SEQ), BF16).ap()
    order = nc.dram_tensor("reorder", (TOK, D), F32).ap()
    with ExitStack() as ctx:
        k = Kit(nc, ctx, "")
        X = k.sb("X", [P, NT, D])
        const = {"ident": k.sb("ident", [P, P]), "identb": k.sb("identb", [P, P], BF16), "eps": k.sb("eps", [P, 1]),
                 "ident_d": a["c_ident"], "identb_d": a["c_identb"]}
        load_pass(nc, const, X, a["L0_attn_x"])
        global_attention_stage(nc, X, a, parts, const)
        fp4_pass(nc, X, a["L0_ffn_w_gate"], a["L0_ffn_w_up"], a["L0_ffn_w_down"], const)
        Y = k.sb("Y", [P, NT, D])
        add_norm_pass(nc, "n1_", X, Y, False)
        window_stage(nc, Y, a, order, const)
        add_norm_pass(nc, "n2_", X, Y, True)
        rotary_stage(nc, Y, a, const)
        add_pass(nc, X, Y)
        store_pass(nc, X, out)


def host_tables():
    bf16 = mybir.dt.np(BF16)
    f32 = np.float32
    p = np.arange(P)
    half = np.arange(0, HD, 2, dtype=f32)
    inv_freq = (f32(1.0) / f32(10000.0) ** (half / f32(HD))).astype(f32)
    freqs = np.arange(SEQ, dtype=f32)[:, None] * inv_freq[None, :]
    base = (half.astype(np.float64) + 0.4 * HD) / (1.4 * HD)
    scale = base[None, :] ** ((p[:, None] - P // 2) / 16.0)
    cos = np.cos(freqs.astype(np.float64)).reshape(NTB, P, 32)
    sin = np.sin(freqs.astype(np.float64)).reshape(NTB, P, 32)
    rot = np.zeros((P, NT, 256))
    for t in range(NT):
        c, s = cos[t % NTB], sin[t % NTB]
        for o, m in ((0, scale), (128, 1.0 / scale)):
            rot[:, t, o:o + 128] = np.concatenate([c * m, c * m, s * m, -s * m], axis=1)
    mask = np.zeros((P, NT, 2 * W32))
    i, j = (p % W32)[:, None], (np.arange(2 * W32) - W32)[None, :]
    mask[:] = np.where((i < j) | (i > j + W32), -1e30, 0.0)[:, None, :]
    mask[:W32, ::NTB, :W32] = -1e30
    inner = np.ones((P, NT))
    inner[:, ::NTB] = 0.0
    own = (p[:, None] % 64 == np.arange(64)[None, :])
    own32 = (p[:, None] % 32 == np.arange(32)[None, :])
    return {
        "c_ident": np.eye(P, dtype=f32),
        "c_identb": np.eye(P).astype(bf16),
        "c_rot": rot.astype(f32),
        "c_mask": mask.astype(bf16),
        "c_kfac": np.tile(base ** (P / 16.0), 4).astype(f32)[:, None],
        "c_inner": inner.astype(f32),
        "c_own64": own.astype(f32),
        "c_own32": own32.astype(f32),
    }


def kernel(**inputs):
    import concourse.bacc as bacc
    from concourse.bass_utils import run_bass_kernel_spmd

    nc = bacc.Bacc("TRN2", target_bir_lowering=False, num_devices=1)
    arrays = {n: np.ascontiguousarray(v) for n, v in inputs.items()}
    arrays.update(host_tables())
    a = {n: nc.dram_tensor(n, v.shape, mybir.dt.from_np(v.dtype), kind="ExternalInput").ap()
         for n, v in arrays.items()}
    out = nc.dram_tensor("out", (BATCH, SEQ, D), F32, kind="ExternalOutput").ap()
    preln_program(nc, a, out)
    result = run_bass_kernel_spmd(nc, [arrays], core_ids=[0])
    return result.results[0]["out"]
```

```python
from contextlib import ExitStack

import concourse.bass as bass
from concourse import mybir
from concourse.alu_op_type import AluOpType as ALU
import numpy as np

F32 = mybir.dt.float32
BF16 = mybir.dt.bfloat16
ACT = mybir.ActivationFunctionType
AX = mybir.AxisListType
ds = bass.ds

P = 128
D = 128
BATCH, SEQ = 2, 2048
TOK = BATCH * SEQ
NT = TOK // P
NTB = SEQ // P
CH = 4
NC = NT // CH
CW = CH * P
EPS = 1e-5
W32 = 32

H0, HD0 = 16, 8
NPART = 3
KST = NPART * NPART * HD0
MROW = 96
HPG = 4
NG0 = H0 // HPG
QC = 512

H, HD = 16, 64
INNER = H * HD
HP = H // 2
DEPTH = 6
F0 = 352
FB = 16
F1 = 512
F2 = 341
NJ2 = 3
JW2 = [128, 128, F2 - 256]
ONE_ROW = 96


def upto(i, per=1, extra=0):
    n = (i + 1) * per + extra
    return max(n, 0) if isinstance(i, int) else n


def lagged(eng, n, unroll, lag, ahead, emit, peel=0):
    head = max(lag + (-lag) % unroll, peel)
    rounds = (n - head - ahead) // unroll
    for t in range(head):
        emit(t, t % unroll)
    if rounds > 0:
        with eng.Fori(0, rounds) as r:
            for p in range(unroll):
                emit(r * unroll + (head + p), p)
    for t in range(head + rounds * unroll, n + lag):
        emit(t, t % unroll)


def has(t, n):
    return not isinstance(t, int) or 0 <= t < n


class Kit:
    def __init__(self, nc, ctx, tag):
        self.nc, self.ctx, self.tag = nc, ctx, tag
        self.sems = []
        ctx.callback(self.clear)

    def sb(self, name, shape, dt=F32):
        return self.ctx.enter_context(self.nc.sbuf_tensor(self.tag + name, shape, dt))

    def ps(self, name, shape, dt=F32):
        return self.ctx.enter_context(self.nc.psum_tensor(self.tag + name, shape, dt))

    def sem(self, name):
        self.sems.append(self.nc.alloc_semaphore(name=self.tag + name))
        return self.sems[-1]

    def clear(self):
        if self.sems:
            self.nc.clear_and_free_semaphores(self.sems)
            self.nc.all_engine_barrier()


def bcast(ap, n):
    return ap.unsqueeze(2).broadcast_to([ap.shape[0], ap.shape[1], n])


def fetch(sp, moves, arrived):
    if not moves:
        return
    for to, src in moves:
        sp.dma_start(to, src).then_inc(arrived, 16)
    sp.wait_ge(arrived, 16 * len(moves))


def move_pass(nc, tag, moves):
    with ExitStack() as ctx:
        k = Kit(nc, ctx, tag)
        moved = k.sem("moved")
        block = ctx.enter_context(nc.Block())

        @block.sync
        def _(sp):
            fetch(sp, moves, moved)


def add_norm_pass(nc, tag, X, Y, add):
    with ExitStack() as ctx:
        k = Kit(nc, ctx, tag)
        st, mv = k.sb("st", [P, NT, 6]), k.sb("mv", [P, NT, 2])
        sd, rs = k.sb("sd", [P, NT]), k.sb("rs", [P, NT])
        eps = k.sb("eps", [P, 1])
        momented, rooted = k.sem("momented"), k.sem("rooted")
        block = ctx.enter_context(nc.Block())

        @block.scalar
        def _(act):
            act.wait_ge(momented, 1)
            nc.scalar.activation(sd[:, :], mv[:, :, 1], ACT.Sqrt, bias=eps[:, 0:1]).then_inc(rooted, 1)

        @block.vector
        def _(dve):
            nc.vector.memset(eps[:, :], EPS)
            if add:
                with dve.Fori(0, NC) as c:
                    x4 = X[:, ds(c * CH, CH), :]
                    nc.vector.tensor_tensor(out=x4, in0=x4, in1=Y[:, ds(c * CH, CH), :], op=ALU.add)
                dve.drain()
            with dve.Fori(0, NC) as c:
                for i in range(CH):
                    nc.vector.bn_stats(st[:, ds(c * CH + i, 1), :].rearrange("p a s -> p (a s)"),
                                       X[:, ds(c * CH + i, 1), :].rearrange("p a f -> p (a f)"))
            dve.drain()
            for t in range(NT):
                nc.vector.bn_aggr(mv[:, t, :], st[:, t, :])
            dve.drain().then_inc(momented, 1)
            dve.wait_ge(rooted, 1)
            nc.vector.reciprocal(rs[:, :], sd[:, :])
            dve.drain()
            with dve.Fori(0, NC) as c:
                for i in range(CH):
                    t = c * CH + i
                    nc.vector.tensor_scalar(Y[:, ds(t, 1), :].rearrange("p a f -> p (a f)"),
                                            X[:, ds(t, 1), :].rearrange("p a f -> p (a f)"),
                                            mv[:, ds(t, 1), 0:1].rearrange("p a s -> p (a s)"), rs[:, ds(t, 1)],
                                            ALU.subtract, ALU.mult)


def add_pass(nc, X, Y):
    with nc.Block() as block:

        @block.vector
        def _(dve):
            with dve.Fori(0, NC) as c:
                x4 = X[:, ds(c * CH, CH), :]
                nc.vector.tensor_tensor(out=x4, in0=x4, in1=Y[:, ds(c * CH, CH), :], op=ALU.add)


def load_pass(nc, const, X, x):
    with ExitStack() as ctx:
        k = Kit(nc, ctx, "ld_")
        loaded = k.sem("loaded")
        block = ctx.enter_context(nc.Block())

        @block.sync
        def _(sp):
            sp.dma_start(X[:, :, :], x.rearrange("b (t p) f -> p (b t) f", p=P)).then_inc(loaded, 16)
            sp.dma_start(const["ident"][:, :], const["ident_d"]).then_inc(loaded, 16)
            sp.dma_start(const["identb"][:, :], const["identb_d"]).then_inc(loaded, 16)
            sp.wait_ge(loaded, 48)

        @block.vector
        def _(dve):
            nc.vector.memset(const["eps"][:, :], EPS)


def store_pass(nc, X, out):
    with ExitStack() as ctx:
        k = Kit(nc, ctx, "st_")
        stored = k.sem("stored")
        block = ctx.enter_context(nc.Block())

        @block.sync
        def _(sp):
            sp.dma_start(out.rearrange("b (t p) f -> p (b t) f", p=P), X[:, :, :]).then_inc(stored, 16)
            sp.wait_ge(stored, 16)


def attention_pass(nc, tag, kind, R, w, const, prefetch=()):
    local = kind == "local"
    W = 32 if kind == "w32" else 64
    SCALE = 8.0 if local else 1.0 / 8.0
    with ExitStack() as ctx:
        k = Kit(nc, ctx, tag)
        xt = k.sb("xt", [P, 2, D])
        xs = k.sb("xs", [P, 2, P])
        carry = k.sb("carry", [P, 2])
        qT = k.sb("qT", [P, HP, P])
        kT = k.sb("kT", [P, 2, HP, W32 + P])
        v = k.sb("v", [P, 4, INNER])
        z = k.sb("z", [P, H * W])
        pr = k.sb("pr", [P, H * W])
        pn = k.sb("pn", [P, H * W])
        pT = k.sb("pT", [P, H, W // 32, 32])
        band = k.sb("band", [P, H, P])
        edge = k.sb("edge", [P, H, W32]) if local else None
        oT = k.sb("oT", [P, HP, P])
        mx = k.sb("mx", [P, H])
        sm = k.sb("sm", [P, H])
        rs = k.sb("rs", [P, H])
        if local:
            sq = k.sb("sq", [P, 2, 512])
            ss = k.sb("ss", [P, 2 * H])
            nr = k.sb("nr", [P, 2 * H])
            rn = k.sb("rn", [P, 2 * H])
            qc = k.sb("qc", [P, 4, 512])
            qs = k.sb("qs", [P, 4, 512])
            qn = k.sb("qn", [P, 4, 512])
            rot = k.sb("rot", [P, 2, 256])

        pj = k.ps("pj", [P, 2, 512])
        pt = k.ps("pt", [P, 2, 512])
        pS = k.ps("pS", [P, 2, 512])
        pO = k.ps("pO", [P, 2, 512])

        x_in = k.sem("x_in")
        x_T = k.sem("x_T")
        x_s = k.sem("x_s")
        projected = k.sem("projected")
        squared = k.sem("squared")
        rotated = k.sem("rotated")
        added = k.sem("added")
        clamped = k.sem("clamped")
        rooted = k.sem("rooted")
        normed = k.sem("normed")
        rot_ready = k.sem("rot_ready")
        t_ps = k.sem("t_ps")
        t_sb = k.sem("t_sb")
        k_next = k.sem("k_next")
        scored = k.sem("scored")
        shifted = k.sem("shifted")
        exped = k.sem("exped")
        scaled = k.sem("scaled")
        p_T = k.sem("p_T")
        banded = k.sem("banded")
        v_ps = k.sem("v_ps")
        v_sb = k.sem("v_sb")
        o_ps = k.sem("o_ps")
        o_sb = k.sem("o_sb")
        y_ps = k.sem("y_ps")
        y_sb = k.sem("y_sb")
        zeroed = k.sem("zeroed")
        fetched = k.sem("fetched")
        block = ctx.enter_context(nc.Block())

        @block.sync
        def _(sp):
            fetch(sp, prefetch, fetched)

        def heads(ap):
            return ap.rearrange("p (r h w) -> p (r h) w", r=2, w=W)

        S4 = pS[:, :, 0:HP * W].rearrange("p r (h w) -> p r h w", w=W)
        if W == 64:
            S3 = pS[:, :, :].rearrange("p r (h w) -> p (r h) w", w=W)

        @block.tensor
        def _(pe):
            pe.wait_ge(zeroed, upto(0))

            def x_transpose(t, p):
                pe.wait_ge(x_in, upto(t))
                if isinstance(t, int) and t == 1:
                    pe.wait_ge(x_s, upto(0))
                pe.wait_ge(t_sb, upto(t - 2, 4, -1))
                nc.tensor.transpose(pt[:, 0, 0:P], xt[:, p % 2, :], const["ident"][:, :]).then_inc(x_T, 1)

            def qk_chunk(t, p, c):
                if c == 0:
                    pe.wait_ge(x_s, upto(t))
                before = (t, c - 2) if c >= 2 else (t - 1, c + 2)
                pe.wait_ge(squared, upto(before[0], 4, before[1] - 3))
                pe.wait_ge(rotated, upto(before[0], 4, before[1] - 3))
                nc.tensor.matmul(pj[:, c % 2, :], xs[:, p % 2, :], w["wqk"][:, c * 512:(c + 1) * 512],
                                 start=True, stop=True).then_inc(projected, 1)

            def qk_features(t, p, c):
                if c == 0:
                    pe.wait_ge(x_s, upto(t + 1 if has(t + 1, NT) else t))
                if c == 1:
                    pe.wait_ge(y_sb, upto(t - 2))
                if c >= 2:
                    pe.wait_ge(t_sb, upto(t, 4, c - 5))
                if local:
                    pe.wait_ge(normed, upto(t, 4, c - 3))
                for i in range(4):
                    o = pt[:, c % 2, i * P:(i + 1) * P]
                    if local:
                        last = nc.tensor.transpose(o, qn[:, c, i * P:(i + 1) * P], const["ident"][:, :])
                    else:
                        col = (c * 4 + i) * P
                        last = nc.tensor.matmul(o, w["wqk"][:, col:col + P], xs[:, p % 2, :],
                                                start=True, stop=True)
                last.then_inc(t_ps, 1)

            def scores(t, p, r):
                if r == 0:
                    pe.wait_ge(t_sb, upto(t, 4))
                    if local:
                        pe.wait_ge(k_next, upto(t - 1))
                    pe.wait_ge(shifted, upto(t - 1))
                    if not local:
                        nc.tensor.matmul(pS[:, 0, 0:2], const["identb"][:, :], const["identb"][:, 0:2],
                                         start=True, stop=True, skip_group_check=True)
                if local:
                    nc.tensor.matmul(pS[:, r, :], const["identb"][:, :],
                                     w["mask"][:, ds(t, 1), :].broadcast_to([P, HP, 64]),
                                     start=True, stop=False, skip_group_check=True)
                for i in range(HP):
                    n = P // (32 if local else W)
                    m = P // n
                    for q in range(n):
                        lo = m * q if local else W32 + m * q
                        last = nc.tensor.matmul(
                            pS[m * q:m * (q + 1), r, i * W:(i + 1) * W],
                            qT[64 * r:64 * r + 64, i, m * q:m * (q + 1)],
                            kT[64 * r:64 * r + 64, p % 2, i, lo:lo + W],
                            start=not local, stop=True, skip_group_check=True)
                if r == 1:
                    last.then_inc(scored, 1)

            def attend(t, p):
                pe.wait_ge(banded, upto(t))
                pe.wait_ge(v_sb, upto(t + 1 if has(t + 1, NT) else t, 2))
                for i in range(HP):
                    for r in range(2):
                        o = pO[64 * r:64 * r + 64, i // 4, (i % 4) * P:(i % 4 + 1) * P]
                        h = r * HP + i
                        col = (2 * i + r) * HD
                        last = nc.tensor.matmul(o, v[:, p, col:col + HD], band[:, h, :],
                                                start=True, stop=not local)
                        if local:
                            last = nc.tensor.matmul(o[:, 0:W32], v[:, (p - 1) % 4, col:col + HD], edge[:, h, :],
                                                    start=False, stop=True)
                last.then_inc(o_ps, 1)

            def v_chunks(t, p):
                pe.wait_ge(x_s, upto(t))
                pe.wait_ge(o_sb, upto(t - 2))
                if isinstance(t, int) and t < 2:
                    pe.wait_ge(v_sb, upto(t - 1, 2))
                for c in range(2):
                    nc.tensor.matmul(pO[:, c, :], xs[:, p % 2, :], w["wv"][:, c * 512:(c + 1) * 512],
                                     start=True, stop=True).then_inc(v_ps, 1)

            def project(t):
                pe.wait_ge(o_sb, upto(t))
                if not has(t + 1, NT):
                    pe.wait_ge(y_sb, upto(t - 1))
                for i in range(HP):
                    last = nc.tensor.matmul(pt[:, 1, 0:D], oT[:, i, :], w["wo"][:, i, :],
                                            start=(i == 0), stop=(i == HP - 1))
                last.then_inc(y_ps, 1)

            def step(t, p):
                now, one, two = has(t, NT), has(t - 1, NT), has(t - 2, NT)
                if isinstance(t, int) and t == 0:
                    x_transpose(0, 0)
                    if local:
                        qk_chunk(0, 0, 0)
                        qk_chunk(0, 0, 1)
                if one:
                    for c in range(4):
                        qk_features(t - 1, p - 1, c)
                if local and now:
                    qk_chunk(t, p, 2)
                if has(t + 1, NT):
                    x_transpose(t + 1, p + 1)
                if one:
                    scores(t - 1, p - 1, 0)
                if local and now:
                    qk_chunk(t, p, 3)
                if one:
                    scores(t - 1, p - 1, 1)
                if two:
                    attend(t - 2, (p - 2) % 4)
                if local and has(t + 1, NT):
                    qk_chunk(t + 1, p + 1, 0)
                    qk_chunk(t + 1, p + 1, 1)
                if two:
                    project(t - 2)
                if now:
                    v_chunks(t, p)

            lagged(pe, NT, 4, 2, 2, step)

        @block.scalar
        def _(act):

            def x_copy(t, p):
                act.wait_ge(x_T, upto(t - 2))
                nc.scalar.copy(xt[:, p % 2, :], R[:, ds(t, 1), :].rearrange("p a f -> p (a f)")).then_inc(x_in, 1)

            def square(t, c):
                act.wait_ge(projected, upto(t, 4, c - 3))
                before = (t, c - 2) if c >= 2 else (t - 1, c + 2)
                act.wait_ge(rotated, upto(before[0], 4, before[1] - 3))
                nc.scalar.activation(sq[:, c % 2, :], pj[:, c % 2, :], ACT.Square).then_inc(squared, 1)

            def features(t, p, c):
                act.wait_ge(t_ps, upto(t, 4, c - 3))
                if c == 0:
                    act.wait_ge(scored, upto(t - 1))
                src = pt[:, c % 2, :].rearrange("p (a n) -> p a n", n=P)
                dst = (qT[:, 4 * c:4 * c + 4, :] if c < 2 else
                       kT[:, p % 2, 4 * (c - 2):4 * (c - 2) + 4, W32:])
                nc.scalar.copy(dst, src).then_inc(t_sb, 1)

            def v_copies(t, p):
                for c in range(2):
                    act.wait_ge(v_ps, upto(t, 2, c - 1))
                    nc.scalar.copy(v[:, p % 4, c * 512:(c + 1) * 512], pO[:, c, :]).then_inc(v_sb, 1)

            def make_band(t, half):
                if half == 0:
                    act.wait_ge(p_T, upto(t))
                    act.wait_ge(o_ps, upto(t - 1))
                if kind == "w64":
                    moves = [(64 * a + 32 * kb, 64 * a + 32 * qb, kb) for a in range(2)
                             for kb in range(2) for qb in range(2)]
                elif kind == "w32":
                    moves = [(32 * a, 32 * a, 0) for a in range(4)]
                else:
                    moves = [(32 * a, 32 * a, 1) for a in range(4)] + [(32 * a - 32, 32 * a, 0) for a in range(4)]
                for kp, qp, kb in moves[4 * half:4 * half + 4]:
                    dst = (band[kp:kp + 32, :, qp:qp + 32] if kp >= 0 else edge[96:128, :, :])
                    last = nc.scalar.copy(dst, pT[qp:qp + 32, :, kb, :])
                if moves[4 * half + 4:] == []:
                    last.then_inc(banded, 1)

            def step(t, p):
                now, one, two = has(t, NT), has(t - 1, NT), has(t - 2, NT)
                if isinstance(t, int) and t == 0:
                    x_copy(0, 0)
                    x_copy(1, 1)
                    if local:
                        square(0, 0)
                        square(0, 1)
                if one:
                    for c in range(4):
                        features(t - 1, p - 1, c)
                if not local and one:
                    v_copies(t - 1, p - 1)
                if local and two:
                    make_band(t - 2, 0)
                if local and now:
                    square(t, 2)
                if two and W == 64:
                    make_band(t - 2, 1)
                if local and now:
                    square(t, 3)
                if has(t + 2, NT):
                    x_copy(t + 2, p)
                if local and now:
                    act.wait_ge(clamped, upto(t))
                    nc.scalar.activation(nr[:, :], ss[:, :], ACT.Sqrt).then_inc(rooted, 1)
                if one:
                    act.wait_ge(shifted, upto(t - 1))
                    act.wait_ge(scaled, upto(t - 2))
                    nc.scalar.activation(pr[:, :], z[:, :], ACT.Exp, scale=SCALE).then_inc(exped, 1)
                if local and one:
                    act.wait_ge(t_sb, upto(t - 1, 4))
                    nc.scalar.activation(kT[:, p % 2, :, 0:W32], kT[:, (p - 1) % 2, :, P:P + W32], ACT.Copy,
                                         scale=w["kfac"][:, 0:1]).then_inc(k_next, 1)
                if two:
                    act.wait_ge(o_ps, upto(t - 2))
                    act.wait_ge(y_ps, upto(t - 3))
                    nc.scalar.copy(oT[:, :, :].rearrange("p h q -> p (h q)"),
                                   pO[:, :, :].rearrange("p a b -> p (a b)")).then_inc(o_sb, 1)
                if local and has(t + 1, NT):
                    square(t + 1, 0)
                    square(t + 1, 1)
                if local and now:
                    v_copies(t, p)
                if not local and one:
                    make_band(t - 1, 0)

            lagged(act, NT, 4, 2, 2, step)

        @block.vector
        def _(dve):
            nc.vector.memset(band[:, :, :], 0.0)
            if local:
                nc.vector.memset(edge[:, :, :], 0.0)
                nc.vector.memset(carry[:, :], 0.0)
                nc.vector.memset(kT[:, 0, :, 0:W32], 0.0)
                nc.vector.memset(v[:, 3, :], 0.0)
            dve.drain()
            nc.vector.memset(mx[:, :], 0.0).then_inc(zeroed, 1)

            def x_shift(t, p):
                p = p % 2
                dve.wait_ge(x_T, upto(t))
                if isinstance(t, int) and t < 2:
                    pass
                else:
                    dve.wait_ge(v_ps, upto(t - 2, 2))
                if not local:
                    nc.vector.tensor_copy(xs[:, p, :], pt[:, 0, 0:P]).then_inc(x_s, 1)
                    return
                nc.vector.tensor_tensor(out=xs[64:128, p, 0:1], in0=carry[64:128, 1 - p:2 - p],
                                        in1=w["inner"][64:128, ds(t, 1)], op=ALU.mult)
                nc.vector.tensor_copy(carry[64:128, p:p + 1], pt[64:128, 0, P - 1:P])
                nc.vector.tensor_copy(xs[0:64, p, :], pt[0:64, 0, 0:P])
                nc.vector.tensor_copy(xs[64:128, p, 1:P], pt[64:128, 0, 0:P - 1])
                dve.drain().then_inc(x_s, 1)

            def rotate(t, p, c):
                if c == 0:
                    dve.wait_ge(rot_ready, upto(t))
                dve.wait_ge(projected, upto(t, 4, c - 3))
                dve.wait_ge(squared, upto(t, 4, c - 3))
                dve.wait_ge(added, upto(t - 1, 4, c - 3))
                dve.wait_ge(normed, upto(t - 1, 4, c - 3))
                src = pj[:, c % 2, :].rearrange("p (h d) -> p h d", d=HD)
                tab = rot[:, p % 2, 128 * (c // 2):128 * (c // 2) + 128]
                for d, o in ((qc, 0), (qs, HD)):
                    nc.vector.tensor_tensor(
                        out=d[:, c, :].rearrange("p (h d) -> p h d", d=HD), in0=src,
                        in1=tab[:, o:o + HD].unsqueeze(1).broadcast_to([P, 8, HD]), op=ALU.mult)
                nc.vector.tensor_reduce(ss[:, 8 * c:8 * c + 8], sq[:, c % 2, :].rearrange("p (h d) -> p h d", d=HD),
                                        AX.X, ALU.add).then_inc(rotated, 1)

            def add_y(t):
                dve.wait_ge(y_ps, upto(t))
                r2 = R[:, ds(t, 1), :].rearrange("p a f -> p (a f)")
                if "pb" in w:
                    nc.vector.tensor_tensor(out=r2, in0=r2, in1=w["pb"][:, :], op=ALU.add)
                    dve.drain()
                nc.vector.tensor_tensor(out=r2, in0=r2, in1=pt[:, 1, 0:D], op=ALU.add).then_inc(y_sb, 1)

            def step(t, p):
                now, one, two = has(t, NT), has(t - 1, NT), has(t - 2, NT)
                if isinstance(t, int) and t == 0:
                    x_shift(0, 0)
                if local and now:
                    for c in range(4):
                        rotate(t, p, c)
                    dve.drain()
                    nc.vector.tensor_scalar(ss[:, :], ss[:, :], 1e-24, None, ALU.max).then_inc(clamped, 1)
                if one:
                    dve.wait_ge(scored, upto(t - 1))
                    if W == 64:
                        nc.vector.tensor_reduce(mx[:, :], S3, AX.X, ALU.max)
                    else:
                        nc.vector.tensor_reduce(mx[:, :].rearrange("p (r h) -> p r h", r=2), S4, AX.X, ALU.max)
                    dve.drain()
                    dve.wait_ge(exped, upto(t - 2))
                    if W == 64:
                        nc.vector.tensor_tensor(out=heads(z[:, :]), in0=S3, in1=bcast(mx[:, :], W),
                                                op=ALU.subtract).then_inc(shifted, 1)
                    else:
                        for r in range(2):
                            last = nc.vector.tensor_tensor(
                                out=z[:, r * HP * W:(r + 1) * HP * W].rearrange("p (h w) -> p h w", w=W),
                                in0=S4[:, r], in1=bcast(mx[:, r * HP:(r + 1) * HP], W), op=ALU.subtract)
                        last.then_inc(shifted, 1)
                if has(t + 1, NT):
                    x_shift(t + 1, p + 1)
                if local and now:
                    dve.wait_ge(rooted, upto(t))
                    nc.vector.reciprocal(rn[:, :], nr[:, :])
                    dve.drain()
                    dve.wait_ge(t_ps, upto(t - 1, 4))
                    for c in range(4):
                        dve.wait_ge(added, upto(t, 4, c - 3))
                        nc.vector.tensor_tensor(
                            out=qn[:, c, :].rearrange("p (h d) -> p h d", d=HD),
                            in0=qc[:, c, :].rearrange("p (h d) -> p h d", d=HD),
                            in1=bcast(rn[:, 8 * c:8 * c + 8], HD), op=ALU.mult).then_inc(normed, 1)
                if one:
                    dve.wait_ge(exped, upto(t - 1))
                    nc.vector.tensor_reduce(sm[:, :], heads(pr[:, :]), AX.X, ALU.add)
                    dve.drain()
                    nc.vector.reciprocal(rs[:, :], sm[:, :])
                    dve.drain()
                    nc.vector.tensor_tensor(out=heads(pn[:, :]), in0=heads(pr[:, :]), in1=bcast(rs[:, :], W),
                                            op=ALU.mult).then_inc(scaled, 1)
                    if local and two:
                        add_y(t - 2)
                    dve.drain()
                    if not local:
                        nc.vector.tensor_tensor(out=heads(pn[:, :]), in0=heads(pn[:, :]),
                                                in1=w["own"][:, 0:W].unsqueeze(1).broadcast_to([P, H, W]),
                                                op=ALU.subtract)
                        dve.drain()
                    dve.wait_ge(banded, upto(t - 2))
                    nc.vector.transpose(pT[:, :, :, :].rearrange("p h a b -> p (h a b)"), pn[:, :]).then_inc(p_T, 1)
                if two and not (local and one):
                    add_y(t - 2)

            lagged(dve, NT, 4, 2, 2, step)

        if local:
            @block.gpsimd
            def _(pool):

                def tables(t, p):
                    pool.wait_ge(rotated, upto(t - 2, 4))
                    nc.gpsimd.tensor_tensor(out=rot[:, p % 2, :], in0=w["rot"][:, ds(t, 1), :].rearrange("p a f -> p (a f)"),
                                            in1=w["qk_scale"][:, :], op=ALU.mult).then_inc(rot_ready, 1)

                def step(t, p):
                    if isinstance(t, int) and t == 0:
                        tables(0, 0)
                    if has(t + 1, NT):
                        tables(t + 1, p + 1)
                    if not has(t, NT):
                        return
                    for c in range(4):
                        pool.wait_ge(rotated, upto(t, 4, c - 3))
                        a = qc[:, c, :].rearrange("p (h e d) -> p h e d", e=2, d=32)
                        b = qs[:, c, :].rearrange("p (h e d) -> p h e d", e=2, d=32)
                        for e in range(2):
                            last = nc.gpsimd.tensor_tensor(out=a[:, :, e, :], in0=a[:, :, e, :],
                                                           in1=b[:, :, 1 - e, :], op=ALU.add)
                        last.then_inc(added, 1)

                lagged(pool, NT, 4, 2, 2, step)


def moments(nc, dve, st, mv, src):
    for i in range(CH):
        nc.vector.bn_stats(st[:, i, :], src[:, i, :])
    dve.drain()
    for i in range(CH):
        last = nc.vector.bn_aggr(mv[:, i, :], st[:, i, :])
    return last


def normalise(nc, dve, out, src, mv, sd, rs):
    nc.vector.reciprocal(rs[:, :], sd[:, :])
    dve.drain()
    for i in range(CH):
        last = nc.vector.tensor_scalar(out[:, i, :], src[:, i, :], mv[:, i, 0:1], rs[:, i:i + 1],
                                       ALU.subtract, ALU.mult)
    return last


def gated_pass(nc, tag, R, w, const, prefetch=()):
    with ExitStack() as ctx:
        k = Kit(nc, ctx, tag)
        xt = k.sb("xt", [P, 2, CH, D])
        xs = k.sb("xs", [P, CW])
        carry = k.sb("carry", [P, 2])
        st = k.sb("st", [P, CH, 6])
        mv = k.sb("mv", [P, CH, 2])
        sd = k.sb("sd", [P, CH])
        rs = k.sb("rs", [P, CH])
        xn = k.sb("xn", [P, CH, D])
        xnT = k.sb("xnT", [P, 2, CW])
        gl = k.sb("gl", [P, 2, CW])
        hT = k.sb("hT", [P, NJ2, CW])
        pa = k.ps("pa", [P, CW])
        pb = k.ps("pb", [P, CW])
        pg = k.ps("pg", [P, 2, CW])
        ph = k.ps("ph", [P, 2, CW])
        py = k.ps("py", [P, CW])
        x_in, x_T, x_s = k.sem("x_in"), k.sem("x_T"), k.sem("x_s")
        s_ps = k.sem("s_ps")
        momented, rooted = k.sem("momented"), k.sem("rooted")
        n_sb, n_ps, n_T = k.sem("n_sb"), k.sem("n_ps"), k.sem("n_T")
        gate_ps, gate_sb = k.sem("gate_ps"), k.sem("gate_sb")
        a_ps, h_sb = k.sem("a_ps"), k.sem("h_sb")
        y_ps, y_sb = k.sem("y_ps"), k.sem("y_sb")
        ready = k.sem("ready")
        fetched = k.sem("fetched")
        block = ctx.enter_context(nc.Block())

        @block.sync
        def _(sp):
            fetch(sp, prefetch, fetched)

        def fm(ap):
            return ap.rearrange("p (a n) -> p a n", n=P)

        @block.tensor
        def _(pe):
            pe.wait_ge(ready, 1)

            def hidden(c, p, j):
                m = JW2[j]
                pe.wait_ge(n_T, upto(c))
                pe.wait_ge(gate_sb, upto(c, NJ2, j - 2 - NJ2 + 1)) if not isinstance(c, int) or NJ2 * c + j >= 2 else None
                nc.tensor.matmul(pg[0:m, (NJ2 * p + j) % 2, :], w["w1"][:, F2 + 128 * j:F2 + 128 * j + m],
                                 xnT[:, p, :], start=True, stop=True).then_inc(gate_ps, 1)
                pe.wait_ge(h_sb, upto(c, NJ2, j - 2 - NJ2 + 1)) if not isinstance(c, int) or NJ2 * c + j >= 2 else None
                nc.tensor.matmul(ph[0:m, (NJ2 * p + j) % 2, :], w["w1"][:, 128 * j:128 * j + m],
                                 xnT[:, p, :], start=True, stop=True).then_inc(a_ps, 1)

            def step(c, p):
                now, one = has(c, NC), has(c - 1, NC)
                if now:
                    pe.wait_ge(x_in, upto(c))
                    pe.wait_ge(n_T, upto(c - 1))
                    for i in range(CH):
                        last = nc.tensor.transpose(pa[:, i * P:(i + 1) * P], xt[:, p, i, :], const["ident"][:, :])
                    last.then_inc(x_T, 1)
                if one:
                    hidden(c - 1, 1 - p, 0)
                if now:
                    pe.wait_ge(x_s, upto(c))
                    pe.wait_ge(n_sb, upto(c - 1))
                    for i in range(CH):
                        last = nc.tensor.transpose(pb[:, i * P:(i + 1) * P], xs[:, i * P:(i + 1) * P], const["ident"][:, :])
                    last.then_inc(s_ps, 1)
                if one:
                    hidden(c - 1, 1 - p, 1)
                    hidden(c - 1, 1 - p, 2)
                    pe.wait_ge(h_sb, upto(c - 1, NJ2))
                    pe.wait_ge(y_sb, upto(c - 2))
                    for i in range(CH):
                        for j in range(NJ2):
                            m = P if j < NJ2 - 1 else ONE_ROW + 1
                            last = nc.tensor.matmul(py[:, i * P:(i + 1) * P], hT[0:m, j, i * P:(i + 1) * P],
                                                    w["w2"][0:m, j, :], start=(j == 0), stop=(j == NJ2 - 1))
                    last.then_inc(y_ps, 1)
                if now:
                    pe.wait_ge(n_sb, upto(c))
                    for i in range(CH):
                        last = nc.tensor.transpose(pa[:, i * P:(i + 1) * P], xn[:, i, :], const["ident"][:, :])
                    last.then_inc(n_ps, 1)

            lagged(pe, NC, 2, 1, 1, step)

        @block.scalar
        def _(act):

            def x_copy(c, p):
                act.wait_ge(x_T, upto(c - 2))
                nc.scalar.copy(xt[:, p, :, :], R[:, ds(c * CH, CH), :]).then_inc(x_in, 1)

            def step(c, p):
                now, one = has(c, NC), has(c - 1, NC)
                if isinstance(c, int) and c == 0:
                    x_copy(0, 0)
                if has(c + 1, NC):
                    x_copy(c + 1, 1 - p)
                if one:
                    for j in range(NJ2):
                        m = JW2[j]
                        act.wait_ge(gate_ps, upto(c - 1, NJ2, j - NJ2 + 1))
                        if not isinstance(c, int) or NJ2 * (c - 1) + j >= 2:
                            act.wait_ge(h_sb, upto(c - 1, NJ2, j - 2 - NJ2 + 1))
                        nc.scalar.activation(gl[0:m, (NJ2 * (1 - p) + j) % 2, :], pg[0:m, (NJ2 * (1 - p) + j) % 2, :],
                                             ACT.Gelu, bias=w["b1g"][0:m, j:j + 1]).then_inc(gate_sb, 1)
                if now:
                    act.wait_ge(momented, upto(c))
                    nc.scalar.activation(sd[:, :], mv[:, :, 1], ACT.Sqrt, bias=const["eps"][:, 0:1]).then_inc(rooted, 1)
                    act.wait_ge(n_ps, upto(c))
                    act.wait_ge(a_ps, upto(c - 2, NJ2))
                    nc.scalar.activation(xnT[:, p, :], pa[:, :], ACT.Identity, scale=w["g"][:, 0:1],
                                         bias=w["b"][:, 0:1]).then_inc(n_T, 1)

            lagged(act, NC, 2, 1, 1, step)

        @block.vector
        def _(dve):
            nc.vector.memset(carry[:, :], 0.0)
            nc.vector.memset(hT[64:128, NJ2 - 1, :], 0.0)
            dve.drain()
            nc.vector.memset(hT[ONE_ROW:ONE_ROW + 1, NJ2 - 1, :], 1.0).then_inc(ready, 1)
            dve.drain()

            def step(c, p):
                now, one = has(c, NC), has(c - 1, NC)
                if now:
                    dve.wait_ge(x_T, upto(c))
                    dve.wait_ge(s_ps, upto(c - 1))
                    nc.vector.tensor_tensor(out=xs[64:128, 0:1], in0=carry[64:128, 1 - p:2 - p],
                                            in1=w["inner"][64:128, ds(c * CH, 1)], op=ALU.mult)
                    nc.vector.tensor_copy(carry[64:128, p:p + 1], pa[64:128, CW - 1:CW])
                    nc.vector.tensor_copy(xs[0:64, :], pa[0:64, :])
                    nc.vector.tensor_copy(xs[64:128, 1:CW], pa[64:128, 0:CW - 1])
                    dve.drain().then_inc(x_s, 1)
                    dve.wait_ge(s_ps, upto(c))
                    moments(nc, dve, st, mv, fm(pb[:, :])).then_inc(momented, 1)
                if one:
                    for j in range(NJ2):
                        m = JW2[j]
                        dve.wait_ge(gate_sb, upto(c - 1, NJ2, j - NJ2 + 1))
                        dve.wait_ge(a_ps, upto(c - 1, NJ2, j - NJ2 + 1))
                        dve.wait_ge(y_ps, upto(c - 2))
                        b = (NJ2 * (1 - p) + j) % 2
                        nc.vector.scalar_tensor_tensor(out=hT[0:m, j, :], in0=ph[0:m, b, :],
                                                       scalar=w["b1a"][0:m, j:j + 1], in1=gl[0:m, b, :],
                                                       op0=ALU.add, op1=ALU.mult).then_inc(h_sb, 1)
                if now:
                    dve.wait_ge(rooted, upto(c))
                    dve.wait_ge(n_ps, upto(c - 1))
                    normalise(nc, dve, xn, fm(pb[:, :]), mv, sd, rs).then_inc(n_sb, 1)
                if one:
                    dve.wait_ge(y_ps, upto(c - 1))
                    dve.wait_ge(x_T, upto(c - 1))
                    r4 = R[:, ds((c - 1) * CH, CH), :]
                    nc.vector.tensor_tensor(out=r4, in0=r4, in1=fm(py[:, :]), op=ALU.add).then_inc(y_sb, 1)

            lagged(dve, NC, 2, 1, 1, step)


def relu_pass(nc, tag, R, w, const):
    NJ = F1 // P
    with ExitStack() as ctx:
        k = Kit(nc, ctx, tag)
        st = k.sb("st", [P, 2, CH, 6])
        mv = k.sb("mv", [P, 2, CH, 2])
        sd = k.sb("sd", [P, 2, CH])
        rs = k.sb("rs", [P, 2, CH])
        xn = k.sb("xn", [P, CH, D])
        x1 = k.sb("x1", [P, 2, CH, D])
        x1T = k.sb("x1T", [P, 2, CW])
        hT = k.sb("hT", [P, NJ, CW])
        r2 = k.sb("r2", [P, CH, D])
        yn = k.sb("yn", [P, CH, D])
        pa = k.ps("pa", [P, CW])
        ph = k.ps("ph", [P, NJ, CW])
        py = k.ps("py", [P, CW])
        momented, rooted, n_sb = k.sem("momented"), k.sem("rooted"), k.sem("n_sb")
        gained, x1_sb, x_ps, x_T = k.sem("gained"), k.sem("x1_sb"), k.sem("x_ps"), k.sem("x_T")
        h_ps, h_sb, y_ps = k.sem("h_ps"), k.sem("h_sb"), k.sem("y_ps")
        y_in = k.sem("y_in")
        momented2, rooted2, n2_sb = k.sem("momented2"), k.sem("rooted2"), k.sem("n2_sb")
        gained2, done = k.sem("gained2"), k.sem("done")
        block = ctx.enter_context(nc.Block())

        def fm(ap):
            return ap.rearrange("p (a n) -> p a n", n=P)

        def wide(ap):
            return ap.unsqueeze(1).broadcast_to([P, CH, D])

        @block.tensor
        def _(pe):

            def step(c, p):
                if has(c, NC):
                    pe.wait_ge(x1_sb, upto(c))
                    pe.wait_ge(x_T, upto(c - 1))
                    for i in range(CH):
                        last = nc.tensor.transpose(pa[:, i * P:(i + 1) * P], x1[:, p, i, :], const["ident"][:, :])
                    last.then_inc(x_ps, 1)
                if has(c - 1, NC):
                    pe.wait_ge(x_T, upto(c - 1))
                    for j in range(NJ):
                        pe.wait_ge(h_sb, upto(c - 2, NJ, j - NJ + 1))
                        nc.tensor.matmul(ph[:, j, :], w["w1"][:, j * P:(j + 1) * P], x1T[:, 1 - p, :],
                                         start=True, stop=True).then_inc(h_ps, 1)
                    pe.wait_ge(h_sb, upto(c - 1, NJ))
                    pe.wait_ge(y_in, upto(c - 2))
                    for i in range(CH):
                        for j in range(NJ):
                            last = nc.tensor.matmul(py[:, i * P:(i + 1) * P], hT[:, j, i * P:(i + 1) * P],
                                                    w["w2"][:, j, :], start=(j == 0), stop=(j == NJ - 1))
                    last.then_inc(y_ps, 1)

            lagged(pe, NC, 2, 1, 1, step)

        @block.scalar
        def _(act):

            def step(c, p):
                if has(c, NC):
                    act.wait_ge(momented, upto(c))
                    nc.scalar.activation(sd[:, 0, :], mv[:, 0, :, 1], ACT.Sqrt, bias=const["eps"][:, 0:1]).then_inc(rooted, 1)
                    act.wait_ge(x_ps, upto(c))
                    act.wait_ge(h_ps, upto(c - 2, NJ))
                    nc.scalar.copy(x1T[:, p, :], pa[:, :]).then_inc(x_T, 1)
                if has(c - 1, NC):
                    act.wait_ge(y_ps, upto(c - 2))
                    for j in range(NJ):
                        act.wait_ge(h_ps, upto(c - 1, NJ, j - NJ + 1))
                        nc.scalar.activation(hT[:, j, :], ph[:, j, :], ACT.Relu, bias=w["b1"][:, j:j + 1]).then_inc(h_sb, 1)
                    act.wait_ge(momented2, upto(c - 1))
                    nc.scalar.activation(sd[:, 1, :], mv[:, 1, :, 1], ACT.Sqrt, bias=const["eps"][:, 0:1]).then_inc(rooted2, 1)

            lagged(act, NC, 2, 1, 1, step)

        @block.vector
        def _(dve):

            def step(c, p):
                if has(c, NC):
                    moments(nc, dve, st[:, 0], mv[:, 0], R[:, ds(c * CH, CH), :]).then_inc(momented, 1)
                    dve.wait_ge(rooted, upto(c))
                    dve.wait_ge(gained, upto(c - 1))
                    normalise(nc, dve, xn, R[:, ds(c * CH, CH), :], mv[:, 0], sd[:, 0], rs[:, 0]).then_inc(n_sb, 1)
                if has(c - 1, NC):
                    dve.wait_ge(y_ps, upto(c - 1))
                    nc.vector.tensor_tensor(out=r2[:, :, :], in0=fm(py[:, :]), in1=x1[:, 1 - p, :, :],
                                            op=ALU.add).then_inc(y_in, 1)
                    dve.drain()
                    nc.vector.tensor_tensor(out=r2[:, :, :], in0=r2[:, :, :], in1=wide(w["b2"][:, :]), op=ALU.add)
                    dve.drain()
                    moments(nc, dve, st[:, 1], mv[:, 1], r2).then_inc(momented2, 1)
                    dve.wait_ge(rooted2, upto(c - 1))
                    dve.wait_ge(gained2, upto(c - 2))
                    normalise(nc, dve, yn, r2, mv[:, 1], sd[:, 1], rs[:, 1]).then_inc(n2_sb, 1)
                    dve.drain()

            lagged(dve, NC, 2, 1, 1, step)

        @block.gpsimd
        def _(pool):

            def step(c, p):
                if has(c, NC):
                    pool.wait_ge(n_sb, upto(c))
                    pool.wait_ge(y_in, upto(c - 2))
                    nc.gpsimd.tensor_tensor(out=x1[:, p, :, :], in0=xn[:, :, :], in1=wide(w["g1"][:, :]),
                                            op=ALU.mult).then_inc(gained, 1)
                    pool.drain()
                    nc.gpsimd.tensor_tensor(out=x1[:, p, :, :], in0=x1[:, p, :, :], in1=wide(w["o1"][:, :]),
                                            op=ALU.add).then_inc(x1_sb, 1)
                if has(c - 1, NC):
                    pool.wait_ge(n2_sb, upto(c - 1))
                    r4 = R[:, ds((c - 1) * CH, CH), :]
                    nc.gpsimd.tensor_tensor(out=r4, in0=yn[:, :, :], in1=wide(w["g2"][:, :]),
                                            op=ALU.mult).then_inc(gained2, 1)
                    pool.drain()
                    nc.gpsimd.tensor_tensor(out=r4, in0=r4, in1=wide(w["o2"][:, :]), op=ALU.add)
                    pool.drain()

            lagged(pool, NC, 2, 1, 1, step)


def split_qkv_pass(nc, R, Vc, scratch, w, const):
    with ExitStack() as ctx:
        k = Kit(nc, ctx, "sp_")
        st, mv = k.sb("st", [P, CH, 6]), k.sb("mv", [P, CH, 2])
        sd, rs = k.sb("sd", [P, CH]), k.sb("rs", [P, CH])
        xn = k.sb("xn", [P, CH, D])
        xnT = k.sb("xnT", [P, CW])
        rest = k.sb("rest", [P, 2, CW])
        parts = k.sb("parts", [P, 2, 2, NPART, CW], BF16)
        pa = k.ps("pa", [P, CW])
        pqk = k.ps("pqk", [P, 2, CW])
        pv = k.ps("pv", [P, CW])
        momented, rooted, n_sb, n_ps, n_T = (k.sem(n) for n in ("momented", "rooted", "n_sb", "n_ps", "n_T"))
        qk_ps, high, split = k.sem("qk_ps"), k.sem("high"), k.sem("split")
        v_ps, v_sb, ones = k.sem("v_ps"), k.sem("v_sb"), k.sem("ones")
        written = [k.sem(f"written{p}") for p in range(2)]
        NW = 2 * NPART * NG0 * 16
        block = ctx.enter_context(nc.Block())
        CPB = NC // BATCH

        @block.tensor
        def _(pe):

            def step(c, p):
                pe.wait_ge(n_sb, upto(c))
                pe.wait_ge(n_T, upto(c - 1))
                for i in range(CH):
                    last = nc.tensor.transpose(pa[:, i * P:(i + 1) * P], xn[:, i, :], const["ident"][:, :])
                last.then_inc(n_ps, 1)
                pe.wait_ge(n_T, upto(c))
                pe.wait_ge(split, upto(c - 1))
                for i in range(2):
                    last = nc.tensor.matmul(pqk[:, i, :], w["qkv"][:, i * D:(i + 1) * D], xnT[:, :],
                                            start=True, stop=True)
                last.then_inc(qk_ps, 1)
                pe.wait_ge(v_sb, upto(c - 1))
                for i in range(CH):
                    last = nc.tensor.matmul(pv[:, i * P:(i + 1) * P], xnT[:, i * P:(i + 1) * P],
                                            w["qkv"][:, 2 * D:3 * D], start=True, stop=True)
                last.then_inc(v_ps, 1)

            for c in range(2):
                step(c, c)
            with pe.Fori(1, NC // 2) as r:
                for p in range(2):
                    step(r * 2 + p, p)

        @block.scalar
        def _(act):
            act.wait_ge(ones, 1)

            def step(c, p, b, cb, before):
                act.wait_ge(momented, upto(c))
                nc.scalar.activation(sd[:, :], mv[:, :, 1], ACT.Sqrt, bias=const["eps"][:, 0:1]).then_inc(rooted, 1)
                act.wait_ge(n_ps, upto(c))
                act.wait_ge(v_ps, upto(c - 1))
                nc.scalar.copy(xnT[:, :], pa[:, :]).then_inc(n_T, 1)
                act.wait_ge(qk_ps, upto(c))
                act.wait_ge(written[p], upto(before - 1, NW))
                nc.scalar.copy(parts[:, p, :, 0, :], pqk[:, :, :]).then_inc(high, 1)
                act.wait_ge(v_ps, upto(c))
                for i in range(CH):
                    dst = Vc[:, ds(b * NG0, NG0), ds(cb * CH + i, 1), :, 0:HD0].rearrange("p g a j d -> p g (a j) d")
                    last = nc.scalar.copy(dst, pv[:, i * P:(i + 1) * P].rearrange("p (g j d) -> p g j d", g=NG0, j=HPG))
                last.then_inc(v_sb, 1)

            for c in range(2):
                step(c, c, 0, c, 0)
            for b in range(BATCH):
                first = 1 if b == 0 else 0
                with act.Fori(first, CPB // 2) as r:
                    for p in range(2):
                        step(r * 2 + (p + b * CPB), p, b, r * 2 + p, r + b * CPB // 2)

        @block.vector
        def _(dve):
            nc.vector.memset(Vc[:, :, :, :, :], 1.0).then_inc(ones, 1)

            def step(c, p):
                src = R[:, ds(c * CH, CH), :]
                moments(nc, dve, st, mv, src).then_inc(momented, 1)
                dve.wait_ge(rooted, upto(c))
                dve.wait_ge(n_ps, upto(c - 1))
                normalise(nc, dve, xn, src, mv, sd, rs).then_inc(n_sb, 1)
                dve.wait_ge(high, upto(c))
                nc.vector.tensor_tensor(out=rest[:, :, :], in0=pqk[:, :, :], in1=parts[:, p, :, 0, :], op=ALU.subtract)
                dve.drain()
                nc.vector.tensor_copy(parts[:, p, :, 1, :], rest[:, :, :])
                dve.drain()
                nc.vector.tensor_tensor(out=rest[:, :, :], in0=rest[:, :, :], in1=parts[:, p, :, 1, :], op=ALU.subtract)
                dve.drain()
                nc.vector.tensor_copy(parts[:, p, :, 2, :], rest[:, :, :]).then_inc(split, 1)
                dve.drain()

            for c in range(2):
                step(c, c)
            with dve.Fori(1, NC // 2) as r:
                for p in range(2):
                    step(r * 2 + p, p)

        @block.sync
        def _(sp):
            for b in range(BATCH):
                with sp.Fori(0, CPB // 2) as r:
                    for p in range(2):
                        cb = r * 2 + p
                        sp.wait_ge(split, upto(cb + b * CPB))
                        for i in range(2):
                            for a in range(NPART):
                                for g in range(NG0):
                                    sp.dma_start(
                                        scratch[b * NG0 + g, i, a, :, ds(cb * CW, CW)],
                                        parts[32 * g:32 * g + 32, p, i, a, :]).then_inc(written[p], 16)
            for p in range(2):
                sp.wait_ge(written[p], NC // 2 * NW)


def full_attention_pass(nc, Vc, AO, scratch, const):
    KT = NTB
    NQ = SEQ // QC
    NQT = QC // P
    NKB = SEQ // 512
    NGRP = BATCH * NG0
    with ExitStack() as ctx:
        k = Kit(nc, ctx, "fa_")
        qst = k.sb("qst", [P, 2, HPG, SEQ], BF16)
        kst = k.sb("kst", [P, 2, HPG, SEQ], BF16)
        vst = k.sb("vst", [P, 2, KT, HPG, 32])
        pe_ = k.sb("pexp", [P, 2, HPG, QC])
        mxb = k.sb("mxb", [P, HPG, NQT, NKB])
        mx = k.sb("mx", [P, NQT, HPG])
        mr = k.sb("mr", [P, NQT, HPG])
        mpart = k.sb("mpart", [P, NQT, HPG, NPART], BF16)
        oS = k.sb("oS", [P, QC])
        rs = k.sb("rs", [P, NQT * HPG])
        pM = k.ps("pM", [P, 2, 512])
        pS = k.ps("pS", [P, 4, 512])
        pO = k.ps("pO", [P, 512])
        pX = k.ps("pX", [P, 512])
        NDMA = 2 * NPART * NPART * HPG
        stacks = [k.sem(f"stacks{p}") for p in range(2)]
        v_in = k.sem("v_in")
        group_done = k.sem("group_done")
        cleared = k.sem("cleared")
        max_ps = k.sem("max_ps")
        max_sb = k.sem("max_sb")
        m_split = k.sem("m_split")
        m_ps = k.sem("m_ps")
        m_row = k.sem("m_row")
        s_ps = k.sem("s_ps")
        e_sb = k.sem("e_sb")
        pv_done = k.sem("pv_done")
        o_sb = k.sem("o_sb")
        o_tp = k.sem("o_tp")
        o_out = k.sem("o_out")
        block = ctx.enter_context(nc.Block())
        K3 = MROW + NPART

        def rounds(eng, emit):
            with eng.Fori(0, NGRP // 2) as r:
                for par in range(2):
                    gi = r * 2 + par
                    with eng.Fori(0, NQ - 1) as qc:
                        emit(gi, par, qc, gi * NQ + qc, False)
                    emit(gi, par, NQ - 1, gi * NQ + (NQ - 1), True)

        @block.sync
        def _(sp):

            def load(gi, par):
                for j in range(HPG):
                    for a in range(NPART):
                        for b in range(NPART):
                            row = (a * NPART + b) * HD0
                            for i, part, to in ((0, a, qst), (1, b, kst)):
                                src = scratch[ds(gi, 1), i, part, j * HD0:(j + 1) * HD0, :]
                                sp.dma_start(to[row:row + HD0, par, j, :],
                                             src.rearrange("g d t -> (g d) t")).then_inc(stacks[par], 16)

            sp.wait_ge(cleared, 1)
            load(0, 0)
            load(1, 1)
            with sp.Fori(1, NGRP // 2) as r:
                for par in range(2):
                    sp.wait_ge(group_done, r * 2 + (par - 1))
                    load(r * 2 + par, par)

        @block.gpsimd
        def _(pool):
            def take(gi, par):
                src = Vc[:, ds(gi, 1), :, :, :].rearrange("p g t j d -> p (g t) j d")
                nc.gpsimd.tensor_copy(vst[:, par, :, :, 0:HD0 + 1], src).then_inc(v_in, 1)
            nc.gpsimd.memset(vst[:, :, :, :, :], 0.0)
            pool.drain()
            take(0, 0)
            take(1, 1)
            with pool.Fori(1, NGRP // 2) as r:
                for par in range(2):
                    pool.wait_ge(group_done, r * 2 + (par - 1))
                    take(r * 2 + par, par)

        def n_max(n, s):
            return (n * KT + s) * NKB

        @block.tensor
        def _(pe):
            def max_scores(par, qc, n, s):
                j, qt = s // NQT, s % NQT
                for kb in range(NKB):
                    m = n_max(n, s) + kb
                    if not isinstance(m, int) or m >= 2:
                        pe.wait_ge(max_sb, m - 1)
                    nc.tensor.matmul(pM[:, kb % 2, :], qst[0:KST, par, j, ds(qc * QC + qt * P, P)],
                                     kst[0:KST, par, j, kb * 512:(kb + 1) * 512],
                                     start=True, stop=True).then_inc(max_ps, 1)

            def max_rows(n, first):
                pe.wait_ge(m_split, n + 1)
                if not first:
                    pe.wait_ge(o_out, n)
                for qt in range(NQT):
                    if not first or qt:
                        pe.wait_ge(m_row, n * NQT + qt)
                    for j in range(HPG):
                        last = nc.tensor.matmul(pX[MROW:MROW + NPART, j * P:(j + 1) * P], mpart[:, qt, j, :],
                                                const["identb"][:, :], start=True, stop=True)
                    last.then_inc(m_ps, 1)

            def scores(gi, par, qc, n, kt):
                for hp in range(2):
                    if kt == 0 and hp == 0:
                        pe.wait_ge(v_in, gi + 1)
                        pe.wait_ge(m_row, (n + 1) * NQT)
                    if kt:
                        pe.wait_ge(e_sb, (n * KT + kt) * 2 + (hp - 1))
                    for j in (2 * hp, 2 * hp + 1):
                        last = nc.tensor.matmul(pS[:, j, :], kst[0:K3, par, j, kt * P:(kt + 1) * P],
                                                qst[0:K3, par, j, ds(qc * QC, QC)], start=True, stop=True)
                    last.then_inc(s_ps, 1)

            def times_v(par, n, kt):
                pe.wait_ge(e_sb, (n * KT + kt + 1) * 2)
                for j in range(HPG):
                    last = nc.tensor.matmul(pO[32 * j:32 * j + 32, :], vst[:, par, kt, j, :], pe_[:, kt % 2, j, :],
                                            start=(kt == 0), stop=(kt == KT - 1))
                last.then_inc(pv_done, 1)

            def emit(r, par, qc, n, last_q, lead=True):
                if last_q and lead:
                    pe.wait_ge(stacks[1 - par], (r + (1 + par)) * (16 * NDMA))
                for kt in range(KT):
                    scores(r * 2 + par, par, qc, n, kt)
                    if lead:
                        if last_q:
                            max_scores(1 - par, 0, n + 1, kt)
                        else:
                            max_scores(par, qc + 1, n + 1, kt)
                    if kt:
                        times_v(par, n, kt - 1)
                times_v(par, n, KT - 1)
                if lead:
                    max_rows(n + 1, False)
                pe.wait_ge(o_sb, n + 1)
                if not lead:
                    pe.wait_ge(o_out, n + 1)
                pe.wait_ge(m_row, (n + 2) * NQT if lead else (n + 1) * NQT)
                for qt in range(NQT):
                    t = nc.tensor.transpose(pX[:, qt * P:(qt + 1) * P], oS[:, qt * P:(qt + 1) * P], const["ident"][:, :])
                t.then_inc(o_tp, 1)

            pe.wait_ge(stacks[0], 16 * NDMA)
            for s in range(KT):
                max_scores(0, 0, 0, s)
            max_rows(0, True)

            def group(r, par, lead):
                gi = r * 2 + par
                with pe.Fori(0, NQ - 1) as qc:
                    emit(r, par, qc, qc + gi * NQ, False)
                emit(r, par, NQ - 1, gi * NQ + (NQ - 1), True, lead)

            with pe.Fori(0, NGRP // 2 - 1) as r:
                group(r, 0, True)
                group(r, 1, True)
            group(NGRP // 2 - 1, 0, True)
            group(NGRP // 2 - 1, 1, False)

        @block.scalar
        def _(act):
            def emit(gi, par, qc, n, last_q):
                for kt in range(KT):
                    for hp in range(2):
                        act.wait_ge(s_ps, (n * KT + kt) * 2 + hp + 1)
                        if kt >= 2:
                            act.wait_ge(pv_done, n * KT + (kt - 1))
                        nc.scalar.activation(pe_[:, kt % 2, 2 * hp:2 * hp + 2, :], pS[:, 2 * hp:2 * hp + 2, :],
                                             ACT.Exp, scale=float(HD0) ** -0.5).then_inc(e_sb, 1)
                act.wait_ge(pv_done, (n + 1) * KT)
                nc.scalar.copy(oS[:, :], pO[:, :]).then_inc(o_sb, 1)

            rounds(act, emit)

        @block.vector
        def _(dve):
            nc.vector.memset(kst[:, :, :, :], 0.0)
            nc.vector.memset(qst[:, :, :, :], 0.0)
            dve.drain()
            nc.vector.memset(kst[MROW:MROW + NPART, :, :, :], -1.0).then_inc(cleared, 1)
            dve.drain()

            def maxima(n):
                for s in range(KT):
                    j, qt = s // NQT, s % NQT
                    for kb in range(NKB):
                        dve.wait_ge(max_ps, n_max(n, s) + kb + 1)
                        nc.vector.tensor_reduce(mxb[:, j, qt, kb:kb + 1], pM[:, kb % 2, :], AX.X, ALU.max).then_inc(max_sb, 1)

            def split(par, qc, n):
                dve.drain()
                nc.vector.tensor_reduce(mx[:, :, :].rearrange("p q j -> p j q"), mxb[:, :, :, :], AX.X, ALU.max)
                dve.drain()
                nc.vector.tensor_copy(mpart[:, :, :, 0], mx[:, :, :])
                dve.drain()
                nc.vector.tensor_tensor(out=mr[:, :, :], in0=mx[:, :, :], in1=mpart[:, :, :, 0], op=ALU.subtract)
                dve.drain()
                nc.vector.tensor_copy(mpart[:, :, :, 1], mr[:, :, :])
                dve.drain()
                nc.vector.tensor_tensor(out=mr[:, :, :], in0=mr[:, :, :], in1=mpart[:, :, :, 1], op=ALU.subtract)
                dve.drain()
                nc.vector.tensor_copy(mpart[:, :, :, 2], mr[:, :, :]).then_inc(m_split, 1)
                for qt in range(NQT):
                    dve.wait_ge(m_ps, n * NQT + qt + 1)
                    nc.vector.tensor_copy(qst[MROW:MROW + NPART, par, :, ds(qc * QC + qt * P, P)],
                                          pX[MROW:MROW + NPART, :].rearrange("p (j q) -> p j q", j=HPG)).then_inc(m_row, 1)

            def output(gi, qc, n):
                dve.wait_ge(o_tp, n + 1)
                o = pX[:, :].rearrange("p (a d) -> p a d", d=32)
                nc.vector.reciprocal(rs[:, :].unsqueeze(2), o[:, :, HD0:HD0 + 1])
                dve.drain()
                nc.vector.tensor_tensor(
                    out=AO[:, ds(gi * NQ + qc, 1), :, :].rearrange("p g a d -> p (g a) d"),
                    in0=o[:, :, 0:HD0], in1=bcast(rs[:, :], HD0), op=ALU.mult).then_inc(o_out, 1)

            def emit(gi, par, qc, n, last_q, lead=True):
                if lead:
                    maxima(n + 1)
                    if last_q:
                        split(1 - par, 0, n + 1)
                    else:
                        split(par, qc + 1, n + 1)
                output(gi, qc, n)
                if last_q:
                    dve.drain()
                    nc.vector.memset(mr[:, 0, 0:1], 0.0).then_inc(group_done, 1)

            nc.vector.memset(mx[:, :, :], 0.0).then_inc(o_out, 1)
            maxima(0)
            split(0, 0, 0)
            with dve.Fori(0, NGRP // 2 - 1) as r:
                for par in range(2):
                    gi = r * 2 + par
                    with dve.Fori(0, NQ - 1) as qc:
                        emit(gi, par, qc, gi * NQ + qc, False)
                    emit(gi, par, NQ - 1, gi * NQ + (NQ - 1), True)
            for par in range(2):
                gi = NGRP - 2 + par
                with dve.Fori(0, NQ - 1) as qc:
                    emit(gi, par, qc, qc + gi * NQ, False)
                emit(gi, par, NQ - 1, gi * NQ + (NQ - 1), True, lead=(par == 0))


def head_output_pass(nc, AO, R, w, const):
    NQ, NQT = SEQ // QC, QC // P
    with ExitStack() as ctx:
        k = Kit(nc, ctx, "ho_")
        at = k.sb("at", [P, 2, CH, D])
        aT = k.sb("aT", [P, CW])
        pa, py = k.ps("pa", [P, CW]), k.ps("py", [P, CW])
        a_in, a_ps, a_T, y_ps, y_in = (k.sem(n) for n in ("a_in", "a_ps", "a_T", "y_ps", "y_in"))
        block = ctx.enter_context(nc.Block())

        @block.tensor
        def _(pe):
            for c in range(NC):
                pe.wait_ge(a_in, upto(c))
                pe.wait_ge(a_T, upto(c - 1))
                for i in range(CH):
                    last = nc.tensor.transpose(pa[:, i * P:(i + 1) * P], at[:, c % 2, i, :], const["ident"][:, :])
                last.then_inc(a_ps, 1)
                pe.wait_ge(a_T, upto(c))
                pe.wait_ge(y_in, upto(c - 1))
                for i in range(CH):
                    last = nc.tensor.matmul(py[:, i * P:(i + 1) * P], aT[:, i * P:(i + 1) * P], w["proj"][:, :],
                                            start=True, stop=True)
                last.then_inc(y_ps, 1)

        @block.scalar
        def _(act):
            for c in range(NC):
                b, qc = c // NQ, c % NQ
                act.wait_ge(a_ps, upto(c - 2))
                for g in range(NG0):
                    src = AO[:, (b * NG0 + g) * NQ + qc, :, :].rearrange("p (t j) d -> p t (j d)", j=HPG)
                    last = nc.scalar.copy(at[:, c % 2, :, 32 * g:32 * g + 32], src)
                last.then_inc(a_in, 1)
                act.wait_ge(a_ps, upto(c))
                act.wait_ge(y_ps, upto(c - 1))
                nc.scalar.copy(aT[:, :], pa[:, :]).then_inc(a_T, 1)

        @block.vector
        def _(dve):
            for c in range(NC):
                r4 = R[:, c * CH:(c + 1) * CH, :]
                nc.vector.tensor_tensor(out=r4, in0=r4, in1=w["bias"][:, :].unsqueeze(1).broadcast_to([P, CH, D]), op=ALU.add)
                dve.wait_ge(y_ps, upto(c))
                dve.drain()
                nc.vector.tensor_tensor(out=r4, in0=r4, in1=py[:, :].rearrange("p (a n) -> p a n", n=D),
                                        op=ALU.add).then_inc(y_in, 1)
                dve.drain()


def fp4_levels(nc, dve, x, xabs, nb, b, halved, absed):
    ab, lev, up = b["ab"][:, 0:nb, :], b["lev"][:, 0:nb, :], b["up"][:, 0:nb, :]
    bm, sc, rc, hs = (b[n][:, 0:nb] for n in ("bm", "sc", "rc", "hs"))
    nc.vector.tensor_reduce(bm, x, AX.X, ALU.max, apply_absolute_value=True)
    dve.drain()
    nc.vector.tensor_scalar(sc, bm, 1.0 / 6.0, 1e-12, ALU.mult, ALU.max)
    dve.drain()
    nc.vector.tensor_scalar(hs, sc, 0.5, None, ALU.mult).then_inc(halved, 1)
    nc.vector.reciprocal(rc, sc)
    dve.drain()
    absed()
    nc.vector.tensor_tensor(out=ab, in0=xabs, in1=bcast(rc, FB), op=ALU.mult)
    dve.drain()
    nc.vector.tensor_scalar(lev, ab, 5.0, 2.0, ALU.is_gt, ALU.mult)
    nc.vector.tensor_scalar(up, ab, 1.75, None, ALU.is_gt)
    for mid in (3.5, 2.5):
        dve.drain()
        nc.vector.scalar_tensor_tensor(out=lev, in0=ab, scalar=mid, in1=lev, op0=ALU.is_gt, op1=ALU.add)
    dve.drain()
    nc.vector.scalar_tensor_tensor(out=lev, in0=lev, scalar=2.0, in1=up, op0=ALU.mult, op1=ALU.add)
    for mid in (1.25, 0.75, 0.25):
        dve.drain()
        nc.vector.scalar_tensor_tensor(out=lev, in0=ab, scalar=mid, in1=lev, op0=ALU.is_gt, op1=ALU.add)
    dve.drain()


def fp4_pass(nc, R, w_gate, w_up, w_down, const):
    NBX, NBH = D // FB, F0 // FB
    FCH = [P, P, F0 - 2 * P]
    NWB = 2 * 3 * NBX + NBH
    with ExitStack() as ctx:
        k = Kit(nc, ctx, "fp_")
        ws = k.sb("ws", [P, NWB, FB])
        wg, wu = k.sb("wg", [P, F0]), k.sb("wu", [P, F0])
        wd = k.sb("wd", [P, 3, D])
        buf = {"ab": k.sb("ab", [P, CH * NBH, FB]), "lev": k.sb("lev", [P, CH * NBH, FB]),
               "up": k.sb("up", [P, CH * NBH, FB])}
        for n in ("bm", "sc", "rc", "hs"):
            buf[n] = k.sb(n, [P, CH * NBH])
        sg = k.sb("sg", [P, CH * NBH, FB])
        ax = k.sb("ax", [P, CH * NBH, FB])
        st, mv = k.sb("st", [P, CH, 6]), k.sb("mv", [P, CH, 2])
        sd, rs = k.sb("sd", [P, CH]), k.sb("rs", [P, CH])
        xn = k.sb("xn", [P, CH, D])
        xq = k.sb("xq", [P, CH, D])
        xqT = k.sb("xqT", [P, 2, CW])
        gs = k.sb("gs", [P, 2, F0])
        h = k.sb("h", [P, CH, F0])
        hq = k.sb("hq", [P, CH, F0])
        hqT = k.sb("hqT", [P, 2, 3, P])
        pa = k.ps("pa", [P, CW])
        pg, pu = k.ps("pg", [P, 2, 512]), k.ps("pu", [P, 2, 512])
        pt = k.ps("pt", [P, 2, 512])
        py = k.ps("py", [P, CW])
        w_in, w_zero = k.sem("w_in"), k.sem("w_zero")
        halved, signs, signed = k.sem("halved"), k.sem("signs"), k.sem("signed")
        rounded, absed = k.sem("rounded"), k.sem("absed")
        w_ps, w_sb = k.sem("w_ps"), k.sem("w_sb")
        wctx = ExitStack()
        blockw = wctx.enter_context(nc.Block())

        @blockw.sync
        def _(sp):
            sp.wait_ge(w_zero, 1)
            n = 0
            for o, src in ((0, w_gate), (3 * NBX, w_up)):
                for j, m in enumerate(FCH):
                    sp.dma_start(ws[0:m, o + j * NBX:o + (j + 1) * NBX, :].rearrange("p a b -> p (a b)"),
                                 src[j * P:j * P + m, :]).then_inc(w_in, 16)
            sp.dma_start(ws[:, 6 * NBX:, :].rearrange("p a b -> p (a b)"), w_down).then_inc(w_in, 16)

        @blockw.scalar
        def _(act):
            act.wait_ge(w_in, 16 * 7)
            nc.scalar.activation(ax[:, 0:NWB, :], ws[:, :, :], ACT.Abs).then_inc(absed, 1)
            nc.scalar.activation(sg[:, 0:NWB, :], ws[:, :, :], ACT.Sign).then_inc(signs, 1)
            for n in range(9):
                act.wait_ge(w_ps, n + 1)
                kind, j = n // 3, n % 3
                if kind < 2:
                    dst = (wg, wu)[kind][:, j * P:j * P + FCH[j]]
                    src = pt[:, n % 2, 0:FCH[j]]
                else:
                    dst = wd[0:FCH[j], j, :]
                    src = pt[0:FCH[j], n % 2, 0:D]
                nc.scalar.copy(dst, src).then_inc(w_sb, 1)

        @blockw.gpsimd
        def _(pool):
            pool.wait_ge(signs, 1)
            pool.wait_ge(halved, 1)
            nc.gpsimd.tensor_tensor(out=sg[:, 0:NWB, :], in0=sg[:, 0:NWB, :], in1=bcast(buf["hs"][:, 0:NWB], FB),
                                    op=ALU.mult).then_inc(signed, 1)

        @blockw.vector
        def _(dve):
            nc.vector.memset(ws[:, :, :], 0.0).then_inc(w_zero, 1)
            dve.wait_ge(w_in, 16 * 7)
            fp4_levels(nc, dve, ws[:, :, :], ax[:, 0:NWB, :], NWB, buf, halved, lambda: dve.wait_ge(absed, 1))
            dve.wait_ge(signed, 1)
            nc.vector.tensor_tensor(out=ws[:, :, :], in0=buf["lev"][:, 0:NWB, :], in1=sg[:, 0:NWB, :],
                                    op=ALU.mult).then_inc(rounded, 1)

        @blockw.tensor
        def _(pe):
            pe.wait_ge(rounded, 1)
            for n in range(9):
                if n >= 2:
                    pe.wait_ge(w_sb, n - 1)
                kind, j = n // 3, n % 3
                m = FCH[j]
                if kind < 2:
                    src = ws[0:m, (kind * 3 + j) * NBX:(kind * 3 + j + 1) * NBX, :].rearrange("p a b -> p (a b)")
                    nc.tensor.transpose(pt[:, n % 2, 0:m], src, const["ident"][0:m, 0:m]).then_inc(w_ps, 1)
                else:
                    o = 6 * NBX + j * NBX
                    src = ws[:, o:o + m // FB, :].rearrange("p a b -> p (a b)")
                    nc.tensor.transpose(pt[0:m, n % 2, 0:D], src, const["ident"][:, :]).then_inc(w_ps, 1)

        wctx.close()
        sgx = k.sb("sgx", [P, CH * NBX, FB])
        axx = k.sb("axx", [P, CH * NBX, FB])
        n_in = k.sem("n_in")
        absed_x, absed_h = k.sem("absed_x"), k.sem("absed_h")
        momented, rooted = k.sem("momented"), k.sem("rooted")
        halved_x, signs_x, signed_x, xq_sb = (k.sem(n) for n in ("halved_x", "signs_x", "signed_x", "xq_sb"))
        halved_h, signs_h, signed_h, hq_sb = (k.sem(n) for n in ("halved_h", "signs_h", "signed_h", "hq_sb"))
        x_ps, x_T = k.sem("x_ps"), k.sem("x_T")
        g_ps, u_ps, g_sb, h_sb = k.sem("g_ps"), k.sem("u_ps"), k.sem("g_sb"), k.sem("h_sb")
        t_ps, t_sb, y_ps, y_in = k.sem("t_ps"), k.sem("t_sb"), k.sem("y_ps"), k.sem("y_in")
        block = ctx.enter_context(nc.Block())

        def blocks(ap):
            return ap.rearrange("p a (n b) -> p (a n) b", b=FB)

        @block.tensor
        def _(pe):

            def turn(c, i):
                pe.wait_ge(t_sb, upto(c, CH, i - 2 - CH + 1)) if not isinstance(c, int) or c * CH + i >= 2 else None
                for j, m in enumerate(FCH):
                    last = nc.tensor.transpose(pt[0:m, i % 2, j * P:(j + 1) * P], hq[:, i, j * P:j * P + m],
                                               const["ident"][:, :])
                last.then_inc(t_ps, 1)

            def down(c, i):
                pe.wait_ge(t_sb, upto(c, CH, i - CH + 1))
                if i == 0:
                    pe.wait_ge(y_in, upto(c - 1))
                for j, m in enumerate(FCH):
                    last = nc.tensor.matmul(py[:, i * P:(i + 1) * P], hqT[0:m, i % 2, j, :], wd[0:m, j, :],
                                            start=(j == 0), stop=(j == 2))
                last.then_inc(y_ps, 1)

            def step(c, p):
                if has(c - 2, NC):
                    pe.wait_ge(hq_sb, upto(c - 2))
                    turn(c - 2, 0)
                    for i in range(1, CH):
                        turn(c - 2, i)
                        down(c - 2, i - 1)
                    down(c - 2, CH - 1)
                if has(c - 1, NC):
                    pe.wait_ge(x_T, upto(c - 1))
                    for i in range(CH):
                        skip = isinstance(c, int) and (c - 1) * CH + i < 2
                        if not skip:
                            pe.wait_ge(g_sb, upto(c - 1, CH, i - 2 - CH + 1))
                        nc.tensor.matmul(pg[:, i % 2, 0:F0], xqT[:, 1 - p, i * P:(i + 1) * P], wg[:, :],
                                         start=True, stop=True).then_inc(g_ps, 1)
                        if not skip:
                            pe.wait_ge(h_sb, upto(c - 1, CH, i - 2 - CH + 1))
                        nc.tensor.matmul(pu[:, i % 2, 0:F0], xqT[:, 1 - p, i * P:(i + 1) * P], wu[:, :],
                                         start=True, stop=True).then_inc(u_ps, 1)
                if has(c, NC):
                    pe.wait_ge(xq_sb, upto(c))
                    pe.wait_ge(x_T, upto(c - 1))
                    for i in range(CH):
                        last = nc.tensor.transpose(pa[:, i * P:(i + 1) * P], xq[:, i, :], const["ident"][:, :])
                    last.then_inc(x_ps, 1)

            lagged(pe, NC, 2, 2, 0, step, peel=4)

        @block.scalar
        def _(act):

            def step(c, p):
                if has(c - 2, NC):
                    for i in range(CH):
                        act.wait_ge(t_ps, upto(c - 2, CH, i - CH + 1))
                        if not (isinstance(c, int) and (c - 2) * CH + i < 2):
                            act.wait_ge(y_ps, upto(c - 2, CH, i - 2 - CH + 1))
                        nc.scalar.copy(hqT[:, i % 2, 0:2, :], pt[:, i % 2, 0:2 * P].rearrange("p (j n) -> p j n", n=P))
                        nc.scalar.copy(hqT[0:FCH[2], i % 2, 2, :], pt[0:FCH[2], i % 2, 2 * P:3 * P]).then_inc(t_sb, 1)
                if has(c, NC):
                    act.wait_ge(momented, upto(c))
                    nc.scalar.activation(sd[:, :], mv[:, :, 1], ACT.Sqrt, bias=const["eps"][:, 0:1]).then_inc(rooted, 1)
                    act.wait_ge(n_in, upto(c))
                    act.wait_ge(xq_sb, upto(c - 1))
                    nc.scalar.activation(axx[:, :, :], blocks(xn[:, :, :]), ACT.Abs).then_inc(absed_x, 1)
                    nc.scalar.activation(sgx[:, :, :], blocks(xn[:, :, :]), ACT.Sign).then_inc(signs_x, 1)
                if has(c - 1, NC):
                    for i in range(CH):
                        act.wait_ge(g_ps, upto(c - 1, CH, i - CH + 1))
                        if not (isinstance(c, int) and (c - 1) * CH + i < 2):
                            act.wait_ge(h_sb, upto(c - 1, CH, i - 2 - CH + 1))
                        nc.scalar.activation(gs[:, i % 2, :], pg[:, i % 2, 0:F0], ACT.Silu).then_inc(g_sb, 1)
                    act.wait_ge(h_sb, upto(c - 1, CH))
                    act.wait_ge(hq_sb, upto(c - 2))
                    nc.scalar.activation(ax[:, :, :], blocks(h[:, :, :]), ACT.Abs).then_inc(absed_h, 1)
                    nc.scalar.activation(sg[:, :, :], blocks(h[:, :, :]), ACT.Sign).then_inc(signs_h, 1)
                if has(c, NC):
                    act.wait_ge(x_ps, upto(c))
                    nc.scalar.copy(xqT[:, p, :], pa[:, :]).then_inc(x_T, 1)

            lagged(act, NC, 2, 2, 0, step, peel=4)

        @block.gpsimd
        def _(pool):

            def step(c, p):
                for sign, hv, out, t, d, nb in ((signs_x, halved_x, signed_x, sgx, c, CH * NBX),
                                                (signs_h, halved_h, signed_h, sg, c - 1, CH * NBH)):
                    if has(d, NC):
                        pool.wait_ge(sign, upto(d))
                        pool.wait_ge(hv, upto(d))
                        nc.gpsimd.tensor_tensor(out=t[:, :, :], in0=t[:, :, :], in1=bcast(buf["hs"][:, 0:nb], FB),
                                                op=ALU.mult).then_inc(out, 1)

            lagged(pool, NC, 2, 2, 0, step, peel=4)

        @block.vector
        def _(dve):

            def step(c, p):
                if has(c, NC):
                    src = R[:, ds(c * CH, CH), :]
                    moments(nc, dve, st, mv, src).then_inc(momented, 1)
                    dve.wait_ge(rooted, upto(c))
                    dve.wait_ge(signs_x, upto(c - 1))
                    normalise(nc, dve, xn, src, mv, sd, rs).then_inc(n_in, 1)
                    dve.drain()
                    fp4_levels(nc, dve, blocks(xn[:, :, :]), axx[:, :, :], CH * NBX, buf, halved_x,
                               lambda: dve.wait_ge(absed_x, upto(c)))
                    dve.wait_ge(signed_x, upto(c))
                    dve.wait_ge(x_ps, upto(c - 1))
                    nc.vector.tensor_tensor(out=blocks(xq[:, :, :]), in0=buf["lev"][:, 0:CH * NBX, :],
                                            in1=sgx[:, :, :], op=ALU.mult).then_inc(xq_sb, 1)
                if has(c - 1, NC):
                    dve.wait_ge(signs_h, upto(c - 2))
                    for i in range(CH):
                        dve.wait_ge(g_sb, upto(c - 1, CH, i - CH + 1))
                        dve.wait_ge(u_ps, upto(c - 1, CH, i - CH + 1))
                        nc.vector.tensor_tensor(out=h[:, i, :], in0=gs[:, i % 2, :], in1=pu[:, i % 2, 0:F0],
                                                op=ALU.mult).then_inc(h_sb, 1)
                    dve.drain()
                    fp4_levels(nc, dve, blocks(h[:, :, :]), ax[:, :, :], CH * NBH, buf, halved_h,
                               lambda: dve.wait_ge(absed_h, upto(c - 1)))
                    dve.wait_ge(signed_h, upto(c - 1))
                    dve.wait_ge(t_ps, upto(c - 2, CH))
                    nc.vector.tensor_tensor(out=blocks(hq[:, :, :]), in0=buf["lev"][:, :, :],
                                            in1=sg[:, :, :], op=ALU.mult).then_inc(hq_sb, 1)
                    dve.drain()
                if has(c - 2, NC):
                    dve.wait_ge(y_ps, upto(c - 2, CH))
                    r4 = R[:, ds((c - 2) * CH, CH), :]
                    nc.vector.tensor_tensor(out=r4, in0=r4, in1=py[:, :].rearrange("p (a n) -> p a n", n=D),
                                            op=ALU.add).then_inc(y_in, 1)

            lagged(dve, NC, 2, 2, 0, step, peel=4)


def row(a, n=P):
    return a.unsqueeze(0).broadcast_to([P, n])


def global_attention_stage(nc, X, a, scratch, const):
    with ExitStack() as ctx:
        k = Kit(nc, ctx, "A_")
        w = {"qkv": k.sb("qkv", [P, 3 * D]), "proj": k.sb("proj", [P, D]), "bias": k.sb("bias", [P, D])}
        AO = k.sb("AO", [P, NT, H0, HD0])
        Vc = k.sb("Vc", [P, BATCH * NG0, NTB, HPG, HD0 + 1])
        move_pass(nc, "A_w_", [(w["qkv"][:, :], a["L0_attn_w_qkv"]), (w["proj"][:, :], a["L0_attn_w_proj"]),
                               (w["bias"][:, :], row(a["L0_attn_b_proj"]))])
        split_qkv_pass(nc, X, Vc, scratch, w, const)
        full_attention_pass(nc, Vc, AO, scratch, const)
        head_output_pass(nc, AO, X, w, const)


def window_stage(nc, E, a, scratch, const):
    perm = scratch.rearrange("(b m t j) f -> b j m t f", b=BATCH, m=64, t=NTB, j=2)
    plain = scratch.rearrange("(t p) f -> p t f", p=P)
    permuted = [(E[64 * j:64 * j + 64, b * NTB:(b + 1) * NTB, :], perm[b, j]) for b in range(BATCH) for j in range(2)]
    for pre, ff, kind, own in (("la", "lf", "w32", W32), ("sa", "pf", "w64", 64)):
        A, B = "L1_attn_" + pre, "L1_attn_" + ff
        with ExitStack() as ctx:
            k = Kit(nc, ctx, "C_" + pre)
            w = {"wqk": k.sb("wqk", [P, 2 * INNER]), "wv": k.sb("wv", [P, INNER]), "wo": k.sb("wo", [P, HP, D]),
                 "own": k.sb("own", [P, own]), "pb": k.sb("pb", [P, D])}
            f = {"w1": k.sb("w1", [P, F1]), "w2": k.sb("w2", [P, F1 // P, D]), "b1": k.sb("b1", [P, F1 // P])}
            for n in ("g1", "o1", "b2", "g2", "o2"):
                f[n] = k.sb(n, [P, D])

            def per_head(ap):
                return ap.rearrange("p (h k) -> p h k", k=HD)

            move_pass(nc, "C_w_" + pre, [
                (per_head(w["wqk"][:, 0:INNER]), a[A + "_wqs"].rearrange("h d k -> d h k")),
                (per_head(w["wqk"][:, INNER:]), a[A + "_wks"].rearrange("h d k -> d h k")),
                (per_head(w["wv"][:, :]), a[A + "_wvs"].rearrange("h d k -> d h k")),
                (w["wo"][:, :, :], a[A + "_pw"].rearrange("(c p) n -> p c n", p=P)),
                (w["own"][:, :], a["c_own%d" % own]), (w["pb"][:, :], row(a[A + "_pb"]))]
                + (permuted if kind == "w64" else []))
            attention_pass(nc, "C_a_" + pre, kind, E, w, const, prefetch=[
                (f["w1"][:, :], a[B + "_w1"]),
                (f["w2"][:, :, :], a[B + "_w2"].rearrange("(c p) n -> p c n", p=P)),
                (f["g1"][:, :], row(a[A + "_g"])), (f["o1"][:, :], row(a[A + "_b"])),
                (f["b2"][:, :], row(a[B + "_b2"])), (f["g2"][:, :], row(a[B + "_g"])),
                (f["o2"][:, :], row(a[B + "_b"]))] + [
                (f["b1"][:, j:j + 1], a[B + "_b1"][P * j:P * j + P].unsqueeze(1)) for j in range(F1 // P)])
            relu_pass(nc, "C_f_" + pre, E, f, const)
            if kind == "w32":
                move_pass(nc, "C_s_", [(plain, E[:, :, :])])
            else:
                move_pass(nc, "C_t_", [(src, to) for to, src in permuted])
                move_pass(nc, "C_u_", [(E[:, :, :], plain)])


def rotary_stage(nc, Y, a, const):
    with ExitStack() as ctx:
        k = Kit(nc, ctx, "D_")
        w = {"wqk": k.sb("wqk", [P, 2 * INNER]), "wv": k.sb("wv", [P, INNER]), "wo": k.sb("wo", [P, HP, D]),
             "mask": k.sb("mask", [P, NT, 64], BF16), "kfac": k.sb("kfac", [P, 1]), "inner": k.sb("inner", [P, NT]),
             "rot": k.sb("rot", [P, NT, 4 * HD]), "qk_scale": k.sb("qk_scale", [P, 4 * HD])}
        f = {"w1": k.sb("w1", [P, 2 * F2]), "w2": k.sb("w2", [P, NJ2, D]), "b1a": k.sb("b1a", [P, NJ2]),
             "b1g": k.sb("b1g", [P, NJ2]), "g": k.sb("g", [P, 1]), "b": k.sb("b", [P, 1]), "inner": w["inner"]}

        def layer_of(name, l):
            return a["L1_ffn_" + name][ds(l, 1)]

        def attention_weights(l):
            wqkv = layer_of("Wqkv", l).rearrange("l k n -> (l k) n")
            return [(w["wqk"][:, :], wqkv[:, 0:2 * INNER]), (w["wv"][:, :], wqkv[:, 2 * INNER:]),
                    (w["wo"][:, :, :], layer_of("Wo", l).rearrange("l (c p) n -> p (l c) n", p=P))] + [
                    (w["qk_scale"][:, HD * i:HD * i + HD],
                     layer_of("q_scale" if i < 2 else "k_scale", l).broadcast_to([P, HD])) for i in range(4)]

        def feed_weights(l):
            w2 = layer_of("W2", l)
            moves = [(f["w1"][:, :], layer_of("W1", l).rearrange("l k n -> (l k) n")),
                     (f["w2"][:, 0:2, :], w2[:, 0:2 * P, :].rearrange("l (c p) n -> p (l c) n", p=P)),
                     (f["w2"][0:JW2[2], 2, :], w2[:, 2 * P:F2, :].rearrange("l k n -> (l k) n")),
                     (f["w2"][ONE_ROW:ONE_ROW + 1, 2, :], layer_of("b2", l)),
                     (f["g"][:, :], layer_of("ln_g", l).rearrange("l p -> p l")),
                     (f["b"][:, :], layer_of("ln_b", l).rearrange("l p -> p l"))]
            b1 = layer_of("b1", l)
            for j, m in enumerate(JW2):
                for o, t in ((0, "b1a"), (F2, "b1g")):
                    moves.append((f[t][0:m, j:j + 1], b1[:, o + P * j:o + P * j + m].rearrange("l p -> p l")))
            return moves

        with nc.Block() as block:
            @block.vector
            def _(dve):
                nc.vector.memset(f["w2"][64:P, NJ2 - 1, :], 0.0)
        move_pass(nc, "D_w_", attention_weights(0) + [
            (w["mask"][:, :, :], a["c_mask"]), (w["kfac"][:, :], a["c_kfac"]),
            (w["inner"][:, :], a["c_inner"]), (w["rot"][:, :, :], a["c_rot"])])
        with nc.Fori(0, DEPTH - 1) as l:
            attention_pass(nc, "D_a_", "local", Y, w, const, prefetch=feed_weights(l))
            gated_pass(nc, "D_f_", Y, f, const, prefetch=attention_weights(l + 1))
        attention_pass(nc, "D_b_", "local", Y, w, const, prefetch=feed_weights(DEPTH - 1))
        gated_pass(nc, "D_g_", Y, f, const)


def preln_program(nc, a, out):
    parts = nc.dram_tensor("qk_parts", (BATCH * NG0, 2, NPART, HPG * HD0, SEQ), BF16).ap()
    order = nc.dram_tensor("reorder", (TOK, D), F32).ap()
    with ExitStack() as ctx:
        k = Kit(nc, ctx, "")
        X = k.sb("X", [P, NT, D])
        const = {"ident": k.sb("ident", [P, P]), "identb": k.sb("identb", [P, P], BF16), "eps": k.sb("eps", [P, 1]),
                 "ident_d": a["c_ident"], "identb_d": a["c_identb"]}
        load_pass(nc, const, X, a["L0_attn_x"])
        global_attention_stage(nc, X, a, parts, const)
        fp4_pass(nc, X, a["L0_ffn_w_gate"], a["L0_ffn_w_up"], a["L0_ffn_w_down"], const)
        Y = k.sb("Y", [P, NT, D])
        add_norm_pass(nc, "n1_", X, Y, False)
        window_stage(nc, Y, a, order, const)
        add_norm_pass(nc, "n2_", X, Y, True)
        rotary_stage(nc, Y, a, const)
        add_pass(nc, X, Y)
        store_pass(nc, X, out)


def host_tables():
    bf16 = mybir.dt.np(BF16)
    f32 = np.float32
    p = np.arange(P)
    half = np.arange(0, HD, 2, dtype=f32)
    inv_freq = (f32(1.0) / f32(10000.0) ** (half / f32(HD))).astype(f32)
    freqs = np.arange(SEQ, dtype=f32)[:, None] * inv_freq[None, :]
    base = (half.astype(np.float64) + 0.4 * HD) / (1.4 * HD)
    scale = base[None, :] ** ((p[:, None] - P // 2) / 16.0)
    cos = np.cos(freqs.astype(np.float64)).reshape(NTB, P, 32)
    sin = np.sin(freqs.astype(np.float64)).reshape(NTB, P, 32)
    rot = np.zeros((P, NT, 256))
    for t in range(NT):
        c, s = cos[t % NTB], sin[t % NTB]
        for o, m in ((0, scale), (128, 1.0 / scale)):
            rot[:, t, o:o + 128] = np.concatenate([c * m, c * m, s * m, -s * m], axis=1)
    mask = np.zeros((P, NT, 2 * W32))
    i, j = (p % W32)[:, None], (np.arange(2 * W32) - W32)[None, :]
    mask[:] = np.where((i < j) | (i > j + W32), -1e30, 0.0)[:, None, :]
    mask[:W32, ::NTB, :W32] = -1e30
    inner = np.ones((P, NT))
    inner[:, ::NTB] = 0.0
    own = (p[:, None] % 64 == np.arange(64)[None, :])
    own32 = (p[:, None] % 32 == np.arange(32)[None, :])
    return {
        "c_ident": np.eye(P, dtype=f32),
        "c_identb": np.eye(P).astype(bf16),
        "c_rot": rot.astype(f32),
        "c_mask": mask.astype(bf16),
        "c_kfac": np.tile(base ** (P / 16.0), 4).astype(f32)[:, None],
        "c_inner": inner.astype(f32),
        "c_own64": own.astype(f32),
        "c_own32": own32.astype(f32),
    }


def kernel(**inputs):
    import concourse.bacc as bacc
    from concourse.bass_utils import run_bass_kernel_spmd

    nc = bacc.Bacc("TRN2", target_bir_lowering=False, num_devices=1)
    arrays = {n: np.ascontiguousarray(v) for n, v in inputs.items()}
    arrays.update(host_tables())
    a = {n: nc.dram_tensor(n, v.shape, mybir.dt.from_np(v.dtype), kind="ExternalInput").ap()
         for n, v in arrays.items()}
    out = nc.dram_tensor("out", (BATCH, SEQ, D), F32, kind="ExternalOutput").ap()
    preln_program(nc, a, out)
    result = run_bass_kernel_spmd(nc, [arrays], core_ids=[0])
    return result.results[0]["out"]
```

```python
from contextlib import ExitStack

import concourse.bass as bass
from concourse import mybir
from concourse.alu_op_type import AluOpType as ALU
import numpy as np

F32 = mybir.dt.float32
BF16 = mybir.dt.bfloat16
ACT = mybir.ActivationFunctionType
AX = mybir.AxisListType
ds = bass.ds

P = 128
D = 128
BATCH, SEQ = 2, 2048
TOK = BATCH * SEQ
NT = TOK // P
NTB = SEQ // P
CH = 4
NC = NT // CH
CW = CH * P
EPS = 1e-5
W32 = 32

H0, HD0 = 16, 8
NPART = 3
KST = NPART * NPART * HD0
MROW = 96
HPG = 4
NG0 = H0 // HPG
QC = 512

H, HD = 16, 64
INNER = H * HD
HP = H // 2
DEPTH = 6
F0 = 352
FB = 16
F1 = 512
F2 = 341
NJ2 = 3
JW2 = [128, 128, F2 - 256]
ONE_ROW = 96


def upto(i, per=1, extra=0):
    n = (i + 1) * per + extra
    return max(n, 0) if isinstance(i, int) else n


def lagged(eng, n, unroll, lag, ahead, emit, peel=0):
    head = max(lag + (-lag) % unroll, peel)
    rounds = (n - head - ahead) // unroll
    for t in range(head):
        emit(t, t % unroll)
    if rounds > 0:
        with eng.Fori(0, rounds) as r:
            for p in range(unroll):
                emit(r * unroll + (head + p), p)
    for t in range(head + rounds * unroll, n + lag):
        emit(t, t % unroll)


def has(t, n):
    return not isinstance(t, int) or 0 <= t < n


class Kit:
    def __init__(self, nc, ctx, tag):
        self.nc, self.ctx, self.tag = nc, ctx, tag
        self.sems = []
        ctx.callback(self.clear)

    def sb(self, name, shape, dt=F32):
        return self.ctx.enter_context(self.nc.sbuf_tensor(self.tag + name, shape, dt))

    def ps(self, name, shape, dt=F32):
        return self.ctx.enter_context(self.nc.psum_tensor(self.tag + name, shape, dt))

    def sem(self, name):
        self.sems.append(self.nc.alloc_semaphore(name=self.tag + name))
        return self.sems[-1]

    def clear(self):
        if self.sems:
            self.nc.clear_and_free_semaphores(self.sems)
            self.nc.all_engine_barrier()


def bcast(ap, n):
    return ap.unsqueeze(2).broadcast_to([ap.shape[0], ap.shape[1], n])


def fetch(sp, moves, arrived):
    if not moves:
        return
    for to, src in moves:
        sp.dma_start(to, src).then_inc(arrived, 16)
    sp.wait_ge(arrived, 16 * len(moves))


def move_pass(nc, tag, moves):
    with ExitStack() as ctx:
        k = Kit(nc, ctx, tag)
        moved = k.sem("moved")
        block = ctx.enter_context(nc.Block())

        @block.sync
        def _(sp):
            fetch(sp, moves, moved)


def add_norm_pass(nc, tag, X, Y, add):
    with ExitStack() as ctx:
        k = Kit(nc, ctx, tag)
        st, mv = k.sb("st", [P, NT, 6]), k.sb("mv", [P, NT, 2])
        sd, rs = k.sb("sd", [P, NT]), k.sb("rs", [P, NT])
        eps = k.sb("eps", [P, 1])
        momented, rooted = k.sem("momented"), k.sem("rooted")
        block = ctx.enter_context(nc.Block())

        @block.scalar
        def _(act):
            act.wait_ge(momented, 1)
            nc.scalar.activation(sd[:, :], mv[:, :, 1], ACT.Sqrt, bias=eps[:, 0:1]).then_inc(rooted, 1)

        @block.vector
        def _(dve):
            nc.vector.memset(eps[:, :], EPS)
            if add:
                with dve.Fori(0, NC) as c:
                    x4 = X[:, ds(c * CH, CH), :]
                    nc.vector.tensor_tensor(out=x4, in0=x4, in1=Y[:, ds(c * CH, CH), :], op=ALU.add)
                dve.drain()
            with dve.Fori(0, NC) as c:
                for i in range(CH):
                    nc.vector.bn_stats(st[:, ds(c * CH + i, 1), :].rearrange("p a s -> p (a s)"),
                                       X[:, ds(c * CH + i, 1), :].rearrange("p a f -> p (a f)"))
            dve.drain()
            for t in range(NT):
                nc.vector.bn_aggr(mv[:, t, :], st[:, t, :])
            dve.drain().then_inc(momented, 1)
            dve.wait_ge(rooted, 1)
            nc.vector.reciprocal(rs[:, :], sd[:, :])
            dve.drain()
            with dve.Fori(0, NC) as c:
                for i in range(CH):
                    t = c * CH + i
                    nc.vector.tensor_scalar(Y[:, ds(t, 1), :].rearrange("p a f -> p (a f)"),
                                            X[:, ds(t, 1), :].rearrange("p a f -> p (a f)"),
                                            mv[:, ds(t, 1), 0:1].rearrange("p a s -> p (a s)"), rs[:, ds(t, 1)],
                                            ALU.subtract, ALU.mult)


def add_pass(nc, X, Y):
    with nc.Block() as block:

        @block.vector
        def _(dve):
            with dve.Fori(0, NC) as c:
                x4 = X[:, ds(c * CH, CH), :]
                nc.vector.tensor_tensor(out=x4, in0=x4, in1=Y[:, ds(c * CH, CH), :], op=ALU.add)


def load_pass(nc, const, X, x):
    with ExitStack() as ctx:
        k = Kit(nc, ctx, "ld_")
        loaded = k.sem("loaded")
        block = ctx.enter_context(nc.Block())

        @block.sync
        def _(sp):
            sp.dma_start(X[:, :, :], x.rearrange("b (t p) f -> p (b t) f", p=P)).then_inc(loaded, 16)
            sp.dma_start(const["ident"][:, :], const["ident_d"]).then_inc(loaded, 16)
            sp.dma_start(const["identb"][:, :], const["identb_d"]).then_inc(loaded, 16)
            sp.wait_ge(loaded, 48)

        @block.vector
        def _(dve):
            nc.vector.memset(const["eps"][:, :], EPS)


def store_pass(nc, X, out):
    with ExitStack() as ctx:
        k = Kit(nc, ctx, "st_")
        stored = k.sem("stored")
        block = ctx.enter_context(nc.Block())

        @block.sync
        def _(sp):
            sp.dma_start(out.rearrange("b (t p) f -> p (b t) f", p=P), X[:, :, :]).then_inc(stored, 16)
            sp.wait_ge(stored, 16)


def attention_pass(nc, tag, kind, R, w, const, prefetch=()):
    local = kind == "local"
    W = 32 if kind == "w32" else 64
    SCALE = 8.0 if local else 1.0 / 8.0
    with ExitStack() as ctx:
        k = Kit(nc, ctx, tag)
        xt = k.sb("xt", [P, 2, D])
        xs = k.sb("xs", [P, 2, P])
        carry = k.sb("carry", [P, 2])
        qT = k.sb("qT", [P, HP, P])
        kT = k.sb("kT", [P, 2, HP, W32 + P])
        v = k.sb("v", [P, 4, INNER])
        z = k.sb("z", [P, H * W])
        pr = k.sb("pr", [P, H * W])
        pn = k.sb("pn", [P, H * W])
        pT = k.sb("pT", [P, H, W // 32, 32])
        band = k.sb("band", [P, H, P])
        edge = k.sb("edge", [P, H, W32]) if local else None
        oT = k.sb("oT", [P, HP, P])
        mx = k.sb("mx", [P, H])
        sm = k.sb("sm", [P, H])
        rs = k.sb("rs", [P, H])
        if local:
            sq = k.sb("sq", [P, 2, 512])
            ss = k.sb("ss", [P, 2 * H])
            nr = k.sb("nr", [P, 2 * H])
            rn = k.sb("rn", [P, 2 * H])
            qc = k.sb("qc", [P, 4, 512])
            qs = k.sb("qs", [P, 4, 512])
            qn = k.sb("qn", [P, 4, 512])
            rot = k.sb("rot", [P, 2, 256])

        pj = k.ps("pj", [P, 2, 512])
        pt = k.ps("pt", [P, 2, 512])
        pS = k.ps("pS", [P, 2, 512])
        pO = k.ps("pO", [P, 2, 512])

        x_in = k.sem("x_in")
        x_T = k.sem("x_T")
        x_s = k.sem("x_s")
        projected = k.sem("projected")
        squared = k.sem("squared")
        rotated = k.sem("rotated")
        added = k.sem("added")
        clamped = k.sem("clamped")
        rooted = k.sem("rooted")
        inverted = k.sem("inverted")
        q_normed = k.sem("q_normed")
        k_normed = k.sem("k_normed")
        rot_ready = k.sem("rot_ready")
        t_ps = k.sem("t_ps")
        t_sb = k.sem("t_sb")
        k_next = k.sem("k_next")
        scored = k.sem("scored")
        shifted = k.sem("shifted")
        exped = k.sem("exped")
        scaled = k.sem("scaled")
        p_T = k.sem("p_T")
        banded = k.sem("banded")
        v_ps = k.sem("v_ps")
        v_sb = k.sem("v_sb")
        o_ps = k.sem("o_ps")
        o_sb = k.sem("o_sb")
        y_ps = k.sem("y_ps")
        y_sb = k.sem("y_sb")
        zeroed = k.sem("zeroed")
        fetched = k.sem("fetched")
        block = ctx.enter_context(nc.Block())

        @block.sync
        def _(sp):
            fetch(sp, prefetch, fetched)

        def heads(ap):
            return ap.rearrange("p (r h w) -> p (r h) w", r=2, w=W)

        S4 = pS[:, :, 0:HP * W].rearrange("p r (h w) -> p r h w", w=W)
        if W == 64:
            S3 = pS[:, :, :].rearrange("p r (h w) -> p (r h) w", w=W)

        @block.tensor
        def _(pe):
            pe.wait_ge(zeroed, upto(0))

            def x_transpose(t, p):
                pe.wait_ge(x_in, upto(t))
                if isinstance(t, int) and t == 1:
                    pe.wait_ge(x_s, upto(0))
                pe.wait_ge(t_sb, upto(t - 2, 4, -1))
                nc.tensor.transpose(pt[:, 0, 0:P], xt[:, p % 2, :], const["ident"][:, :]).then_inc(x_T, 1)

            def qk_chunk(t, p, c):
                if c == 0:
                    pe.wait_ge(x_s, upto(t))
                before = (t, c - 2) if c >= 2 else (t - 1, c + 2)
                pe.wait_ge(squared, upto(before[0], 4, before[1] - 3))
                pe.wait_ge(rotated, upto(before[0], 4, before[1] - 3))
                nc.tensor.matmul(pj[:, c % 2, :], xs[:, p % 2, :], w["wqk"][:, c * 512:(c + 1) * 512],
                                 start=True, stop=True).then_inc(projected, 1)

            def qk_features(t, p, c):
                if c == 0:
                    pe.wait_ge(x_s, upto(t + 1 if has(t + 1, NT) else t))
                if c == 1:
                    pe.wait_ge(y_sb, upto(t - 2))
                if c >= 2:
                    pe.wait_ge(t_sb, upto(t, 4, c - 5))
                if local:
                    pe.wait_ge(q_normed if c < 2 else k_normed, upto(t, 2, c % 2 - 1))
                for i in range(4):
                    o = pt[:, c % 2, i * P:(i + 1) * P]
                    if local:
                        last = nc.tensor.transpose(o, qn[:, c, i * P:(i + 1) * P], const["ident"][:, :])
                    else:
                        col = (c * 4 + i) * P
                        last = nc.tensor.matmul(o, w["wqk"][:, col:col + P], xs[:, p % 2, :],
                                                start=True, stop=True)
                last.then_inc(t_ps, 1)

            def scores(t, p, r):
                if r == 0:
                    pe.wait_ge(t_sb, upto(t, 4))
                    if local:
                        pe.wait_ge(k_next, upto(t - 1))
                    pe.wait_ge(shifted, upto(t - 1))
                    if not local:
                        nc.tensor.matmul(pS[:, 0, 0:2], const["identb"][:, :], const["identb"][:, 0:2],
                                         start=True, stop=True, skip_group_check=True)
                if local:
                    nc.tensor.matmul(pS[:, r, :], const["identb"][:, :],
                                     w["mask"][:, ds(t, 1), :].broadcast_to([P, HP, 64]),
                                     start=True, stop=False, skip_group_check=True)
                for i in range(HP):
                    n = P // (32 if local else W)
                    m = P // n
                    for q in range(n):
                        lo = m * q if local else W32 + m * q
                        last = nc.tensor.matmul(
                            pS[m * q:m * (q + 1), r, i * W:(i + 1) * W],
                            qT[64 * r:64 * r + 64, i, m * q:m * (q + 1)],
                            kT[64 * r:64 * r + 64, p % 2, i, lo:lo + W],
                            start=not local, stop=True, skip_group_check=True)
                if r == 1:
                    last.then_inc(scored, 1)

            def attend(t, p):
                pe.wait_ge(banded, upto(t))
                pe.wait_ge(v_sb, upto(t + 1 if has(t + 1, NT) else t, 2))
                for i in range(HP):
                    for r in range(2):
                        o = pO[64 * r:64 * r + 64, i // 4, (i % 4) * P:(i % 4 + 1) * P]
                        h = r * HP + i
                        col = (2 * i + r) * HD
                        last = nc.tensor.matmul(o, v[:, p, col:col + HD], band[:, h, :],
                                                start=True, stop=not local)
                        if local:
                            last = nc.tensor.matmul(o[:, 0:W32], v[:, (p - 1) % 4, col:col + HD], edge[:, h, :],
                                                    start=False, stop=True)
                last.then_inc(o_ps, 1)

            def v_chunks(t, p):
                pe.wait_ge(x_s, upto(t))
                pe.wait_ge(o_sb, upto(t - 2))
                if isinstance(t, int) and t < 2:
                    pe.wait_ge(v_sb, upto(t - 1, 2))
                for c in range(2):
                    nc.tensor.matmul(pO[:, c, :], xs[:, p % 2, :], w["wv"][:, c * 512:(c + 1) * 512],
                                     start=True, stop=True).then_inc(v_ps, 1)

            def project(t):
                pe.wait_ge(o_sb, upto(t))
                if not has(t + 1, NT):
                    pe.wait_ge(y_sb, upto(t - 1))
                for i in range(HP):
                    last = nc.tensor.matmul(pt[:, 1, 0:D], oT[:, i, :], w["wo"][:, i, :],
                                            start=(i == 0), stop=(i == HP - 1))
                last.then_inc(y_ps, 1)

            def step(t, p):
                now, one, two = has(t, NT), has(t - 1, NT), has(t - 2, NT)
                if isinstance(t, int) and t == 0:
                    x_transpose(0, 0)
                    if local:
                        qk_chunk(0, 0, 0)
                        qk_chunk(0, 0, 1)
                if one:
                    for c in range(4):
                        qk_features(t - 1, p - 1, c)
                if local and now:
                    qk_chunk(t, p, 2)
                if has(t + 1, NT):
                    x_transpose(t + 1, p + 1)
                if one:
                    scores(t - 1, p - 1, 0)
                if local and now:
                    qk_chunk(t, p, 3)
                if one:
                    scores(t - 1, p - 1, 1)
                if two:
                    attend(t - 2, (p - 2) % 4)
                if local and has(t + 1, NT):
                    qk_chunk(t + 1, p + 1, 0)
                    qk_chunk(t + 1, p + 1, 1)
                if two:
                    project(t - 2)
                if now:
                    v_chunks(t, p)

            lagged(pe, NT, 4, 2, 2, step)

        @block.scalar
        def _(act):

            def x_copy(t, p):
                act.wait_ge(x_T, upto(t - 2))
                nc.scalar.copy(xt[:, p % 2, :], R[:, ds(t, 1), :].rearrange("p a f -> p (a f)")).then_inc(x_in, 1)

            def square(t, c):
                act.wait_ge(projected, upto(t, 4, c - 3))
                before = (t, c - 2) if c >= 2 else (t - 1, c + 2)
                act.wait_ge(rotated, upto(before[0], 4, before[1] - 3))
                nc.scalar.activation(sq[:, c % 2, :], pj[:, c % 2, :], ACT.Square).then_inc(squared, 1)

            def features(t, p, c):
                act.wait_ge(t_ps, upto(t, 4, c - 3))
                if c == 0:
                    act.wait_ge(scored, upto(t - 1))
                src = pt[:, c % 2, :].rearrange("p (a n) -> p a n", n=P)
                dst = (qT[:, 4 * c:4 * c + 4, :] if c < 2 else
                       kT[:, p % 2, 4 * (c - 2):4 * (c - 2) + 4, W32:])
                nc.scalar.copy(dst, src).then_inc(t_sb, 1)

            def exponentials(t):
                act.wait_ge(shifted, upto(t))
                act.wait_ge(scaled, upto(t - 1))
                nc.scalar.activation(pr[:, :], z[:, :], ACT.Exp, scale=SCALE).then_inc(exped, 1)

            def v_copies(t, p):
                for c in range(2):
                    act.wait_ge(v_ps, upto(t, 2, c - 1))
                    nc.scalar.copy(v[:, p % 4, c * 512:(c + 1) * 512], pO[:, c, :]).then_inc(v_sb, 1)

            def make_band(t, half):
                if half == 0:
                    act.wait_ge(p_T, upto(t))
                    act.wait_ge(o_ps, upto(t - 1))
                if kind == "w64":
                    moves = [(64 * a + 32 * kb, 64 * a + 32 * qb, kb) for a in range(2)
                             for kb in range(2) for qb in range(2)]
                elif kind == "w32":
                    moves = [(32 * a, 32 * a, 0) for a in range(4)]
                else:
                    moves = [(32 * a, 32 * a, 1) for a in range(4)] + [(32 * a - 32, 32 * a, 0) for a in range(4)]
                for kp, qp, kb in moves[4 * half:4 * half + 4]:
                    dst = (band[kp:kp + 32, :, qp:qp + 32] if kp >= 0 else edge[96:128, :, :])
                    last = nc.scalar.copy(dst, pT[qp:qp + 32, :, kb, :])
                if moves[4 * half + 4:] == []:
                    last.then_inc(banded, 1)

            def step(t, p):
                now, one, two = has(t, NT), has(t - 1, NT), has(t - 2, NT)
                if isinstance(t, int) and t == 0:
                    x_copy(0, 0)
                    x_copy(1, 1)
                    if local:
                        square(0, 0)
                        square(0, 1)
                if one:
                    for c in range(4):
                        features(t - 1, p - 1, c)
                if not local and one:
                    v_copies(t - 1, p - 1)
                if local and two:
                    make_band(t - 2, 0)
                if local and now:
                    square(t, 2)
                if two and W == 64:
                    make_band(t - 2, 1)
                if local and now:
                    square(t, 3)
                if has(t + 2, NT):
                    x_copy(t + 2, p)
                if local and now:
                    act.wait_ge(clamped, upto(t))
                    nc.scalar.activation(nr[:, :], ss[:, :], ACT.Sqrt).then_inc(rooted, 1)
                if not local and one:
                    exponentials(t - 1)
                if two:
                    act.wait_ge(o_ps, upto(t - 2))
                    act.wait_ge(y_ps, upto(t - 3))
                    nc.scalar.copy(oT[:, :, :].rearrange("p h q -> p (h q)"),
                                   pO[:, :, :].rearrange("p a b -> p (a b)")).then_inc(o_sb, 1)
                if local and one:
                    exponentials(t - 1)
                if local and one:
                    act.wait_ge(t_sb, upto(t - 1, 4))
                    nc.scalar.activation(kT[:, p % 2, :, 0:W32], kT[:, (p - 1) % 2, :, P:P + W32], ACT.Copy,
                                         scale=w["kfac"][:, 0:1]).then_inc(k_next, 1)
                if local and has(t + 1, NT):
                    square(t + 1, 0)
                    square(t + 1, 1)
                if local and now:
                    v_copies(t, p)
                if not local and one:
                    make_band(t - 1, 0)

            lagged(act, NT, 4, 2, 2, step)

        @block.vector
        def _(dve):
            nc.vector.memset(band[:, :, :], 0.0)
            if local:
                nc.vector.memset(edge[:, :, :], 0.0)
                nc.vector.memset(carry[:, :], 0.0)
                nc.vector.memset(kT[:, 0, :, 0:W32], 0.0)
                nc.vector.memset(v[:, 3, :], 0.0)
            dve.drain()
            nc.vector.memset(mx[:, :], 0.0).then_inc(zeroed, 1)

            def x_shift(t, p):
                p = p % 2
                dve.wait_ge(x_T, upto(t))
                if isinstance(t, int) and t < 2:
                    pass
                else:
                    dve.wait_ge(v_ps, upto(t - 2, 2))
                if not local:
                    nc.vector.tensor_copy(xs[:, p, :], pt[:, 0, 0:P]).then_inc(x_s, 1)
                    return
                nc.vector.tensor_tensor(out=xs[64:128, p, 0:1], in0=carry[64:128, 1 - p:2 - p],
                                        in1=w["inner"][64:128, ds(t, 1)], op=ALU.mult)
                nc.vector.tensor_copy(carry[64:128, p:p + 1], pt[64:128, 0, P - 1:P])
                nc.vector.tensor_copy(xs[0:64, p, :], pt[0:64, 0, 0:P])
                nc.vector.tensor_copy(xs[64:128, p, 1:P], pt[64:128, 0, 0:P - 1])
                dve.drain().then_inc(x_s, 1)

            def rotate(t, p, c):
                if c == 0:
                    dve.wait_ge(rot_ready, upto(t))
                dve.wait_ge(projected, upto(t, 4, c - 3))
                dve.wait_ge(squared, upto(t, 4, c - 3))
                dve.wait_ge(added, upto(t - 1, 4, c - 3))
                dve.wait_ge(q_normed if c < 2 else k_normed, upto(t - 1, 2, c % 2 - 1))
                src = pj[:, c % 2, :].rearrange("p (h d) -> p h d", d=HD)
                tab = rot[:, p % 2, 128 * (c // 2):128 * (c // 2) + 128]
                for d, o in ((qc, 0), (qs, HD)):
                    nc.vector.tensor_tensor(
                        out=d[:, c, :].rearrange("p (h d) -> p h d", d=HD), in0=src,
                        in1=tab[:, o:o + HD].unsqueeze(1).broadcast_to([P, 8, HD]), op=ALU.mult)
                nc.vector.tensor_reduce(ss[:, 8 * c:8 * c + 8], sq[:, c % 2, :].rearrange("p (h d) -> p h d", d=HD),
                                        AX.X, ALU.add).then_inc(rotated, 1)

            def add_y(t):
                dve.wait_ge(y_ps, upto(t))
                r2 = R[:, ds(t, 1), :].rearrange("p a f -> p (a f)")
                if "pb" in w:
                    nc.vector.tensor_tensor(out=r2, in0=r2, in1=w["pb"][:, :], op=ALU.add)
                    dve.drain()
                nc.vector.tensor_tensor(out=r2, in0=r2, in1=pt[:, 1, 0:D], op=ALU.add).then_inc(y_sb, 1)

            def step(t, p):
                now, one, two = has(t, NT), has(t - 1, NT), has(t - 2, NT)
                if isinstance(t, int) and t == 0:
                    x_shift(0, 0)
                if local and now:
                    for c in range(4):
                        rotate(t, p, c)
                    dve.drain()
                    nc.vector.tensor_scalar(ss[:, :], ss[:, :], 1e-24, None, ALU.max).then_inc(clamped, 1)
                if local and has(t + 1, NT):
                    x_shift(t + 1, p + 1)
                if one:
                    dve.wait_ge(scored, upto(t - 1))
                    if W == 64:
                        nc.vector.tensor_reduce(mx[:, :], S3, AX.X, ALU.max)
                    else:
                        nc.vector.tensor_reduce(mx[:, :].rearrange("p (r h) -> p r h", r=2), S4, AX.X, ALU.max)
                    dve.drain()
                    dve.wait_ge(exped, upto(t - 2))
                    if W == 64:
                        nc.vector.tensor_tensor(out=heads(z[:, :]), in0=S3, in1=bcast(mx[:, :], W),
                                                op=ALU.subtract).then_inc(shifted, 1)
                    else:
                        for r in range(2):
                            last = nc.vector.tensor_tensor(
                                out=z[:, r * HP * W:(r + 1) * HP * W].rearrange("p (h w) -> p h w", w=W),
                                in0=S4[:, r], in1=bcast(mx[:, r * HP:(r + 1) * HP], W), op=ALU.subtract)
                        last.then_inc(shifted, 1)
                if not local and has(t + 1, NT):
                    x_shift(t + 1, p + 1)
                if local and now:
                    dve.wait_ge(rooted, upto(t))
                    nc.vector.reciprocal(rn[:, :], nr[:, :]).then_inc(inverted, 1)
                    dve.drain()
                    dve.wait_ge(t_ps, upto(t - 1, 4))
                    for c in range(2):
                        dve.wait_ge(added, upto(t, 4, c - 3))
                        nc.vector.tensor_tensor(
                            out=qn[:, c, :].rearrange("p (h d) -> p h d", d=HD),
                            in0=qc[:, c, :].rearrange("p (h d) -> p h d", d=HD),
                            in1=bcast(rn[:, 8 * c:8 * c + 8], HD), op=ALU.mult).then_inc(q_normed, 1)
                if one:
                    dve.wait_ge(exped, upto(t - 1))
                    nc.vector.tensor_reduce(sm[:, :], heads(pr[:, :]), AX.X, ALU.add)
                    dve.drain()
                    nc.vector.reciprocal(rs[:, :], sm[:, :])
                    dve.drain()
                    nc.vector.tensor_tensor(out=heads(pn[:, :]), in0=heads(pr[:, :]), in1=bcast(rs[:, :], W),
                                            op=ALU.mult).then_inc(scaled, 1)
                    if local and two:
                        add_y(t - 2)
                    dve.drain()
                    if not local:
                        nc.vector.tensor_tensor(out=heads(pn[:, :]), in0=heads(pn[:, :]),
                                                in1=w["own"][:, 0:W].unsqueeze(1).broadcast_to([P, H, W]),
                                                op=ALU.subtract)
                        dve.drain()
                    dve.wait_ge(banded, upto(t - 2))
                    nc.vector.transpose(pT[:, :, :, :].rearrange("p h a b -> p (h a b)"), pn[:, :]).then_inc(p_T, 1)
                if two and not (local and one):
                    add_y(t - 2)

            lagged(dve, NT, 4, 2, 2, step)

        if local:
            @block.gpsimd
            def _(pool):

                def tables(t, p):
                    pool.wait_ge(rotated, upto(t - 2, 4))
                    nc.gpsimd.tensor_tensor(out=rot[:, p % 2, :], in0=w["rot"][:, ds(t, 1), :].rearrange("p a f -> p (a f)"),
                                            in1=w["qk_scale"][:, :], op=ALU.mult).then_inc(rot_ready, 1)

                def step(t, p):
                    if isinstance(t, int) and t == 0:
                        tables(0, 0)
                    if has(t + 1, NT):
                        tables(t + 1, p + 1)
                    if not has(t, NT):
                        return
                    for c in range(4):
                        pool.wait_ge(rotated, upto(t, 4, c - 3))
                        a = qc[:, c, :].rearrange("p (h e d) -> p h e d", e=2, d=32)
                        b = qs[:, c, :].rearrange("p (h e d) -> p h e d", e=2, d=32)
                        for e in range(2):
                            last = nc.gpsimd.tensor_tensor(out=a[:, :, e, :], in0=a[:, :, e, :],
                                                           in1=b[:, :, 1 - e, :], op=ALU.add)
                        last.then_inc(added, 1)
                    pool.wait_ge(added, upto(t, 4))
                    pool.wait_ge(inverted, upto(t))
                    pool.wait_ge(t_ps, upto(t - 1, 4))
                    for c in range(2, 4):
                        nc.gpsimd.tensor_tensor(
                            out=qn[:, c, :].rearrange("p (h d) -> p h d", d=HD),
                            in0=qc[:, c, :].rearrange("p (h d) -> p h d", d=HD),
                            in1=bcast(rn[:, 8 * c:8 * c + 8], HD), op=ALU.mult).then_inc(k_normed, 1)

                lagged(pool, NT, 4, 2, 2, step)


def moments(nc, dve, st, mv, src):
    for i in range(CH):
        nc.vector.bn_stats(st[:, i, :], src[:, i, :])
    dve.drain()
    for i in range(CH):
        last = nc.vector.bn_aggr(mv[:, i, :], st[:, i, :])
    return last


def normalise(nc, dve, out, src, mv, sd, rs):
    nc.vector.reciprocal(rs[:, :], sd[:, :])
    dve.drain()
    for i in range(CH):
        last = nc.vector.tensor_scalar(out[:, i, :], src[:, i, :], mv[:, i, 0:1], rs[:, i:i + 1],
                                       ALU.subtract, ALU.mult)
    return last


def gated_pass(nc, tag, R, w, const, prefetch=()):
    with ExitStack() as ctx:
        k = Kit(nc, ctx, tag)
        xt = k.sb("xt", [P, 2, CH, D])
        xs = k.sb("xs", [P, CW])
        carry = k.sb("carry", [P, 2])
        st = k.sb("st", [P, CH, 6])
        mv = k.sb("mv", [P, CH, 2])
        sd = k.sb("sd", [P, CH])
        rs = k.sb("rs", [P, CH])
        xn = k.sb("xn", [P, CH, D])
        xnT = k.sb("xnT", [P, 2, CW])
        gl = k.sb("gl", [P, 2, CW])
        hT = k.sb("hT", [P, NJ2, CW])
        pa = k.ps("pa", [P, CW])
        pb = k.ps("pb", [P, CW])
        pg = k.ps("pg", [P, 2, CW])
        ph = k.ps("ph", [P, 2, CW])
        py = k.ps("py", [P, CW])
        x_in, x_T, x_s = k.sem("x_in"), k.sem("x_T"), k.sem("x_s")
        s_ps = k.sem("s_ps")
        momented, rooted = k.sem("momented"), k.sem("rooted")
        n_sb, n_ps, n_T = k.sem("n_sb"), k.sem("n_ps"), k.sem("n_T")
        gate_ps, gate_sb = k.sem("gate_ps"), k.sem("gate_sb")
        a_ps, h_sb = k.sem("a_ps"), k.sem("h_sb")
        y_ps, y_sb = k.sem("y_ps"), k.sem("y_sb")
        ready = k.sem("ready")
        fetched = k.sem("fetched")
        block = ctx.enter_context(nc.Block())

        @block.sync
        def _(sp):
            fetch(sp, prefetch, fetched)

        def fm(ap):
            return ap.rearrange("p (a n) -> p a n", n=P)

        @block.tensor
        def _(pe):
            pe.wait_ge(ready, 1)

            def hidden(c, p, j):
                m = JW2[j]
                pe.wait_ge(n_T, upto(c))
                pe.wait_ge(gate_sb, upto(c, NJ2, j - 2 - NJ2 + 1)) if not isinstance(c, int) or NJ2 * c + j >= 2 else None
                nc.tensor.matmul(pg[0:m, (NJ2 * p + j) % 2, :], w["w1"][:, F2 + 128 * j:F2 + 128 * j + m],
                                 xnT[:, p, :], start=True, stop=True).then_inc(gate_ps, 1)
                pe.wait_ge(h_sb, upto(c, NJ2, j - 2 - NJ2 + 1)) if not isinstance(c, int) or NJ2 * c + j >= 2 else None
                nc.tensor.matmul(ph[0:m, (NJ2 * p + j) % 2, :], w["w1"][:, 128 * j:128 * j + m],
                                 xnT[:, p, :], start=True, stop=True).then_inc(a_ps, 1)

            def step(c, p):
                now, one = has(c, NC), has(c - 1, NC)
                if now:
                    pe.wait_ge(x_in, upto(c))
                    pe.wait_ge(n_T, upto(c - 1))
                    for i in range(CH):
                        last = nc.tensor.transpose(pa[:, i * P:(i + 1) * P], xt[:, p, i, :], const["ident"][:, :])
                    last.then_inc(x_T, 1)
                if one:
                    hidden(c - 1, 1 - p, 0)
                if now:
                    pe.wait_ge(x_s, upto(c))
                    pe.wait_ge(n_sb, upto(c - 1))
                    for i in range(CH):
                        last = nc.tensor.transpose(pb[:, i * P:(i + 1) * P], xs[:, i * P:(i + 1) * P], const["ident"][:, :])
                    last.then_inc(s_ps, 1)
                if one:
                    hidden(c - 1, 1 - p, 1)
                    hidden(c - 1, 1 - p, 2)
                    pe.wait_ge(h_sb, upto(c - 1, NJ2))
                    pe.wait_ge(y_sb, upto(c - 2))
                    for i in range(CH):
                        for j in range(NJ2):
                            m = P if j < NJ2 - 1 else ONE_ROW + 1
                            last = nc.tensor.matmul(py[:, i * P:(i + 1) * P], hT[0:m, j, i * P:(i + 1) * P],
                                                    w["w2"][0:m, j, :], start=(j == 0), stop=(j == NJ2 - 1))
                    last.then_inc(y_ps, 1)
                if now:
                    pe.wait_ge(n_sb, upto(c))
                    for i in range(CH):
                        last = nc.tensor.transpose(pa[:, i * P:(i + 1) * P], xn[:, i, :], const["ident"][:, :])
                    last.then_inc(n_ps, 1)

            lagged(pe, NC, 2, 1, 1, step)

        @block.scalar
        def _(act):

            def x_copy(c, p):
                act.wait_ge(x_T, upto(c - 2))
                nc.scalar.copy(xt[:, p, :, :], R[:, ds(c * CH, CH), :]).then_inc(x_in, 1)

            def step(c, p):
                now, one = has(c, NC), has(c - 1, NC)
                if isinstance(c, int) and c == 0:
                    x_copy(0, 0)
                if has(c + 1, NC):
                    x_copy(c + 1, 1 - p)
                if one:
                    for j in range(NJ2):
                        m = JW2[j]
                        act.wait_ge(gate_ps, upto(c - 1, NJ2, j - NJ2 + 1))
                        if not isinstance(c, int) or NJ2 * (c - 1) + j >= 2:
                            act.wait_ge(h_sb, upto(c - 1, NJ2, j - 2 - NJ2 + 1))
                        nc.scalar.activation(gl[0:m, (NJ2 * (1 - p) + j) % 2, :], pg[0:m, (NJ2 * (1 - p) + j) % 2, :],
                                             ACT.Gelu, bias=w["b1g"][0:m, j:j + 1]).then_inc(gate_sb, 1)
                if now:
                    act.wait_ge(momented, upto(c))
                    nc.scalar.activation(sd[:, :], mv[:, :, 1], ACT.Sqrt, bias=const["eps"][:, 0:1]).then_inc(rooted, 1)
                    act.wait_ge(n_ps, upto(c))
                    act.wait_ge(a_ps, upto(c - 2, NJ2))
                    nc.scalar.activation(xnT[:, p, :], pa[:, :], ACT.Identity, scale=w["g"][:, 0:1],
                                         bias=w["b"][:, 0:1]).then_inc(n_T, 1)

            lagged(act, NC, 2, 1, 1, step)

        @block.vector
        def _(dve):
            nc.vector.memset(carry[:, :], 0.0)
            nc.vector.memset(hT[64:128, NJ2 - 1, :], 0.0)
            dve.drain()
            nc.vector.memset(hT[ONE_ROW:ONE_ROW + 1, NJ2 - 1, :], 1.0).then_inc(ready, 1)
            dve.drain()

            def step(c, p):
                now, one = has(c, NC), has(c - 1, NC)
                if now:
                    dve.wait_ge(x_T, upto(c))
                    dve.wait_ge(s_ps, upto(c - 1))
                    nc.vector.tensor_tensor(out=xs[64:128, 0:1], in0=carry[64:128, 1 - p:2 - p],
                                            in1=w["inner"][64:128, ds(c * CH, 1)], op=ALU.mult)
                    nc.vector.tensor_copy(carry[64:128, p:p + 1], pa[64:128, CW - 1:CW])
                    nc.vector.tensor_copy(xs[0:64, :], pa[0:64, :])
                    nc.vector.tensor_copy(xs[64:128, 1:CW], pa[64:128, 0:CW - 1])
                    dve.drain().then_inc(x_s, 1)
                    dve.wait_ge(s_ps, upto(c))
                    moments(nc, dve, st, mv, fm(pb[:, :])).then_inc(momented, 1)
                if one:
                    for j in range(NJ2):
                        m = JW2[j]
                        dve.wait_ge(gate_sb, upto(c - 1, NJ2, j - NJ2 + 1))
                        dve.wait_ge(a_ps, upto(c - 1, NJ2, j - NJ2 + 1))
                        dve.wait_ge(y_ps, upto(c - 2))
                        b = (NJ2 * (1 - p) + j) % 2
                        nc.vector.scalar_tensor_tensor(out=hT[0:m, j, :], in0=ph[0:m, b, :],
                                                       scalar=w["b1a"][0:m, j:j + 1], in1=gl[0:m, b, :],
                                                       op0=ALU.add, op1=ALU.mult).then_inc(h_sb, 1)
                if now:
                    dve.wait_ge(rooted, upto(c))
                    dve.wait_ge(n_ps, upto(c - 1))
                    normalise(nc, dve, xn, fm(pb[:, :]), mv, sd, rs).then_inc(n_sb, 1)
                if one:
                    dve.wait_ge(y_ps, upto(c - 1))
                    dve.wait_ge(x_T, upto(c - 1))
                    r4 = R[:, ds((c - 1) * CH, CH), :]
                    nc.vector.tensor_tensor(out=r4, in0=r4, in1=fm(py[:, :]), op=ALU.add).then_inc(y_sb, 1)

            lagged(dve, NC, 2, 1, 1, step)


def relu_pass(nc, tag, R, w, const, prefetch=()):
    NJ = F1 // P
    with ExitStack() as ctx:
        k = Kit(nc, ctx, tag)
        st = k.sb("st", [P, 2, CH, 6])
        mv = k.sb("mv", [P, 2, CH, 2])
        sd = k.sb("sd", [P, 2, CH])
        rs = k.sb("rs", [P, 2, CH])
        xn = k.sb("xn", [P, CH, D])
        x1 = k.sb("x1", [P, 2, CH, D])
        x1T = k.sb("x1T", [P, 2, CW])
        hT = k.sb("hT", [P, NJ, CW])
        r2 = k.sb("r2", [P, CH, D])
        yn = k.sb("yn", [P, CH, D])
        pa = k.ps("pa", [P, CW])
        ph = k.ps("ph", [P, NJ, CW])
        py = k.ps("py", [P, CW])
        momented, rooted, n_sb = k.sem("momented"), k.sem("rooted"), k.sem("n_sb")
        gained, x1_sb, x_ps, x_T = k.sem("gained"), k.sem("x1_sb"), k.sem("x_ps"), k.sem("x_T")
        h_ps, h_sb, y_ps = k.sem("h_ps"), k.sem("h_sb"), k.sem("y_ps")
        y_in = k.sem("y_in")
        momented2, rooted2, n2_sb = k.sem("momented2"), k.sem("rooted2"), k.sem("n2_sb")
        gained2 = k.sem("gained2")
        fetched = k.sem("fetched")
        block = ctx.enter_context(nc.Block())

        @block.sync
        def _(sp):
            fetch(sp, prefetch, fetched)

        def fm(ap):
            return ap.rearrange("p (a n) -> p a n", n=P)

        def wide(ap):
            return ap.unsqueeze(1).broadcast_to([P, CH, D])

        @block.tensor
        def _(pe):

            def step(c, p):
                if has(c - 1, NC):
                    pe.wait_ge(x_T, upto(c - 1))
                    for j in range(NJ):
                        pe.wait_ge(h_sb, upto(c - 2, NJ, j - NJ + 1))
                        nc.tensor.matmul(ph[:, j, :], w["w1"][:, j * P:(j + 1) * P], x1T[:, 1 - p, :],
                                         start=True, stop=True).then_inc(h_ps, 1)
                    pe.wait_ge(h_sb, upto(c - 1, NJ))
                    pe.wait_ge(y_in, upto(c - 2))
                    for i in range(CH):
                        for j in range(NJ):
                            last = nc.tensor.matmul(py[:, i * P:(i + 1) * P], hT[:, j, i * P:(i + 1) * P],
                                                    w["w2"][:, j, :], start=(j == 0), stop=(j == NJ - 1))
                    last.then_inc(y_ps, 1)
                if has(c, NC):
                    pe.wait_ge(x1_sb, upto(c))
                    pe.wait_ge(x_T, upto(c - 1))
                    for i in range(CH):
                        last = nc.tensor.transpose(pa[:, i * P:(i + 1) * P], x1[:, p, i, :], const["ident"][:, :])
                    last.then_inc(x_ps, 1)

            lagged(pe, NC, 2, 1, 1, step)

        @block.scalar
        def _(act):

            def step(c, p):
                if has(c, NC):
                    act.wait_ge(momented, upto(c))
                    nc.scalar.activation(sd[:, 0, :], mv[:, 0, :, 1], ACT.Sqrt, bias=const["eps"][:, 0:1]).then_inc(rooted, 1)
                if has(c - 1, NC):
                    act.wait_ge(y_ps, upto(c - 2))
                    for j in range(NJ):
                        act.wait_ge(h_ps, upto(c - 1, NJ, j - NJ + 1))
                        nc.scalar.activation(hT[:, j, :], ph[:, j, :], ACT.Relu, bias=w["b1"][:, j:j + 1]).then_inc(h_sb, 1)
                    act.wait_ge(momented2, upto(c - 1))
                    nc.scalar.activation(sd[:, 1, :], mv[:, 1, :, 1], ACT.Sqrt, bias=const["eps"][:, 0:1]).then_inc(rooted2, 1)
                if has(c, NC):
                    act.wait_ge(x_ps, upto(c))
                    act.wait_ge(h_ps, upto(c - 2, NJ))
                    nc.scalar.copy(x1T[:, p, :], pa[:, :]).then_inc(x_T, 1)

            lagged(act, NC, 2, 1, 1, step)

        @block.vector
        def _(dve):

            def step(c, p):
                if has(c, NC):
                    moments(nc, dve, st[:, 0], mv[:, 0], R[:, ds(c * CH, CH), :]).then_inc(momented, 1)
                    dve.wait_ge(rooted, upto(c))
                    dve.wait_ge(gained, upto(c - 1))
                    normalise(nc, dve, xn, R[:, ds(c * CH, CH), :], mv[:, 0], sd[:, 0], rs[:, 0]).then_inc(n_sb, 1)
                if has(c - 1, NC):
                    dve.wait_ge(y_ps, upto(c - 1))
                    nc.vector.tensor_tensor(out=r2[:, :, :], in0=fm(py[:, :]), in1=x1[:, 1 - p, :, :],
                                            op=ALU.add).then_inc(y_in, 1)
                    dve.drain()
                    nc.vector.tensor_tensor(out=r2[:, :, :], in0=r2[:, :, :], in1=wide(w["b2"][:, :]), op=ALU.add)
                    dve.drain()
                    moments(nc, dve, st[:, 1], mv[:, 1], r2).then_inc(momented2, 1)
                    dve.wait_ge(rooted2, upto(c - 1))
                    dve.wait_ge(gained2, upto(c - 2))
                    normalise(nc, dve, yn, r2, mv[:, 1], sd[:, 1], rs[:, 1]).then_inc(n2_sb, 1)
                    dve.drain()

            lagged(dve, NC, 2, 1, 1, step)

        @block.gpsimd
        def _(pool):

            def step(c, p):
                if has(c, NC):
                    pool.wait_ge(n_sb, upto(c))
                    pool.wait_ge(y_in, upto(c - 2))
                    nc.gpsimd.tensor_tensor(out=x1[:, p, :, :], in0=xn[:, :, :], in1=wide(w["g1"][:, :]),
                                            op=ALU.mult).then_inc(gained, 1)
                    pool.drain()
                    nc.gpsimd.tensor_tensor(out=x1[:, p, :, :], in0=x1[:, p, :, :], in1=wide(w["o1"][:, :]),
                                            op=ALU.add).then_inc(x1_sb, 1)
                if has(c - 1, NC):
                    pool.wait_ge(n2_sb, upto(c - 1))
                    r4 = R[:, ds((c - 1) * CH, CH), :]
                    nc.gpsimd.tensor_tensor(out=r4, in0=yn[:, :, :], in1=wide(w["g2"][:, :]),
                                            op=ALU.mult).then_inc(gained2, 1)
                    pool.drain()
                    nc.gpsimd.tensor_tensor(out=r4, in0=r4, in1=wide(w["o2"][:, :]), op=ALU.add)
                    pool.drain()

            lagged(pool, NC, 2, 1, 1, step)


def split_qkv_pass(nc, R, Vc, scratch, w, const):
    with ExitStack() as ctx:
        k = Kit(nc, ctx, "sp_")
        st, mv = k.sb("st", [P, CH, 6]), k.sb("mv", [P, CH, 2])
        sd, rs = k.sb("sd", [P, CH]), k.sb("rs", [P, CH])
        xn = k.sb("xn", [P, CH, D])
        xnT = k.sb("xnT", [P, CW])
        rest = k.sb("rest", [P, 2, CW])
        parts = k.sb("parts", [P, 2, 2, NPART, CW], BF16)
        pa = k.ps("pa", [P, CW])
        pqk = k.ps("pqk", [P, 2, CW])
        pv = k.ps("pv", [P, CW])
        momented, rooted, n_sb, n_ps, n_T = (k.sem(n) for n in ("momented", "rooted", "n_sb", "n_ps", "n_T"))
        qk_ps, high, split = k.sem("qk_ps"), k.sem("high"), k.sem("split")
        v_ps, v_sb, ones = k.sem("v_ps"), k.sem("v_sb"), k.sem("ones")
        written = [k.sem(f"written{p}") for p in range(2)]
        NW = 16
        block = ctx.enter_context(nc.Block())
        CPB = NC // BATCH

        @block.tensor
        def _(pe):

            def step(c, p):
                pe.wait_ge(n_sb, upto(c))
                pe.wait_ge(n_T, upto(c - 1))
                for i in range(CH):
                    last = nc.tensor.transpose(pa[:, i * P:(i + 1) * P], xn[:, i, :], const["ident"][:, :])
                last.then_inc(n_ps, 1)
                pe.wait_ge(n_T, upto(c))
                pe.wait_ge(split, upto(c - 1))
                for i in range(2):
                    last = nc.tensor.matmul(pqk[:, i, :], w["qkv"][:, i * D:(i + 1) * D], xnT[:, :],
                                            start=True, stop=True)
                last.then_inc(qk_ps, 1)
                pe.wait_ge(v_sb, upto(c - 1))
                for i in range(CH):
                    last = nc.tensor.matmul(pv[:, i * P:(i + 1) * P], xnT[:, i * P:(i + 1) * P],
                                            w["qkv"][:, 2 * D:3 * D], start=True, stop=True)
                last.then_inc(v_ps, 1)

            for c in range(2):
                step(c, c)
            with pe.Fori(1, NC // 2) as r:
                for p in range(2):
                    step(r * 2 + p, p)

        @block.scalar
        def _(act):
            act.wait_ge(ones, 1)

            def step(c, p, b, cb, before):
                act.wait_ge(momented, upto(c))
                nc.scalar.activation(sd[:, :], mv[:, :, 1], ACT.Sqrt, bias=const["eps"][:, 0:1]).then_inc(rooted, 1)
                act.wait_ge(n_ps, upto(c))
                act.wait_ge(v_ps, upto(c - 1))
                nc.scalar.copy(xnT[:, :], pa[:, :]).then_inc(n_T, 1)
                act.wait_ge(qk_ps, upto(c))
                act.wait_ge(written[p], upto(before - 1, NW))
                nc.scalar.copy(parts[:, p, :, 0, :], pqk[:, :, :]).then_inc(high, 1)
                act.wait_ge(v_ps, upto(c))
                for i in range(CH):
                    dst = Vc[:, ds(b * NG0, NG0), ds(cb * CH + i, 1), :, 0:HD0].rearrange("p g a j d -> p g (a j) d")
                    last = nc.scalar.copy(dst, pv[:, i * P:(i + 1) * P].rearrange("p (g j d) -> p g j d", g=NG0, j=HPG))
                last.then_inc(v_sb, 1)

            for c in range(2):
                step(c, c, 0, c, 0)
            for b in range(BATCH):
                first = 1 if b == 0 else 0
                with act.Fori(first, CPB // 2) as r:
                    for p in range(2):
                        step(r * 2 + (p + b * CPB), p, b, r * 2 + p, r + b * CPB // 2)

        @block.vector
        def _(dve):
            nc.vector.memset(Vc[:, :, :, :, :], 1.0).then_inc(ones, 1)

            def step(c, p):
                src = R[:, ds(c * CH, CH), :]
                moments(nc, dve, st, mv, src).then_inc(momented, 1)
                dve.wait_ge(rooted, upto(c))
                dve.wait_ge(n_ps, upto(c - 1))
                normalise(nc, dve, xn, src, mv, sd, rs).then_inc(n_sb, 1)
                dve.wait_ge(high, upto(c))
                nc.vector.tensor_tensor(out=rest[:, :, :], in0=pqk[:, :, :], in1=parts[:, p, :, 0, :], op=ALU.subtract)
                dve.drain()
                nc.vector.tensor_copy(parts[:, p, :, 1, :], rest[:, :, :])
                dve.drain()
                nc.vector.tensor_tensor(out=rest[:, :, :], in0=rest[:, :, :], in1=parts[:, p, :, 1, :], op=ALU.subtract)
                dve.drain()
                nc.vector.tensor_copy(parts[:, p, :, 2, :], rest[:, :, :]).then_inc(split, 1)
                dve.drain()

            for c in range(2):
                step(c, c)
            with dve.Fori(1, NC // 2) as r:
                for p in range(2):
                    step(r * 2 + p, p)

        @block.sync
        def _(sp):
            for b in range(BATCH):
                with sp.Fori(0, CPB // 2) as r:
                    for p in range(2):
                        cb = r * 2 + p
                        sp.wait_ge(split, upto(cb + b * CPB))
                        sp.dma_start(scratch[:, :, b * P:(b + 1) * P, ds(cb * CW, CW)].rearrange("i a p t -> p i a t"),
                                     parts[:, p, :, :, :]).then_inc(written[p], 16)
            for p in range(2):
                sp.wait_ge(written[p], NC // 2 * NW)


def full_attention_pass(nc, Vc, AO, scratch, const):
    KT = NTB
    NQ = SEQ // QC
    NQT = QC // P
    NKB = SEQ // 512
    NGRP = BATCH * NG0
    with ExitStack() as ctx:
        k = Kit(nc, ctx, "fa_")
        qst = k.sb("qst", [P, 2, HPG, SEQ], BF16)
        kst = k.sb("kst", [P, 2, HPG, SEQ], BF16)
        vst = k.sb("vst", [P, 2, KT, HPG, 32])
        pe_ = k.sb("pexp", [P, 2, HPG, QC])
        mxb = k.sb("mxb", [P, HPG, NQT, NKB])
        mx = k.sb("mx", [P, NQT, HPG])
        mr = k.sb("mr", [P, NQT, HPG])
        mpart = k.sb("mpart", [P, NQT, HPG, NPART], BF16)
        oS = k.sb("oS", [P, QC])
        rs = k.sb("rs", [P, NQT * HPG])
        pM = k.ps("pM", [P, 3, 512])
        pS = k.ps("pS", [P, 4, 512])
        pO = k.ps("pO", [P, 512])
        NDMA = 2 * NPART * HPG
        stacks = [k.sem(f"stacks{p}") for p in range(2)]
        v_in = k.sem("v_in")
        cleared_q, cleared_k = k.sem("cleared_q"), k.sem("cleared_k")
        max_ps = k.sem("max_ps")
        max_sb = k.sem("max_sb")
        m_split = k.sem("m_split")
        m_ps = k.sem("m_ps")
        m_row = k.sem("m_row")
        s_ps = k.sem("s_ps")
        e_sb = k.sem("e_sb")
        pv_done = k.sem("pv_done")
        o_sb = k.sem("o_sb")
        o_tp = k.sem("o_tp")
        o_out = k.sem("o_out")
        block = ctx.enter_context(nc.Block())
        K3 = MROW + NPART
        NU = KT * NKB
        UPK = 5
        turn = [("unit", u) for u in range(4 * UPK)] + [("output", 0)] + \
               [("unit", u) for u in range(4 * UPK, NU)] + [("row", qt) for qt in range(NQT)]
        assert len(turn) % 3 == 0
        bank = {use: i % 3 for i, use in enumerate(turn)}

        @block.sync
        def _(sp):
            def load(gi, par):
                for j in range(HPG):
                    q, kk = (scratch[i, :, ds(gi * (HPG * HD0) + j * HD0, HD0), :] for i in range(2))
                    for a in range(NPART):
                        rows = slice(a * NPART * HD0, (a + 1) * NPART * HD0)
                        sp.dma_start(qst[rows, par, j, :],
                                     q[a:a + 1].broadcast_to([NPART, HD0, SEQ])).then_inc(stacks[par], 16)
                        sp.dma_start(kst[rows, par, j, :], kk).then_inc(stacks[par], 16)

            sp.wait_ge(cleared_k, 1)
            sp.wait_ge(cleared_q, 1)
            load(0, 0)
            sp.wait_ge(cleared_k, 2)
            sp.wait_ge(cleared_q, 2)
            load(1, 1)
            with sp.Fori(1, NGRP // 2) as r:
                for par in range(2):
                    sp.wait_ge(o_out, (r * 2 + (par - 1)) * NQ)
                    load(r * 2 + par, par)

        @block.gpsimd
        def _(pool):
            def take(gi, par):
                src = Vc[:, ds(gi, 1), :, :, :].rearrange("p g t j d -> p (g t) j d")
                nc.gpsimd.tensor_copy(vst[:, par, :, :, 0:HD0 + 1], src).then_inc(v_in, 1)

            for par in range(2):
                nc.gpsimd.memset(qst[:, par, :, :], 0.0).then_inc(cleared_q, 1)
                pool.drain()
            nc.gpsimd.memset(vst[:, :, :, :, :], 0.0)
            pool.drain()
            take(0, 0)
            take(1, 1)
            with pool.Fori(1, NGRP // 2) as r:
                for par in range(2):
                    pool.wait_ge(o_out, (r * 2 + (par - 1)) * NQ)
                    take(r * 2 + par, par)

        @block.tensor
        def _(pe):
            def bank_free(use, n, first=False):
                i = turn.index(use)
                kind, j = turn[i - 3]
                if i < 3:
                    if not isinstance(n, int) or n >= 1:
                        pe.wait_ge(m_row, n * NQT + (j + 1 - NQT))
                elif kind == "unit":
                    pe.wait_ge(max_sb, n * NU + (j + 1))
                elif kind == "row":
                    pe.wait_ge(m_row, n * NQT + (j + 1))
                elif not first:
                    pe.wait_ge(o_out, n + -1)

            def max_bank(par, qc, n, u, first=False):
                j, qt, kb = u // (NQT * NKB), u // NKB % NQT, u % NKB
                bank_free(("unit", u), n, first)
                nc.tensor.matmul(pM[:, bank["unit", u], :], qst[0:KST, par, j, ds(qc * QC + qt * P, P)],
                                 kst[0:KST, par, j, kb * 512:(kb + 1) * 512],
                                 start=True, stop=True).then_inc(max_ps, 1)

            def max_row(n, qt):
                if qt == 0:
                    pe.wait_ge(m_split, n + 1)
                bank_free(("row", qt), n)
                for j in range(HPG):
                    last = nc.tensor.matmul(pM[MROW:MROW + NPART, bank["row", qt], j * P:(j + 1) * P],
                                            mpart[:, qt, j, :], const["identb"][:, :], start=True, stop=True)
                last.then_inc(m_ps, 1)

            def scores(par, qc, n, kt, hp):
                if kt == 0 and hp == 0:
                    pe.wait_ge(m_row, (n + 1) * NQT)
                if not isinstance(n, int) or n * KT + kt >= 1:
                    pe.wait_ge(e_sb, (n * KT + kt) * 2 + (hp - 1))
                for j in (2 * hp, 2 * hp + 1):
                    last = nc.tensor.matmul(pS[:, j, :], kst[0:K3, par, j, kt * P:(kt + 1) * P],
                                            qst[0:K3, par, j, ds(qc * QC, QC)], start=True, stop=True)
                last.then_inc(s_ps, 1)

            def times_v(par, gi, n, kt, hp):
                if kt == 0 and hp == 0:
                    pe.wait_ge(v_in, gi + 1)
                    if not isinstance(n, int) or n >= 1:
                        pe.wait_ge(o_sb, n)
                pe.wait_ge(e_sb, (n * KT + kt) * 2 + (hp + 1))
                for j in (2 * hp, 2 * hp + 1):
                    last = nc.tensor.matmul(pO[32 * j:32 * j + 32, :], vst[:, par, kt, j, :], pe_[:, kt % 2, j, :],
                                            start=(kt == 0), stop=(kt == KT - 1))
                if hp == 1:
                    last.then_inc(pv_done, 1)

            def turn_output(n, lead):
                pe.wait_ge(o_sb, n + 1)
                if lead:
                    bank_free(("output", 0), n + 2)
                elif not isinstance(n, int) or n >= 1:
                    pe.wait_ge(o_out, n)
                for qt in range(NQT):
                    last = nc.tensor.transpose(pM[:, bank["output", 0], qt * P:(qt + 1) * P], oS[:, qt * P:(qt + 1) * P],
                                               const["ident"][:, :])
                last.then_inc(o_tp, 1)

            def step(gi, par, qc, n, ahead, before):
                for kt in range(KT):
                    units = list(range(UPK * kt, min(UPK * (kt + 1), NU))) if ahead else []
                    rows = {KT - 2: [0, 1], KT - 1: [2, 3]}.get(kt, []) if ahead else []

                    def unit():
                        if units:
                            max_bank(ahead[0], ahead[1], n + 1, units.pop(0), not before)

                    for hp in range(2):
                        scores(par, qc, n, kt, hp)
                        unit()
                    for qt in rows:
                        max_row(n + 1, qt)
                    unit()
                    for hp in range(2):
                        if kt:
                            times_v(par, gi, n, kt - 1, hp)
                        elif before:
                            times_v(before[0], before[1], n + -1, KT - 1, hp)
                    unit()
                    unit()
                    if kt == 3 and before:
                        turn_output(n + -1, ahead is not None)

            pe.wait_ge(stacks[0], 16 * NDMA)
            for u in range(NU):
                max_bank(0, 0, 0, u, True)
            for qt in range(NQT):
                max_row(0, qt)

            def group(gi, par, later, arrived):
                step(gi, par, 0, gi * NQ, (par, 1), (1 - par, gi + -1) if later else None)
                with pe.Fori(1, NQ - 1) as qc:
                    step(gi, par, qc, qc + gi * NQ, (par, qc + 1), (par, gi))
                if arrived is not None:
                    pe.wait_ge(stacks[1 - par], arrived)
                step(gi, par, NQ - 1, gi * NQ + (NQ - 1), None if arrived is None else (1 - par, 0), (par, gi))

            group(0, 0, False, 16 * NDMA)
            with pe.Fori(0, NGRP // 2 - 1) as r:
                group(r * 2 + 1, 1, True, (r + 2) * (16 * NDMA))
                group(r * 2 + 2, 0, True, (r + 2) * (16 * NDMA))
            group(NGRP - 1, 1, True, None)
            for hp in range(2):
                times_v(1, NGRP - 1, NGRP * NQ - 1, KT - 1, hp)
            turn_output(NGRP * NQ - 1, False)

        @block.scalar
        def _(act):
            def output(n):
                act.wait_ge(pv_done, (n + 1) * KT)
                if not isinstance(n, int) or n >= 1:
                    act.wait_ge(o_tp, n)
                nc.scalar.copy(oS[:, :], pO[:, :]).then_inc(o_sb, 1)

            def step(n, later):
                for kt in range(KT):
                    for hp in range(2):
                        act.wait_ge(s_ps, (n * KT + kt) * 2 + (hp + 1))
                        if later or kt >= 2:
                            act.wait_ge(pv_done, n * KT + (kt - 1))
                        nc.scalar.activation(pe_[:, kt % 2, 2 * hp:2 * hp + 2, :], pS[:, 2 * hp:2 * hp + 2, :],
                                             ACT.Exp, scale=float(HD0) ** -0.5).then_inc(e_sb, 1)
                    if later and kt == 0:
                        output(n + -1)

            step(0, False)
            with act.Fori(1, NGRP * NQ) as n:
                step(n, True)
            output(NGRP * NQ - 1)

        @block.vector
        def _(dve):
            for par in range(2):
                nc.vector.memset(kst[64:P, par, :, :], 0.0)
                dve.drain()
                nc.vector.memset(kst[MROW:MROW + NPART, par, :, :], -1.0).then_inc(cleared_k, 1)

            def maxima(n, units):
                for u in units:
                    dve.wait_ge(max_ps, n * NU + (u + 1))
                    nc.vector.tensor_reduce(mxb[:, u // (NQT * NKB), u // NKB % NQT, u % NKB:u % NKB + 1],
                                            pM[:, bank["unit", u], :], AX.X, ALU.max).then_inc(max_sb, 1)

            def split(par, qc, n):
                dve.drain()
                nc.vector.tensor_reduce(mx[:, :, :].rearrange("p q j -> p j q"), mxb[:, :, :, :], AX.X, ALU.max)
                dve.drain()
                nc.vector.tensor_copy(mpart[:, :, :, 0], mx[:, :, :])
                dve.drain()
                nc.vector.tensor_tensor(out=mr[:, :, :], in0=mx[:, :, :], in1=mpart[:, :, :, 0], op=ALU.subtract)
                dve.drain()
                nc.vector.tensor_copy(mpart[:, :, :, 1], mr[:, :, :])
                dve.drain()
                nc.vector.tensor_tensor(out=mr[:, :, :], in0=mr[:, :, :], in1=mpart[:, :, :, 1], op=ALU.subtract)
                dve.drain()
                nc.vector.tensor_copy(mpart[:, :, :, 2], mr[:, :, :]).then_inc(m_split, 1)
                for qt in range(NQT):
                    dve.wait_ge(m_ps, n * NQT + (qt + 1))
                    nc.vector.tensor_copy(qst[MROW:MROW + NPART, par, :, ds(qc * QC + qt * P, P)],
                                          pM[MROW:MROW + NPART, bank["row", qt], :].rearrange("p (j q) -> p j q", j=HPG)).then_inc(m_row, 1)

            def output(n):
                dve.wait_ge(o_tp, n + 1)
                o = pM[:, bank["output", 0], :].rearrange("p (a d) -> p a d", d=32)
                nc.vector.reciprocal(rs[:, :].unsqueeze(2), o[:, :, HD0:HD0 + 1])
                dve.drain()
                nc.vector.tensor_tensor(
                    out=AO[:, ds(n, 1), :, :].rearrange("p g a d -> p (g a) d"),
                    in0=o[:, :, 0:HD0], in1=bcast(rs[:, :], HD0), op=ALU.mult).then_inc(o_out, 1)

            def step(par, qc, n, later):
                maxima(n, range(4 * UPK))
                if later:
                    output(n + -2)
                maxima(n, range(4 * UPK, NU))
                split(par, qc, n)

            def group(gi, par, later, lead):
                step(par, 1, gi * NQ + 1, later)
                with dve.Fori(1, NQ - 1) as qc:
                    step(par, qc + 1, qc + (gi * NQ + 1), True)
                if lead:
                    step(1 - par, 0, gi * NQ + NQ, True)

            dve.drain()
            maxima(0, range(NU))
            split(0, 0, 0)
            group(0, 0, False, True)
            with dve.Fori(0, NGRP // 2 - 1) as r:
                group(r * 2 + 1, 1, True, True)
                group(r * 2 + 2, 0, True, True)
            group(NGRP - 1, 1, True, False)
            output(NGRP * NQ - 2)
            output(NGRP * NQ - 1)


def head_output_pass(nc, AO, R, w, const):
    NQ, NQT = SEQ // QC, QC // P
    with ExitStack() as ctx:
        k = Kit(nc, ctx, "ho_")
        at = k.sb("at", [P, 2, CH, D])
        aT = k.sb("aT", [P, CW])
        pa, py = k.ps("pa", [P, CW]), k.ps("py", [P, CW])
        a_in, a_ps, a_T, y_ps, y_in = (k.sem(n) for n in ("a_in", "a_ps", "a_T", "y_ps", "y_in"))
        block = ctx.enter_context(nc.Block())

        @block.tensor
        def _(pe):
            for c in range(NC):
                pe.wait_ge(a_in, upto(c))
                pe.wait_ge(a_T, upto(c - 1))
                for i in range(CH):
                    last = nc.tensor.transpose(pa[:, i * P:(i + 1) * P], at[:, c % 2, i, :], const["ident"][:, :])
                last.then_inc(a_ps, 1)
                pe.wait_ge(a_T, upto(c))
                pe.wait_ge(y_in, upto(c - 1))
                for i in range(CH):
                    last = nc.tensor.matmul(py[:, i * P:(i + 1) * P], aT[:, i * P:(i + 1) * P], w["proj"][:, :],
                                            start=True, stop=True)
                last.then_inc(y_ps, 1)

        @block.scalar
        def _(act):
            for c in range(NC):
                b, qc = c // NQ, c % NQ
                act.wait_ge(a_ps, upto(c - 2))
                for g in range(NG0):
                    src = AO[:, (b * NG0 + g) * NQ + qc, :, :].rearrange("p (t j) d -> p t (j d)", j=HPG)
                    last = nc.scalar.copy(at[:, c % 2, :, 32 * g:32 * g + 32], src)
                last.then_inc(a_in, 1)
                act.wait_ge(a_ps, upto(c))
                act.wait_ge(y_ps, upto(c - 1))
                nc.scalar.copy(aT[:, :], pa[:, :]).then_inc(a_T, 1)

        @block.vector
        def _(dve):
            for c in range(NC):
                r4 = R[:, c * CH:(c + 1) * CH, :]
                nc.vector.tensor_tensor(out=r4, in0=r4, in1=w["bias"][:, :].unsqueeze(1).broadcast_to([P, CH, D]), op=ALU.add)
                dve.wait_ge(y_ps, upto(c))
                dve.drain()
                nc.vector.tensor_tensor(out=r4, in0=r4, in1=py[:, :].rearrange("p (a n) -> p a n", n=D),
                                        op=ALU.add).then_inc(y_in, 1)
                dve.drain()


def fp4_levels(nc, dve, x, xabs, nb, b, halved, absed):
    ab, lev, up = b["ab"][:, 0:nb, :], b["lev"][:, 0:nb, :], b["up"][:, 0:nb, :]
    bm, sc, rc, hs = (b[n][:, 0:nb] for n in ("bm", "sc", "rc", "hs"))
    nc.vector.tensor_reduce(bm, x, AX.X, ALU.max, apply_absolute_value=True)
    dve.drain()
    nc.vector.tensor_scalar(sc, bm, 1.0 / 6.0, 1e-12, ALU.mult, ALU.max)
    dve.drain()
    nc.vector.tensor_scalar(hs, sc, 0.5, None, ALU.mult).then_inc(halved, 1)
    nc.vector.reciprocal(rc, sc)
    dve.drain()
    absed()
    nc.vector.tensor_tensor(out=ab, in0=xabs, in1=bcast(rc, FB), op=ALU.mult)
    dve.drain()
    nc.vector.tensor_scalar(lev, ab, 5.0, 2.0, ALU.is_gt, ALU.mult)
    nc.vector.tensor_scalar(up, ab, 1.75, None, ALU.is_gt)
    for mid in (3.5, 2.5):
        dve.drain()
        nc.vector.scalar_tensor_tensor(out=lev, in0=ab, scalar=mid, in1=lev, op0=ALU.is_gt, op1=ALU.add)
    dve.drain()
    nc.vector.scalar_tensor_tensor(out=lev, in0=lev, scalar=2.0, in1=up, op0=ALU.mult, op1=ALU.add)
    for mid in (1.25, 0.75, 0.25):
        dve.drain()
        nc.vector.scalar_tensor_tensor(out=lev, in0=ab, scalar=mid, in1=lev, op0=ALU.is_gt, op1=ALU.add)
    dve.drain()


def fp4_pass(nc, R, w_gate, w_up, w_down, const, prefetch=()):
    NBX, NBH = D // FB, F0 // FB
    FCH = [P, P, F0 - 2 * P]
    NWB = 2 * 3 * NBX + NBH
    with ExitStack() as ctx:
        k = Kit(nc, ctx, "fp_")
        ws = k.sb("ws", [P, NWB, FB])
        wg, wu = k.sb("wg", [P, F0]), k.sb("wu", [P, F0])
        wd = k.sb("wd", [P, 3, D])
        buf = {"ab": k.sb("ab", [P, CH * NBH, FB]), "lev": k.sb("lev", [P, CH * NBH, FB]),
               "up": k.sb("up", [P, CH * NBH, FB])}
        for n in ("bm", "sc", "rc", "hs"):
            buf[n] = k.sb(n, [P, CH * NBH])
        sg = k.sb("sg", [P, CH * NBH, FB])
        ax = k.sb("ax", [P, CH * NBH, FB])
        st, mv = k.sb("st", [P, CH, 6]), k.sb("mv", [P, CH, 2])
        sd, rs = k.sb("sd", [P, CH]), k.sb("rs", [P, CH])
        xn = k.sb("xn", [P, CH, D])
        xq = k.sb("xq", [P, CH, D])
        xqT = k.sb("xqT", [P, 2, CW])
        gs = k.sb("gs", [P, 2, F0])
        h = k.sb("h", [P, CH, F0])
        hq = k.sb("hq", [P, CH, F0])
        hqT = k.sb("hqT", [P, 2, 3, P])
        pa = k.ps("pa", [P, CW])
        pg, pu = k.ps("pg", [P, 2, 512]), k.ps("pu", [P, 2, 512])
        pt = k.ps("pt", [P, 2, 512])
        py = k.ps("py", [P, CW])
        w_in, w_zero = k.sem("w_in"), k.sem("w_zero")
        halved, signs, signed = k.sem("halved"), k.sem("signs"), k.sem("signed")
        rounded, absed = k.sem("rounded"), k.sem("absed")
        w_ps, w_sb = k.sem("w_ps"), k.sem("w_sb")
        wctx = ExitStack()
        blockw = wctx.enter_context(nc.Block())

        @blockw.sync
        def _(sp):
            sp.wait_ge(w_zero, 1)
            n = 0
            for o, src in ((0, w_gate), (3 * NBX, w_up)):
                for j, m in enumerate(FCH):
                    sp.dma_start(ws[0:m, o + j * NBX:o + (j + 1) * NBX, :].rearrange("p a b -> p (a b)"),
                                 src[j * P:j * P + m, :]).then_inc(w_in, 16)
            sp.dma_start(ws[:, 6 * NBX:, :].rearrange("p a b -> p (a b)"), w_down).then_inc(w_in, 16)

        @blockw.scalar
        def _(act):
            act.wait_ge(w_in, 16 * 7)
            nc.scalar.activation(ax[:, 0:NWB, :], ws[:, :, :], ACT.Abs).then_inc(absed, 1)
            nc.scalar.activation(sg[:, 0:NWB, :], ws[:, :, :], ACT.Sign).then_inc(signs, 1)
            for n in range(9):
                act.wait_ge(w_ps, n + 1)
                kind, j = n // 3, n % 3
                if kind < 2:
                    dst = (wg, wu)[kind][:, j * P:j * P + FCH[j]]
                    src = pt[:, n % 2, 0:FCH[j]]
                else:
                    dst = wd[0:FCH[j], j, :]
                    src = pt[0:FCH[j], n % 2, 0:D]
                nc.scalar.copy(dst, src).then_inc(w_sb, 1)

        @blockw.gpsimd
        def _(pool):
            pool.wait_ge(signs, 1)
            pool.wait_ge(halved, 1)
            nc.gpsimd.tensor_tensor(out=sg[:, 0:NWB, :], in0=sg[:, 0:NWB, :], in1=bcast(buf["hs"][:, 0:NWB], FB),
                                    op=ALU.mult).then_inc(signed, 1)

        @blockw.vector
        def _(dve):
            nc.vector.memset(ws[:, :, :], 0.0).then_inc(w_zero, 1)
            dve.wait_ge(w_in, 16 * 7)
            fp4_levels(nc, dve, ws[:, :, :], ax[:, 0:NWB, :], NWB, buf, halved, lambda: dve.wait_ge(absed, 1))
            dve.wait_ge(signed, 1)
            nc.vector.tensor_tensor(out=ws[:, :, :], in0=buf["lev"][:, 0:NWB, :], in1=sg[:, 0:NWB, :],
                                    op=ALU.mult).then_inc(rounded, 1)

        @blockw.tensor
        def _(pe):
            pe.wait_ge(rounded, 1)
            for n in range(9):
                if n >= 2:
                    pe.wait_ge(w_sb, n - 1)
                kind, j = n // 3, n % 3
                m = FCH[j]
                if kind < 2:
                    src = ws[0:m, (kind * 3 + j) * NBX:(kind * 3 + j + 1) * NBX, :].rearrange("p a b -> p (a b)")
                    nc.tensor.transpose(pt[:, n % 2, 0:m], src, const["ident"][0:m, 0:m]).then_inc(w_ps, 1)
                else:
                    o = 6 * NBX + j * NBX
                    src = ws[:, o:o + m // FB, :].rearrange("p a b -> p (a b)")
                    nc.tensor.transpose(pt[0:m, n % 2, 0:D], src, const["ident"][:, :]).then_inc(w_ps, 1)

        wctx.close()
        sgx = k.sb("sgx", [P, CH * NBX, FB])
        axx = k.sb("axx", [P, CH * NBX, FB])
        n_in = k.sem("n_in")
        absed_x, absed_h = k.sem("absed_x"), k.sem("absed_h")
        momented, rooted = k.sem("momented"), k.sem("rooted")
        halved_x, signs_x, signed_x, xq_sb = (k.sem(n) for n in ("halved_x", "signs_x", "signed_x", "xq_sb"))
        halved_h, signs_h, signed_h, hq_sb = (k.sem(n) for n in ("halved_h", "signs_h", "signed_h", "hq_sb"))
        x_ps, x_T = k.sem("x_ps"), k.sem("x_T")
        g_ps, u_ps, g_sb, h_sb = k.sem("g_ps"), k.sem("u_ps"), k.sem("g_sb"), k.sem("h_sb")
        t_ps, t_sb, y_ps, y_in = k.sem("t_ps"), k.sem("t_sb"), k.sem("y_ps"), k.sem("y_in")
        fetched = k.sem("fetched")
        block = ctx.enter_context(nc.Block())

        @block.sync
        def _(sp):
            fetch(sp, prefetch, fetched)

        def blocks(ap):
            return ap.rearrange("p a (n b) -> p (a n) b", b=FB)

        @block.tensor
        def _(pe):

            def turn(c, i):
                pe.wait_ge(t_sb, upto(c, CH, i - 2 - CH + 1)) if not isinstance(c, int) or c * CH + i >= 2 else None
                for j, m in enumerate(FCH):
                    last = nc.tensor.transpose(pt[0:m, i % 2, j * P:(j + 1) * P], hq[:, i, j * P:j * P + m],
                                               const["ident"][:, :])
                last.then_inc(t_ps, 1)

            def down(c, i):
                pe.wait_ge(t_sb, upto(c, CH, i - CH + 1))
                if i == 0:
                    pe.wait_ge(y_in, upto(c - 1))
                for j, m in enumerate(FCH):
                    last = nc.tensor.matmul(py[:, i * P:(i + 1) * P], hqT[0:m, i % 2, j, :], wd[0:m, j, :],
                                            start=(j == 0), stop=(j == 2))
                last.then_inc(y_ps, 1)

            def step(c, p):
                if has(c - 2, NC):
                    pe.wait_ge(hq_sb, upto(c - 2))
                    turn(c - 2, 0)
                    for i in range(1, CH):
                        turn(c - 2, i)
                        down(c - 2, i - 1)
                    down(c - 2, CH - 1)
                if has(c - 1, NC):
                    pe.wait_ge(x_T, upto(c - 1))
                    for i in range(CH):
                        skip = isinstance(c, int) and (c - 1) * CH + i < 2
                        if not skip:
                            pe.wait_ge(g_sb, upto(c - 1, CH, i - 2 - CH + 1))
                        nc.tensor.matmul(pg[:, i % 2, 0:F0], xqT[:, 1 - p, i * P:(i + 1) * P], wg[:, :],
                                         start=True, stop=True).then_inc(g_ps, 1)
                        if not skip:
                            pe.wait_ge(h_sb, upto(c - 1, CH, i - 2 - CH + 1))
                        nc.tensor.matmul(pu[:, i % 2, 0:F0], xqT[:, 1 - p, i * P:(i + 1) * P], wu[:, :],
                                         start=True, stop=True).then_inc(u_ps, 1)
                if has(c, NC):
                    pe.wait_ge(xq_sb, upto(c))
                    pe.wait_ge(x_T, upto(c - 1))
                    for i in range(CH):
                        last = nc.tensor.transpose(pa[:, i * P:(i + 1) * P], xq[:, i, :], const["ident"][:, :])
                    last.then_inc(x_ps, 1)

            lagged(pe, NC, 2, 2, 0, step, peel=4)

        @block.scalar
        def _(act):

            def step(c, p):
                if has(c - 2, NC):
                    for i in range(CH):
                        act.wait_ge(t_ps, upto(c - 2, CH, i - CH + 1))
                        if not (isinstance(c, int) and (c - 2) * CH + i < 2):
                            act.wait_ge(y_ps, upto(c - 2, CH, i - 2 - CH + 1))
                        nc.scalar.copy(hqT[:, i % 2, 0:2, :], pt[:, i % 2, 0:2 * P].rearrange("p (j n) -> p j n", n=P))
                        nc.scalar.copy(hqT[0:FCH[2], i % 2, 2, :], pt[0:FCH[2], i % 2, 2 * P:3 * P]).then_inc(t_sb, 1)
                if has(c, NC):
                    act.wait_ge(momented, upto(c))
                    nc.scalar.activation(sd[:, :], mv[:, :, 1], ACT.Sqrt, bias=const["eps"][:, 0:1]).then_inc(rooted, 1)
                    act.wait_ge(n_in, upto(c))
                    act.wait_ge(xq_sb, upto(c - 1))
                    nc.scalar.activation(axx[:, :, :], blocks(xn[:, :, :]), ACT.Abs).then_inc(absed_x, 1)
                    nc.scalar.activation(sgx[:, :, :], blocks(xn[:, :, :]), ACT.Sign).then_inc(signs_x, 1)
                if has(c - 1, NC):
                    for i in range(CH):
                        act.wait_ge(g_ps, upto(c - 1, CH, i - CH + 1))
                        if not (isinstance(c, int) and (c - 1) * CH + i < 2):
                            act.wait_ge(h_sb, upto(c - 1, CH, i - 2 - CH + 1))
                        nc.scalar.activation(gs[:, i % 2, :], pg[:, i % 2, 0:F0], ACT.Silu).then_inc(g_sb, 1)
                    act.wait_ge(h_sb, upto(c - 1, CH))
                    act.wait_ge(hq_sb, upto(c - 2))
                    nc.scalar.activation(ax[:, :, :], blocks(h[:, :, :]), ACT.Abs).then_inc(absed_h, 1)
                    nc.scalar.activation(sg[:, :, :], blocks(h[:, :, :]), ACT.Sign).then_inc(signs_h, 1)
                if has(c, NC):
                    act.wait_ge(x_ps, upto(c))
                    nc.scalar.copy(xqT[:, p, :], pa[:, :]).then_inc(x_T, 1)

            lagged(act, NC, 2, 2, 0, step, peel=4)

        @block.gpsimd
        def _(pool):

            def step(c, p):
                for sign, hv, out, t, d, nb in ((signs_x, halved_x, signed_x, sgx, c, CH * NBX),
                                                (signs_h, halved_h, signed_h, sg, c - 1, CH * NBH)):
                    if has(d, NC):
                        pool.wait_ge(sign, upto(d))
                        pool.wait_ge(hv, upto(d))
                        nc.gpsimd.tensor_tensor(out=t[:, :, :], in0=t[:, :, :], in1=bcast(buf["hs"][:, 0:nb], FB),
                                                op=ALU.mult).then_inc(out, 1)

            lagged(pool, NC, 2, 2, 0, step, peel=4)

        @block.vector
        def _(dve):

            def step(c, p):
                if has(c, NC):
                    src = R[:, ds(c * CH, CH), :]
                    moments(nc, dve, st, mv, src).then_inc(momented, 1)
                    dve.wait_ge(rooted, upto(c))
                    dve.wait_ge(signs_x, upto(c - 1))
                    normalise(nc, dve, xn, src, mv, sd, rs).then_inc(n_in, 1)
                    dve.drain()
                    fp4_levels(nc, dve, blocks(xn[:, :, :]), axx[:, :, :], CH * NBX, buf, halved_x,
                               lambda: dve.wait_ge(absed_x, upto(c)))
                    dve.wait_ge(signed_x, upto(c))
                    dve.wait_ge(x_ps, upto(c - 1))
                    nc.vector.tensor_tensor(out=blocks(xq[:, :, :]), in0=buf["lev"][:, 0:CH * NBX, :],
                                            in1=sgx[:, :, :], op=ALU.mult).then_inc(xq_sb, 1)
                if has(c - 1, NC):
                    dve.wait_ge(signs_h, upto(c - 2))
                    for i in range(CH):
                        dve.wait_ge(g_sb, upto(c - 1, CH, i - CH + 1))
                        dve.wait_ge(u_ps, upto(c - 1, CH, i - CH + 1))
                        nc.vector.tensor_tensor(out=h[:, i, :], in0=gs[:, i % 2, :], in1=pu[:, i % 2, 0:F0],
                                                op=ALU.mult).then_inc(h_sb, 1)
                    dve.drain()
                    fp4_levels(nc, dve, blocks(h[:, :, :]), ax[:, :, :], CH * NBH, buf, halved_h,
                               lambda: dve.wait_ge(absed_h, upto(c - 1)))
                    dve.wait_ge(signed_h, upto(c - 1))
                    dve.wait_ge(t_ps, upto(c - 2, CH))
                    nc.vector.tensor_tensor(out=blocks(hq[:, :, :]), in0=buf["lev"][:, :, :],
                                            in1=sg[:, :, :], op=ALU.mult).then_inc(hq_sb, 1)
                    dve.drain()
                if has(c - 2, NC):
                    dve.wait_ge(y_ps, upto(c - 2, CH))
                    r4 = R[:, ds((c - 2) * CH, CH), :]
                    nc.vector.tensor_tensor(out=r4, in0=r4, in1=py[:, :].rearrange("p (a n) -> p a n", n=D),
                                            op=ALU.add).then_inc(y_in, 1)

            lagged(dve, NC, 2, 2, 0, step, peel=4)


def row(a, n=P):
    return a.unsqueeze(0).broadcast_to([P, n])


def global_attention_stage(nc, X, a, scratch, const):
    with ExitStack() as ctx:
        k = Kit(nc, ctx, "A_")
        w = {"qkv": k.sb("qkv", [P, 3 * D]), "proj": k.sb("proj", [P, D]), "bias": k.sb("bias", [P, D])}
        AO = k.sb("AO", [P, NT, H0, HD0])
        Vc = k.sb("Vc", [P, BATCH * NG0, NTB, HPG, HD0 + 1])
        move_pass(nc, "A_w_", [(w["qkv"][:, :], a["L0_attn_w_qkv"]), (w["proj"][:, :], a["L0_attn_w_proj"]),
                               (w["bias"][:, :], row(a["L0_attn_b_proj"]))])
        split_qkv_pass(nc, X, Vc, scratch, w, const)
        full_attention_pass(nc, Vc, AO, scratch, const)
        head_output_pass(nc, AO, X, w, const)


class WindowWeights:
    def __init__(self, k, a):
        self.a = a
        self.w = {"wqk": k.sb("wqk", [P, 2 * INNER]), "wv": k.sb("wv", [P, INNER]), "wo": k.sb("wo", [P, HP, D]),
                  "own": k.sb("own", [P, 64]), "pb": k.sb("pb", [P, D])}
        self.f = {"w1": k.sb("w1", [P, F1]), "w2": k.sb("w2", [P, F1 // P, D]), "b1": k.sb("b1", [P, F1 // P])}
        for n in ("g1", "o1", "b2", "g2", "o2"):
            self.f[n] = k.sb(n, [P, D])

    def attention(self, pre, own):
        w, a, A = self.w, self.a, "L1_attn_" + pre

        def per_head(ap):
            return ap.rearrange("p (h k) -> p h k", k=HD)

        return [(per_head(w["wqk"][:, 0:INNER]), a[A + "_wqs"].rearrange("h d k -> d h k")),
                (per_head(w["wqk"][:, INNER:]), a[A + "_wks"].rearrange("h d k -> d h k")),
                (per_head(w["wv"][:, :]), a[A + "_wvs"].rearrange("h d k -> d h k")),
                (w["wo"][:, :, :], a[A + "_pw"].rearrange("(c p) n -> p c n", p=P)),
                (w["own"][:, 0:own], a["c_own%d" % own]), (w["pb"][:, :], row(a[A + "_pb"]))]

    def feed(self, pre, ff):
        f, a, A, B = self.f, self.a, "L1_attn_" + pre, "L1_attn_" + ff
        return [(f["w1"][:, :], a[B + "_w1"]),
                (f["w2"][:, :, :], a[B + "_w2"].rearrange("(c p) n -> p c n", p=P)),
                (f["g1"][:, :], row(a[A + "_g"])), (f["o1"][:, :], row(a[A + "_b"])),
                (f["b2"][:, :], row(a[B + "_b2"])), (f["g2"][:, :], row(a[B + "_g"])),
                (f["o2"][:, :], row(a[B + "_b"]))] + [
                (f["b1"][:, j:j + 1], a[B + "_b1"][P * j:P * j + P].unsqueeze(1)) for j in range(F1 // P)]


def window_stage(nc, E, weights, scratch, const, prefetch):
    perm = scratch.rearrange("(b m t j) f -> b j m t f", b=BATCH, m=64, t=NTB, j=2)
    plain = scratch.rearrange("(t p) f -> p t f", p=P)
    permuted = [(E[64 * j:64 * j + 64, b * NTB:(b + 1) * NTB, :], perm[b, j]) for b in range(BATCH) for j in range(2)]
    attention_pass(nc, "C_a_", "w32", E, weights.w, const, prefetch=weights.feed("la", "lf") + prefetch)
    relu_pass(nc, "C_f_", E, weights.f, const, prefetch=weights.attention("sa", 64))
    move_pass(nc, "C_s_", [(plain, E[:, :, :])])
    move_pass(nc, "C_t_", permuted)
    attention_pass(nc, "C_b_", "w64", E, weights.w, const, prefetch=weights.feed("sa", "pf"))
    relu_pass(nc, "C_g_", E, weights.f, const)
    move_pass(nc, "C_u_", [(src, to) for to, src in permuted])
    move_pass(nc, "C_v_", [(E[:, :, :], plain)])


class RotaryWeights:
    def __init__(self, nc, k, a):
        w = {"wqk": k.sb("wqk", [P, 2 * INNER]), "wv": k.sb("wv", [P, INNER]), "wo": k.sb("wo", [P, HP, D]),
             "mask": k.sb("mask", [P, NT, 64], BF16), "kfac": k.sb("kfac", [P, 1]), "inner": k.sb("inner", [P, NT]),
             "rot": k.sb("rot", [P, NT, 4 * HD]), "qk_scale": k.sb("qk_scale", [P, 4 * HD])}
        f = {"w1": k.sb("w1", [P, 2 * F2]), "w2": k.sb("w2", [P, NJ2, D]), "b1a": k.sb("b1a", [P, NJ2]),
             "b1g": k.sb("b1g", [P, NJ2]), "g": k.sb("g", [P, 1]), "b": k.sb("b", [P, 1]), "inner": w["inner"]}

        self.w, self.f, self.a = w, f, a
        with nc.Block() as block:
            @block.vector
            def _(dve):
                nc.vector.memset(f["w2"][64:P, NJ2 - 1, :], 0.0)

    def tables(self):
        w, a = self.w, self.a
        return [(w["mask"][:, :, :], a["c_mask"]), (w["kfac"][:, :], a["c_kfac"]),
                (w["inner"][:, :], a["c_inner"]), (w["rot"][:, :, :], a["c_rot"])]

    def layer_of(self, name, l):
        return self.a["L1_ffn_" + name][ds(l, 1)]

    def attention(self, l):
        w, layer_of = self.w, self.layer_of
        wqkv = layer_of("Wqkv", l).rearrange("l k n -> (l k) n")
        return [(w["wqk"][:, :], wqkv[:, 0:2 * INNER]), (w["wv"][:, :], wqkv[:, 2 * INNER:]),
                (w["wo"][:, :, :], layer_of("Wo", l).rearrange("l (c p) n -> p (l c) n", p=P))] + [
                (w["qk_scale"][:, HD * i:HD * i + HD],
                 layer_of("q_scale" if i < 2 else "k_scale", l).broadcast_to([P, HD])) for i in range(4)]

    def feed(self, l):
        f, layer_of = self.f, self.layer_of
        w2 = layer_of("W2", l)
        moves = [(f["w1"][:, :], layer_of("W1", l).rearrange("l k n -> (l k) n")),
                 (f["w2"][:, 0:2, :], w2[:, 0:2 * P, :].rearrange("l (c p) n -> p (l c) n", p=P)),
                 (f["w2"][0:JW2[2], 2, :], w2[:, 2 * P:F2, :].rearrange("l k n -> (l k) n")),
                 (f["w2"][ONE_ROW:ONE_ROW + 1, 2, :], layer_of("b2", l)),
                 (f["g"][:, :], layer_of("ln_g", l).rearrange("l p -> p l")),
                 (f["b"][:, :], layer_of("ln_b", l).rearrange("l p -> p l"))]
        b1 = layer_of("b1", l)
        for j, m in enumerate(JW2):
            for o, t in ((0, "b1a"), (F2, "b1g")):
                moves.append((f[t][0:m, j:j + 1], b1[:, o + P * j:o + P * j + m].rearrange("l p -> p l")))
        return moves


def rotary_stage(nc, Y, weights, const):
    w, f = weights.w, weights.f
    with nc.Fori(0, DEPTH - 1) as l:
        attention_pass(nc, "D_a_", "local", Y, w, const, prefetch=weights.feed(l))
        gated_pass(nc, "D_f_", Y, f, const, prefetch=weights.attention(l + 1))
    attention_pass(nc, "D_b_", "local", Y, w, const, prefetch=weights.feed(DEPTH - 1))
    gated_pass(nc, "D_g_", Y, f, const)


def preln_program(nc, a, out):
    parts = nc.dram_tensor("qk_parts", (2, NPART, BATCH * P, SEQ), BF16).ap()
    order = nc.dram_tensor("reorder", (TOK, D), F32).ap()
    with ExitStack() as ctx:
        k = Kit(nc, ctx, "")
        X = k.sb("X", [P, NT, D])
        const = {"ident": k.sb("ident", [P, P]), "identb": k.sb("identb", [P, P], BF16), "eps": k.sb("eps", [P, 1]),
                 "ident_d": a["c_ident"], "identb_d": a["c_identb"]}
        load_pass(nc, const, X, a["L0_attn_x"])
        global_attention_stage(nc, X, a, parts, const)
        rotary = RotaryWeights(nc, Kit(nc, ctx, "D_"), a)
        Y = k.sb("Y", [P, NT, D])
        with ExitStack() as stage:
            window = WindowWeights(Kit(nc, stage, "C_"), a)
            fp4_pass(nc, X, a["L0_ffn_w_gate"], a["L0_ffn_w_up"], a["L0_ffn_w_down"], const,
                     prefetch=window.attention("la", W32))
            add_norm_pass(nc, "n1_", X, Y, False)
            window_stage(nc, Y, window, order, const, rotary.tables() + rotary.attention(0))
        add_norm_pass(nc, "n2_", X, Y, True)
        rotary_stage(nc, Y, rotary, const)
        add_pass(nc, X, Y)
        store_pass(nc, X, out)


def host_tables():
    bf16 = mybir.dt.np(BF16)
    f32 = np.float32
    p = np.arange(P)
    half = np.arange(0, HD, 2, dtype=f32)
    inv_freq = (f32(1.0) / f32(10000.0) ** (half / f32(HD))).astype(f32)
    freqs = np.arange(SEQ, dtype=f32)[:, None] * inv_freq[None, :]
    base = (half.astype(np.float64) + 0.4 * HD) / (1.4 * HD)
    scale = base[None, :] ** ((p[:, None] - P // 2) / 16.0)
    cos = np.cos(freqs.astype(np.float64)).reshape(NTB, P, 32)
    sin = np.sin(freqs.astype(np.float64)).reshape(NTB, P, 32)
    rot = np.zeros((P, NT, 256))
    for t in range(NT):
        c, s = cos[t % NTB], sin[t % NTB]
        for o, m in ((0, scale), (128, 1.0 / scale)):
            rot[:, t, o:o + 128] = np.concatenate([c * m, c * m, s * m, -s * m], axis=1)
    mask = np.zeros((P, NT, 2 * W32))
    i, j = (p % W32)[:, None], (np.arange(2 * W32) - W32)[None, :]
    mask[:] = np.where((i < j) | (i > j + W32), -1e30, 0.0)[:, None, :]
    mask[:W32, ::NTB, :W32] = -1e30
    inner = np.ones((P, NT))
    inner[:, ::NTB] = 0.0
    own = (p[:, None] % 64 == np.arange(64)[None, :])
    own32 = (p[:, None] % 32 == np.arange(32)[None, :])
    return {
        "c_ident": np.eye(P, dtype=f32),
        "c_identb": np.eye(P).astype(bf16),
        "c_rot": rot.astype(f32),
        "c_mask": mask.astype(bf16),
        "c_kfac": np.tile(base ** (P / 16.0), 4).astype(f32)[:, None],
        "c_inner": inner.astype(f32),
        "c_own64": own.astype(f32),
        "c_own32": own32.astype(f32),
    }


def kernel(**inputs):
    import concourse.bacc as bacc
    from concourse.bass_utils import run_bass_kernel_spmd

    nc = bacc.Bacc("TRN2", target_bir_lowering=False, num_devices=1)
    arrays = {n: np.ascontiguousarray(v) for n, v in inputs.items()}
    arrays.update(host_tables())
    a = {n: nc.dram_tensor(n, v.shape, mybir.dt.from_np(v.dtype), kind="ExternalInput").ap()
         for n, v in arrays.items()}
    out = nc.dram_tensor("out", (BATCH, SEQ, D), F32, kind="ExternalOutput").ap()
    preln_program(nc, a, out)
    result = run_bass_kernel_spmd(nc, [arrays], core_ids=[0])
    return result.results[0]["out"]
```
